# Optimizing a Trainium2 kernel written in Bass

```python
import numpy as np
import jax
import jax.numpy as jnp

def _softmax(x, axis=-1):
    return jax.nn.softmax(x, axis=axis)

def _gelu(x):
    return jax.nn.gelu(x, approximate=True)

def _silu(x):
    return jax.nn.silu(x)

def _sigmoid(x):
    return jax.nn.sigmoid(x)

def _layernorm(x, axis=-1, eps=1e-05):
    m = jnp.mean(x, axis=axis, keepdims=True)
    v = jnp.var(x, axis=axis, keepdims=True)
    return (x - m) / jnp.sqrt(v + eps)

def _scatter_add(tgt, idx, src, axis=0):
    return tgt.at[idx].add(src)

def _segment_sum(src, seg, n):
    return jax.ops.segment_sum(src, seg, n)
kernel_name = 'mk_seq_postln_d2_jaxref_r8_3bfe7b'

def setup_inputs(seed: int=0):
    np.random.seed(seed)
    _w = jnp.asarray

    def _L0_attn_setup():
        import jax, jax.numpy as jnp
        import numpy as np
        B, N, C = (2, 256, 128)
        H = 8
        WS = 32
        D = C // H
        key = jax.random.key(seed)
        k0, k1, k2 = jax.random.split(key, 3)
        s = 0.02
        x = jax.random.normal(k0, (B, N, C), dtype=jnp.float32)
        w_qkv = jax.random.normal(k1, (3 * C, C), dtype=jnp.float32) * s
        b_qkv = jnp.zeros((3 * C,), dtype=jnp.float32)
        w_proj = jax.random.normal(k2, (C, C), dtype=jnp.float32) * s
        b_proj = jnp.zeros((C,), dtype=jnp.float32)
        return {'x': x, 'w_qkv': w_qkv, 'b_qkv': b_qkv, 'w_proj': w_proj, 'b_proj': b_proj}
    _L0_attn_in = _L0_attn_setup()

    def _L0_ffn_setup():
        import jax, jax.numpy as jnp
        import numpy as np
        import math
        D_MODEL = 128
        N_EXPERTS = 16
        D_FF = 512
        CAP_FACTOR = 1.25
        MIN_CAPACITY = 4

        def _capacity(num_tokens, num_experts):
            cap = math.floor(CAP_FACTOR * num_tokens / num_experts)
            cap += cap % 2
            return max(cap, MIN_CAPACITY)

        def _top1_router(gate_logits, capacity):
            s, e = gate_logits.shape
            probs = jax.nn.softmax(gate_logits, axis=-1)
            top1 = jnp.argmax(gate_logits, axis=-1)
            mask = jax.nn.one_hot(top1, e, dtype=jnp.int32)
            ranks = jnp.cumsum(mask, axis=0) - 1
            mask = mask * (ranks < capacity).astype(jnp.int32)
            rank1 = jnp.sum(mask * ranks, axis=-1)
            ranks_oh = jax.nn.one_hot(rank1, capacity, dtype=probs.dtype)
            weight = mask.astype(probs.dtype) * probs
            combine_weights = weight[:, :, None] * ranks_oh[:, None, :]
            sec_mask = combine_weights > 0
            return (combine_weights, sec_mask)
        key = jax.random.key(seed)
        k1, k2, k3, k4 = jax.random.split(key, 4)
        x = jax.random.normal(k1, (4, 256, D_MODEL), dtype=jnp.float32)
        gate_w = jax.random.normal(k2, (N_EXPERTS, D_MODEL), dtype=jnp.float32) * math.sqrt(0.1 / D_MODEL)
        w1 = jax.random.normal(k3, (N_EXPERTS, D_MODEL, D_FF), dtype=jnp.float32) * (1.0 / math.sqrt(D_MODEL))
        w2 = jax.random.normal(k4, (N_EXPERTS, D_FF, D_MODEL), dtype=jnp.float32) * (1.0 / math.sqrt(D_FF))
        return {'x': x, 'gate_w': gate_w, 'w1': w1, 'w2': w2}
    _L0_ffn_in = _L0_ffn_setup()

    def _L1_attn_setup():
        import jax, jax.numpy as jnp
        import numpy as np
        import math
        D_MODEL = 128
        D_QUERY = 64
        key = jax.random.key(seed)
        k1, k2, k3, k4 = jax.random.split(key, 4)
        X = jax.random.normal(k1, (4, 512, D_MODEL), dtype=jnp.float32)
        Wq = jax.random.normal(k2, (D_MODEL, D_QUERY), dtype=jnp.float32) * (1.0 / math.sqrt(D_MODEL))
        Wk = jax.random.normal(k3, (D_MODEL, D_QUERY), dtype=jnp.float32) * (1.0 / math.sqrt(D_MODEL))
        Wv = jax.random.normal(k4, (D_MODEL, D_MODEL), dtype=jnp.float32) * (1.0 / math.sqrt(D_MODEL))
        return {'X': X, 'Wq': Wq, 'Wk': Wk, 'Wv': Wv}
    _L1_attn_in = _L1_attn_setup()

    def _L1_ffn_setup():
        import jax, jax.numpy as jnp
        import numpy as np
        DIM = 128
        NUM_EXPERTS = 8
        ACTIVE_EXPERTS = 2
        EXPERT_DIM = 256
        key = jax.random.key(seed)
        k1, k2, k3, k4 = jax.random.split(key, 4)
        x = jax.random.normal(k1, (1, 256, DIM), dtype=jnp.float32)
        gate_w = jax.random.normal(k2, (NUM_EXPERTS, DIM), dtype=jnp.float32) * 0.02
        balance_bias = jnp.zeros((NUM_EXPERTS,), dtype=jnp.float32)
        w1 = jax.random.normal(k3, (NUM_EXPERTS, EXPERT_DIM, DIM), dtype=jnp.float32) * 0.02
        w2 = jax.random.normal(k4, (NUM_EXPERTS, DIM, EXPERT_DIM), dtype=jnp.float32) * 0.02
        return {'x': x, 'gate_w': gate_w, 'balance_bias': balance_bias, 'w1': w1, 'w2': w2}
    _L1_ffn_in = _L1_ffn_setup()
    _d = {'L0_attn_x': _L0_attn_in['x'], 'L0_attn_w_qkv': _L0_attn_in['w_qkv'], 'L0_attn_b_qkv': _L0_attn_in['b_qkv'], 'L0_attn_w_proj': _L0_attn_in['w_proj'], 'L0_attn_b_proj': _L0_attn_in['b_proj'], 'L0_ffn_gate_w': _L0_ffn_in['gate_w'], 'L0_ffn_w1': _L0_ffn_in['w1'], 'L0_ffn_w2': _L0_ffn_in['w2'], 'L1_attn_Wq': _L1_attn_in['Wq'], 'L1_attn_Wk': _L1_attn_in['Wk'], 'L1_attn_Wv': _L1_attn_in['Wv'], 'L1_ffn_gate_w': _L1_ffn_in['gate_w'], 'L1_ffn_balance_bias': _L1_ffn_in['balance_bias'], 'L1_ffn_w1': _L1_ffn_in['w1'], 'L1_ffn_w2': _L1_ffn_in['w2']}
    _x0 = _d['L0_attn_x']
    _d['L0_attn_x'] = jax.random.normal(jax.random.fold_in(jax.random.key(seed), 1), (16, 512, 128), dtype=_x0.dtype)
    del _x0
    return _d

def reference(L0_attn_x, L0_attn_w_qkv, L0_attn_b_qkv, L0_attn_w_proj, L0_attn_b_proj, L0_ffn_gate_w, L0_ffn_w1, L0_ffn_w2, L1_attn_Wq, L1_attn_Wk, L1_attn_Wv, L1_ffn_gate_w, L1_ffn_balance_bias, L1_ffn_w1, L1_ffn_w2):

    def _L0_attn_ref(x, w_qkv, b_qkv, w_proj, b_proj):
        import jax, jax.numpy as jnp
        import numpy as np
        B, N, C = (2, 256, 128)
        H = 8
        WS = 32
        D = C // H
        b, n, c = x.shape
        qkv = x @ w_qkv.T + b_qkv
        qkv = qkv.reshape(b, n, 3, H, D).transpose(2, 0, 3, 1, 4)
        q, k, v = (qkv[0], qkv[1], qkv[2])
        attn = jnp.einsum('bhqd,bhkd->bhqk', q, k) / jnp.sqrt(jnp.asarray(c, x.dtype))
        i = jnp.arange(n)[:, None]
        j = jnp.arange(n)[None, :]
        band = jnp.abs(i - j) < WS // 2
        attn = jnp.where(band, attn, -jnp.inf)
        attn = jax.nn.softmax(attn, axis=-1)
        out = jnp.einsum('bhqk,bhkd->bhqd', attn, v)
        out = out.transpose(0, 2, 1, 3).reshape(b, n, c)
        return out @ w_proj.T + b_proj

    def _L0_ffn_ref(x, gate_w, w1, w2):
        import jax, jax.numpy as jnp
        import numpy as np
        import math
        D_MODEL = 128
        N_EXPERTS = 16
        D_FF = 512
        CAP_FACTOR = 1.25
        MIN_CAPACITY = 4

        def _capacity(num_tokens, num_experts):
            cap = math.floor(CAP_FACTOR * num_tokens / num_experts)
            cap += cap % 2
            return max(cap, MIN_CAPACITY)

        def _top1_router(gate_logits, capacity):
            s, e = gate_logits.shape
            probs = jax.nn.softmax(gate_logits, axis=-1)
            top1 = jnp.argmax(gate_logits, axis=-1)
            mask = jax.nn.one_hot(top1, e, dtype=jnp.int32)
            ranks = jnp.cumsum(mask, axis=0) - 1
            mask = mask * (ranks < capacity).astype(jnp.int32)
            rank1 = jnp.sum(mask * ranks, axis=-1)
            ranks_oh = jax.nn.one_hot(rank1, capacity, dtype=probs.dtype)
            weight = mask.astype(probs.dtype) * probs
            combine_weights = weight[:, :, None] * ranks_oh[:, None, :]
            sec_mask = combine_weights > 0
            return (combine_weights, sec_mask)
        tokens = x.reshape(-1, D_MODEL)
        s = tokens.shape[0]
        capacity = _capacity(s, N_EXPERTS)
        gate_logits = tokens.astype(jnp.float32) @ gate_w.T
        combine_weights, sec_mask = _top1_router(gate_logits, capacity)
        dispatch = jnp.einsum('sec,sd->ecd', sec_mask.astype(tokens.dtype), tokens)
        h = jax.nn.gelu(jnp.einsum('ecd,edf->ecf', dispatch, w1))
        expert_out = jnp.einsum('ecf,efd->ecd', h, w2)
        out = jnp.einsum('sec,ecd->sd', combine_weights.astype(tokens.dtype), expert_out)
        return out.reshape(x.shape)

    def _L1_attn_ref(X, Wq, Wk, Wv):
        import jax, jax.numpy as jnp
        import numpy as np
        import math
        D_MODEL = 128
        D_QUERY = 64
        B, T, _ = X.shape
        Q = X @ Wq
        K = X @ Wk
        V = X @ Wv
        scores = jnp.einsum('btd,bsd->bts', Q, K)
        causal = jnp.tril(jnp.ones((T, T), dtype=bool))
        scores = jnp.where(causal[None, :, :], scores, -jnp.inf)
        attn = jax.nn.softmax(scores / math.sqrt(D_QUERY), axis=2)
        return attn @ V

    def _L1_ffn_ref(x, gate_w, balance_bias, w1, w2):
        import jax, jax.numpy as jnp
        import numpy as np
        DIM = 128
        NUM_EXPERTS = 8
        ACTIVE_EXPERTS = 2
        EXPERT_DIM = 256
        B, S, D = x.shape
        T = B * S
        xf = x.reshape(T, D)
        gate_logits = jnp.einsum('td,ed->te', xf, gate_w)
        gate_scores = jax.nn.sigmoid(gate_logits + balance_bias)
        topk_scores, topk_idx = jax.lax.top_k(gate_scores, ACTIVE_EXPERTS)
        topk_scores = topk_scores / (topk_scores.sum(axis=-1, keepdims=True) + 1e-06)
        comb = jnp.zeros((T, NUM_EXPERTS), dtype=x.dtype)
        comb = comb.at[jnp.arange(T)[:, None], topk_idx].add(topk_scores)
        h = jax.nn.silu(jnp.einsum('td,ehd->teh', xf, w1))
        expert_out = jnp.einsum('teh,edh->ted', h, w2)
        out = jnp.einsum('te,ted->td', comb, expert_out)
        return out.reshape(B, S, D)
    x = L0_attn_x
    x = _layernorm(x + _L0_attn_ref(x, L0_attn_w_qkv, L0_attn_b_qkv, L0_attn_w_proj, L0_attn_b_proj), axis=-1)
    x = _layernorm(x + _L0_ffn_ref(x, L0_ffn_gate_w, L0_ffn_w1, L0_ffn_w2), axis=-1)
    x = _layernorm(x + _L1_attn_ref(x, L1_attn_Wq, L1_attn_Wk, L1_attn_Wv), axis=-1)
    x = _layernorm(x + _L1_ffn_ref(x, L1_ffn_gate_w, L1_ffn_balance_bias, L1_ffn_w1, L1_ffn_w2), axis=-1)
    return x

_drawn_inputs = setup_inputs


def setup_inputs(seed=0):
    import zlib

    import numpy as np

    out = dict(_drawn_inputs(seed))
    spreads = {'L0_attn_b_qkv': (0.0, 0.1),
     'L0_attn_b_proj': (0.0, 0.1),
     'L1_ffn_balance_bias': (0.0, 0.1)}
    factors = {}
    for name, (base, spread) in spreads.items():
        noise = np.random.default_rng([zlib.crc32(name.encode()), seed]).standard_normal(out[name].shape)
        drawn = base * np.exp(spread * noise) if base else spread * noise
        out[name] = jnp.asarray(drawn.astype(out[name].dtype))
    for name, factor in factors.items():
        out[name] = (out[name] * factor).astype(out[name].dtype)
    return out
```

```python
from contextlib import ExitStack

import concourse.bass as bass
from concourse import mybir

F32 = mybir.dt.float32
BF16 = mybir.dt.bfloat16
U32 = mybir.dt.uint32
ALU = mybir.AluOpType
ACT = mybir.ActivationFunctionType
AX = mybir.AxisListType.X

P = 128
SEQ = 512
NSEQ = 16
TPS = SEQ // P
NT = NSEQ * TPS
C = 128
EPS = 1e-5

H0, D0, BAND = 8, 16, 16
QB = 32
WIN = QB + 2 * BAND
NBLK = P // QB
PAD = BAND
SEQP = SEQ + 2 * PAD

E0, F0 = 16, 512
CAP = 640
SLOTS = E0 * CAP
NCAP = CAP // P

DQ = 64
E1, F1 = 8, 256

BLK1 = 2 * P
REGION1 = NT * P // BLK1 + 1
SPARE1 = E1
TILES1 = 72

UNROLL = 2 * TPS


def wait(eng, sem, n):
    if not (isinstance(n, int) and n <= 0):
        eng.wait_ge(sem, n)


def wait_apart(eng, sem, n):
    if not isinstance(n, int):
        n = eng.to_reg(n)
        eng.wait_ge(sem, 1)
        eng.wait_ge(sem, n)
    elif n > 0:
        eng.wait_ge(sem, n)


def lagged(it, s, lag, total=NT):
    return not isinstance(it, int) or 0 <= UNROLL * it + s - lag < total


def steps(eng, body, peel, lag):
    for it in range(peel):
        for s in range(UNROLL):
            body(it, s)
    with eng.Fori(peel, NT // UNROLL - 1) as it:
        for s in range(UNROLL):
            body(it, s)
    for s in range(UNROLL + lag + 1):
        body(NT // UNROLL - 1 + s // UNROLL, s % UNROLL)


def phase_attention0(nc, dram, const, sem, ctx):
    def sb(name, shape, dt=F32):
        return ctx.enter_context(nc.sbuf_tensor("a_" + name, shape, dt))

    def ps(name, shape=(P, 512)):
        return ctx.enter_context(nc.psum_tensor("a_ps_" + name, list(shape), F32))

    wq, wk, wv, wp = (sb(n, [P, C]) for n in ("wq", "wk", "wv", "wp"))
    bqkv = sb("bqkv", [P, 3])
    bproj = sb("bproj", [P, C])
    gate_w = sb("gate_w", [P, E0])
    maskf = sb("maskf", [P, 3 * WIN])
    mask = sb("mask", [P, 3, WIN], BF16)
    ident16 = sb("ident16", [P, P], BF16)
    ones16 = sb("ones16", [P, P], BF16)
    tri_f = sb("tri_f", [P, P])
    tri16 = sb("tri16", [P, P], BF16)
    rev = sb("rev", [P, TPS, E0])
    zeros = sb("zeros", [P, 1280])

    x = [sb(f"x{i}", [P, TPS, C]) for i in range(2)]
    xT = [sb(f"xT{i}", [P, SEQP]) for i in range(2)]
    kT = sb("kT", [P, SEQ])
    kexp = [sb(f"kexp{i}", [P, H0, SEQP]) for i in range(2)]
    qT = [sb(f"qT{i}", [P, SEQ]) for i in range(2)]
    vexp = [sb(f"vexp{i}", [P, NBLK, 4, 32]) for i in range(TPS)]
    prob = [sb(f"prob{i}", [P, H0, WIN]) for i in range(TPS)]
    probT = [sb(f"probT{i}", [P, 4, P]) for i in range(2)]
    attT = [sb(f"attT{i}", [P, P]) for i in range(2)]
    mx = [sb(f"mx{i}", [P, H0]) for i in range(2)]
    sm = [sb(f"sm{i}", [P, H0]) for i in range(2)]
    rinv = [sb(f"rinv{i}", [P, H0]) for i in range(TPS)]
    res = [sb(f"res{i}", [P, TPS, C]) for i in range(2)]
    y = [sb(f"y{i}", [P, TPS, C]) for i in range(2)]
    yT = sb("yT", [P, SEQ])
    st = [sb(f"st{i}", [P, TPS, 6]) for i in range(2)]
    ln = [sb(f"ln{i}", [P, 6, TPS]) for i in range(2)]
    mv = [sb(f"mv{i}", [P, TPS, 2]) for i in range(2)]
    lmax = sb("lmax", [P, TPS])
    lsub = sb("lsub", [P, TPS, E0])
    lexp = sb("lexp", [P, TPS, E0])
    first = sb("first", [P, TPS, E0])
    rmx = sb("rmx", [P, TPS])
    onehot = sb("onehot", [P, TPS, E0], BF16)
    ranked = sb("ranked", [P, TPS, E0])
    seen = sb("seen", [P, E0], BF16)
    batch_n = sb("batch_n", [P, E0])
    g = sb("g", [P, 6, TPS])
    gweight = [sb(f"gweight{i}", [P, TPS]) for i in range(2)]
    slot = [sb(f"slot{i}", [P, TPS], U32) for i in range(2)]

    p_qk, p_v, p_pt, p_av, p_pj, p_g = (ps(n) for n in ("qk", "v", "pt", "av", "pj", "g"))
    p_s = [ps(f"s{i}") for i in range(2)]
    eps, ident = const["eps"], const["ident"]

    block = ctx.enter_context(nc.Block())
    x_rows = dram["x"].rearrange("b (t p) c -> b p t c", p=P)
    x1_rows = dram["x1"].rearrange("(b t p) c -> b p t c", p=P, t=TPS)

    @block.sync
    def _(sp):
        def load_xT(b, par):
            sp.dma_start(xT[par][:, PAD:PAD + SEQ], dram["xT"][b]).then_inc(sem[f"a_xT_in{par}"], 16)

        def spread_keys(par):
            for h in range(H0):
                rows = slice(D0 * h, D0 * h + D0)
                sp.dma_start(kexp[par][rows, h, PAD:PAD + SEQ], kT[rows, :]).then_inc(sem[f"a_kexp_in{par}"], 16)

        for dst, src in ((wq, dram["wqkvT"][:, 0:C]), (wk, dram["wqkvT"][:, C:2 * C]),
                         (wv, dram["wv_by_parity"]), (wp, dram["wprojT"]), (bqkv, dram["bqkv"]),
                         (maskf, dram["band_mask"]), (tri_f, dram["before"]), (gate_w, dram["gate0T"])):
            sp.dma_start(dst[:, :], src).then_inc(sem["a_const_in"], 16)
        sp.dma_start(ident[:, :], dram["ident"]).then_inc(sem["a_const_in"], 16)
        sp.dma_start(rev[:, :, :], dram["rev"].rearrange("p (t e) -> p t e", e=E0)).then_inc(sem["a_const_in"], 16)
        sp.dma_start(bproj[:, :], dram["bproj"]).then_inc(sem["a_const_in"], 16)
        sp.wait_ge(sem["a_zero"], 1)
        slots_flat = dram["slots"].rearrange("(n p r) c -> n p (r c)", p=P, r=10)
        load_xT(0, 0)
        sp.dma_start(x[0][:, :, :], x_rows[0]).then_inc(sem["a_x_in0"], 16)
        for n in range(SLOTS // (P * 10)):
            sp.dma_start(slots_flat[n], zeros[:, :]).then_inc(sem["slots_zeroed"], 16)
        sp.dma_start(dram["yslots"][SLOTS:SLOTS + 1, :], zeros[0:1, 0:C]).then_inc(sem["slots_zeroed"], 16)

        sp.wait_ge(sem["a_k_sb"], 1)
        spread_keys(0)

        def body(it, s):
            t, par = s % TPS, (s // TPS) % 2
            b = 2 * it + par
            if t == 0 and lagged(it, s, -4):
                wait(sp, sem["a_v_ps"], TPS * b)
                load_xT(b + 1, 1 - par)
            if t == 2 and lagged(it, s, -2):
                wait(sp, sem["a_k_sb"], b + 2)
                wait(sp, sem["a_s_ps"], TPS * b)
                spread_keys(1 - par)
            if t == 3 and lagged(it, s, -1):
                wait(sp, sem["a_res"], TPS * b)
                sp.dma_start(x[1 - par][:, :, :], x_rows[b + 1]).then_inc(sem[f"a_x_in{1 - par}"], 16)
            if t == 1 and lagged(it, s, 9):
                q = par
                bb = b - 2
                sp.wait_ge(sem["a_y"], TPS * (bb + 1))
                sp.dma_start(x1_rows[bb], y[q][:, :, :]).then_inc(sem[f"a_y_out{q}"], 16)
            if t == 3 and lagged(it, s, 11):
                q = par
                bb = b - 2
                sp.wait_ge(sem["a_slot"], bb + 1)
                sp.dma_start(dram["slot_of"][bb], slot[q][:, :]).then_inc(sem[f"a_meta_out{q}"], 16)
                sp.dma_start(dram["weight_of"][bb], gweight[q][:, :]).then_inc(sem[f"a_meta_out{q}"], 16)
        steps(sp, body, 2, 11)
        for q in range(2):
            sp.wait_ge(sem[f"a_y_out{q}"], 16 * NSEQ // 2)
            sp.wait_ge(sem[f"a_meta_out{q}"], 32 * NSEQ // 2)

    @block.tensor
    def _(pe):
        def project(w, b_it, par, done):
            last = nc.tensor.matmul(p_qk[:, :], w[:, :], xT[par][:, PAD:PAD + SEQ], start=True, stop=True)
            last.then_inc(done, 1)

        pe.wait_ge(sem["a_const_in"], 16 * 11)
        pe.wait_ge(sem["a_setup"], 1)
        pe.wait_ge(sem["a_xT_in0"], 16)
        project(wk, 0, 0, sem["a_k_ps"])
        pe.wait_ge(sem["a_k_sb"], 1)
        project(wq, 0, 0, sem["a_q_ps"])

        def body(it, s):
            t, par = s % TPS, (s // TPS) % 2
            n = UNROLL * it + s
            b = 2 * it + par
            if lagged(it, s, 2):
                pe.wait_ge(sem["a_norm"], n - 1)
                wait(pe, sem["a_pt_sb"], n - 2)
                for hp in range(4):
                    last = nc.tensor.transpose(p_pt[:, hp * P:hp * P + P], prob[(s - 2) % TPS][:, 2 * hp:2 * hp + 2, :]
                                               .rearrange("p a b -> p (a b)"),
                                               ident[:, :])
                last.then_inc(sem["a_pt_ps"], 1)
            if lagged(it, s, 3):
                pe.wait_ge(sem["a_pt_sb"], n - 2)
                pe.wait_ge(sem["a_v_sb"], n - 2)
                wait(pe, sem["a_att_sb"], n - 3)
                for j in range(NBLK):
                    for hp in range(4):
                        last = nc.tensor.matmul(p_av[32 * hp:32 * hp + 32, QB * j:QB * j + QB],
                                                vexp[(s - 3) % TPS][:, j, hp, :],
                                                probT[(s - 3) % 2][:, hp, QB * j:QB * j + QB], start=True, stop=True,
                                                skip_group_check=True)
                last.then_inc(sem["a_av_ps"], 1)
            if lagged(it, s, 0):
                wait(pe, sem["a_v_sb"], n)
                for j in range(NBLK):
                    for odd in range(2):
                        last = nc.tensor.matmul(p_v[64 * odd:64 * odd + 64, 64 * j:64 * j + 64],
                                                xT[par][:, P * t + QB * j:P * t + QB * j + WIN],
                                                wv[:, 64 * odd:64 * odd + 64], start=True, stop=True, skip_group_check=True)
                last.then_inc(sem["a_v_ps"], 1)
                if t == 0:
                    pe.wait_ge(sem["a_q_sb"], b + 1)
                    pe.wait_ge(sem[f"a_kexp_in{par}"], 16 * H0 * (it + 1))
                wait(pe, sem["a_sub"], n - 1)
                out = p_s[s % 2]
                edge = 1 if t == 0 else 2 if t == TPS - 1 else 0
                for j in range(NBLK):
                    m = edge if (t == 0 and j == 0) or (t == TPS - 1 and j == NBLK - 1) else 0
                    q = slice(QB * j, QB * j + QB)
                    nc.tensor.matmul(out[q, :], ident16[:, q], mask[:, m:m + 1, :].to_broadcast([P, H0, WIN]),
                                     start=True, stop=False, skip_group_check=True)
                for j in range(NBLK):
                    q = slice(QB * j, QB * j + QB)
                    last = nc.tensor.matmul(out[q, :], qT[par][:, P * t + QB * j:P * t + QB * j + QB],
                                            kexp[par][:, :, P * t + QB * j:P * t + QB * j + WIN], start=False, stop=True,
                                            skip_group_check=True)
                last.then_inc(sem["a_s_ps"], 1)
            if lagged(it, s, 3):
                pe.wait_ge(sem["a_att_sb"], n - 2)
                wait(pe, sem["a_res"], n - 3)
                nc.tensor.matmul(p_pj[:, 0:C], attT[(s - 3) % 2][:, :], wp[:, :], start=True, stop=True)\
                    .then_inc(sem["a_pj_ps"], 1)
            if t == 1 and lagged(it, s, -3):
                pe.wait_ge(sem["a_q_sb"], b + 1)
                pe.wait_ge(sem[f"a_xT_in{1 - par}"], 16 * (it + 1 + par))
                project(wk, it, 1 - par, sem["a_k_ps"])
            if t == 2 and lagged(it, s, -2):
                pe.wait_ge(sem["a_k_sb"], b + 2)
                project(wq, it, 1 - par, sem["a_q_ps"])
            if t == 0 and lagged(it, s, 8):
                bb = b - 2
                pe.wait_ge(sem["a_y"], TPS * (bb + 1))
                wait(pe, sem["a_slot"], bb)
                for u in range(TPS):
                    last = nc.tensor.transpose(p_g[:, P * u:P * u + P], y[par][:, u, :], ident[:, :])
                last.then_inc(sem["a_yT_ps"], 1)
            if t == 1 and lagged(it, s, 9):
                bb = b - 2
                pe.wait_ge(sem["a_yT_sb"], bb + 1)
                for u in range(TPS):
                    last = nc.tensor.matmul(p_g[:, E0 * u:E0 * u + E0], yT[:, P * u:P * u + P], gate_w[:, :],
                                            start=(u == 0), stop=(u == TPS - 1), skip_group_check=True)
                last.then_inc(sem["a_logit_ps"], 1)
            if t == 2 and lagged(it, s, 10):
                bb = b - 2
                pe.wait_ge(sem["a_onehot"], bb + 1)
                out = p_g[:, 64:128]
                nc.tensor.matmul(out, ones16[:, :], seen[:, :].rearrange("p (a e) -> p a e", a=1).to_broadcast([P, TPS, E0]),
                                 start=True, stop=False, skip_group_check=True)
                nc.tensor.matmul(out, tri16[:, :], onehot[:, :, :], start=False, stop=False, skip_group_check=True)
                for u in range(TPS - 1):
                    last = nc.tensor.matmul(out[:, E0 * (u + 1):64], ones16[:, :],
                                            onehot[:, u:u + 1, :].to_broadcast([P, TPS - 1 - u, E0]),
                                            start=False, stop=(u == TPS - 2), skip_group_check=True)
                last.then_inc(sem["a_rank_ps"], 1)
        steps(pe, body, 2, 11)

    @block.scalar
    def _(act):
        nc.scalar.preload_act_table_set("natural_log_exp_and_others")

        def k_out(value, par_of_old, old):
            act.wait_ge(sem["a_k_ps"], value)
            if old is not None:
                act.wait_ge(sem[f"a_kexp_in{par_of_old}"], old)
            nc.scalar.activation(kT[:, :], p_qk[:, :], ACT.Identity, bias=bqkv[:, 1:2]).then_inc(sem["a_k_sb"], 1)

        def q_out(value, par, used):
            act.wait_ge(sem["a_q_ps"], value)
            wait(act, sem["a_s_ps"], used)
            nc.scalar.activation(qT[par][:, :], p_qk[:, :], ACT.Identity, bias=bqkv[:, 0:1]).then_inc(sem["a_q_sb"], 1)

        act.wait_ge(sem["a_const_in"], 16 * 11)
        k_out(1, 0, None)
        q_out(1, 0, 0)

        def body(it, s):
            t, par = s % TPS, (s // TPS) % 2
            n = UNROLL * it + s
            b = 2 * it + par
            if t == 2 and lagged(it, s, -2):
                k_out(b + 2, par, 16 * H0 * (it + 1))
            if t == 3 and lagged(it, s, -1):
                q_out(b + 2, 1 - par, TPS * b)
            if lagged(it, s, 2):
                act.wait_ge(sem["a_pt_ps"], n - 1)
                wait(act, sem["a_av_ps"], n - 3)
                nc.scalar.copy(probT[(s - 2) % 2][:, :, :].rearrange("p a b -> p (a b)"), p_pt[:, :]).then_inc(sem["a_pt_sb"], 1)
            if lagged(it, s, 3):
                act.wait_ge(sem["a_av_ps"], n - 2)
                wait(act, sem["a_pj_ps"], n - 4)
                nc.scalar.activation(attT[(s - 3) % 2][:, :], p_av[:, 0:P], ACT.Identity, bias=bqkv[:, 2:3])\
                    .then_inc(sem["a_att_sb"], 1)
            if lagged(it, s, 0):
                act.wait_ge(sem["a_sub"], n + 1)
                e = prob[t][:, :, :].rearrange("p a b -> p (a b)")
                nc.scalar.activation(e, e, ACT.Exp, scale=float(C) ** -0.5).then_inc(sem["a_exp"], 1)
            if t == 2 and lagged(it, s, 6):
                q = (s // TPS + 1) % 2
                bb = b - 1
                act.wait_ge(sem["a_var"], TPS * (bb + 1))
                nc.scalar.activation(ln[q][:, 0, :], mv[q][:, :, 1], ACT.Ln, bias=eps[:, 0:1]).then_inc(sem["a_ln"], 1)
                act.wait_ge(sem["a_ln"], bb + 1)
                nc.scalar.activation(ln[q][:, 1, :], ln[q][:, 0, :], ACT.Exp, scale=-0.5).then_inc(sem["a_guess"], 1)
            if t == 0 and lagged(it, s, 8):
                bb = b - 2
                act.wait_ge(sem["a_yT_ps"], bb + 1)
                wait(act, sem["a_logit_ps"], bb)
                nc.scalar.copy(yT[:, :], p_g[:, :]).then_inc(sem["a_yT_sb"], 1)
            if t == 1 and lagged(it, s, 9):
                bb = b - 2
                act.wait_ge(sem["a_lsub"], bb + 1)
                wait(act, sem["a_slot"], bb)
                nc.scalar.activation(lexp[:, :, :], lsub[:, :, :], ACT.Exp).then_inc(sem["a_gate_exp"], 1)
        steps(act, body, 2, 11)

    @block.vector
    def _(dve):
        nc.vector.memset(zeros[:, :], 0.0).then_inc(sem["a_zero"], 1)
        nc.vector.memset(eps[:, :], EPS)
        nc.vector.memset(ones16[:, :], 1.0)
        nc.vector.memset(seen[:, :], 0.0)
        for q in range(2):
            nc.vector.memset(kexp[q][:, :, :], 0.0)
            nc.vector.memset(xT[q][:, 0:PAD], 0.0)
            nc.vector.memset(xT[q][:, PAD + SEQ:SEQP], 0.0)
        for t in range(TPS):
            nc.vector.memset(vexp[t][:, :, :, :], 0.0)
        dve.wait_ge(sem["a_const_in"], 16 * 11)
        nc.vector.tensor_copy(mask[:, :, :].rearrange("p a b -> p (a b)"), maskf[:, :])
        nc.vector.tensor_copy(tri16[:, :], tri_f[:, :])
        nc.vector.tensor_copy(ident16[:, :], ident[:, :]).then_inc(sem["a_setup"], 1)

        def body(it, s):
            t, par = s % TPS, (s // TPS) % 2
            n = UNROLL * it + s
            b = 2 * it + par
            if t == 3 and lagged(it, s, 7):
                q = (s // TPS + 1) % 2
                bb = b - 1
                var, guess, u, v, rstd = mv[q][:, :, 1], ln[q][:, 1, :], ln[q][:, 2, :], ln[q][:, 3, :], ln[q][:, 5, :]
                dve.wait_ge(sem["a_guess"], bb + 1)
                nc.vector.scalar_tensor_tensor(u, var, EPS, guess, ALU.add, ALU.mult).then_inc(sem["a_newton"], 1)
                dve.wait_ge(sem["a_newton"], 3 * bb + 1)
                nc.vector.tensor_tensor(v, u, guess, ALU.mult).then_inc(sem["a_newton"], 1)
                dve.wait_ge(sem["a_newton"], 3 * bb + 2)
                nc.vector.tensor_scalar(u, v, -0.5, 1.5, ALU.mult, ALU.add).then_inc(sem["a_newton"], 1)
                dve.wait_ge(sem["a_newton"], 3 * bb + 3)
                nc.vector.tensor_tensor(rstd, u, guess, ALU.mult).then_inc(sem["a_rstd"], 1)
                dve.wait_ge(sem["a_rstd"], bb + 1)
                if not isinstance(it, int) or bb >= 2:
                    dve.wait_ge(sem[f"a_scatter_out{q}"], 64 * (it if q == 0 else it - 1))
                    dve.wait_ge(sem[f"a_y_out{q}"], 16 * (it if q == 0 else it - 1))
                    dve.wait_ge(sem["a_yT_ps"], bb - 1)
                for w in range(TPS):
                    nc.vector.tensor_scalar(y[q][:, w, :], res[q][:, w, :], mv[q][:, w, 0:1], ln[q][:, 5, w:w + 1],
                                            ALU.subtract, ALU.mult).then_inc(sem["a_y"], 1)
            if lagged(it, s, 1):
                dve.wait_ge(sem["a_exp"], n)
                nc.vector.tensor_reduce(sm[(s - 1) % 2][:, :], prob[(s - 1) % TPS][:, :, :], AX, ALU.add)\
                    .then_inc(sem["a_sum"], 1)
                wait(dve, sem["a_norm"], n - 4)
                dve.wait_ge(sem["a_sum"], n)
                nc.vector.reciprocal(rinv[(s - 1) % TPS][:, :], sm[(s - 1) % 2][:, :]).then_inc(sem["a_rinv"], 1)
            if lagged(it, s, 0):
                dve.wait_ge(sem["a_v_ps"], n + 1)
                wait(dve, sem["a_av_ps"], n - 3)
                for odd in range(2):
                    rows = slice(64 * odd, 64 * odd + 64)
                    last = nc.vector.tensor_copy(vexp[t][rows, :, :, 16 * odd:16 * odd + 16],
                                                 p_v[rows, 0:256].rearrange("p (j h d) -> p j h d", j=NBLK, h=4))
                    last.then_inc(sem["a_v_half"] if odd == 0 else sem["a_v_sb"], 1)
                dve.wait_ge(sem["a_s_ps"], n + 1)
                scores = p_s[s % 2][:, :].rearrange("p (h k) -> p h k", h=H0)
                nc.vector.tensor_reduce(mx[s % 2][:, :], scores, AX, ALU.max).then_inc(sem["a_max"], 1)
                wait(dve, sem["a_pt_ps"], n - 3)
                dve.wait_ge(sem["a_max"], n + 1)
                nc.vector.tensor_tensor(prob[t][:, :, :], scores,
                                        mx[s % 2][:, :].rearrange("p (h a) -> p h a", a=1).to_broadcast([P, H0, WIN]),
                                        ALU.subtract).then_inc(sem["a_sub"], 1)
            if lagged(it, s, 3):
                u, q = (s - 3) % TPS, ((s - 3) // TPS) % 2
                bb = b if t == 3 else b - 1
                dve.wait_ge(sem["a_pj_ps"], n - 2)
                dve.wait_ge(sem["a_xb"], bb + 1)
                wait(dve, sem["a_y"], TPS * (bb - 1))
                nc.vector.tensor_tensor(res[q][:, u, :], x[q][:, u, :], p_pj[:, 0:C], ALU.add).then_inc(sem["a_res"], 1)
                dve.wait_ge(sem["a_res"], n - 2)
                nc.vector.bn_stats(st[q][:, u, :], res[q][:, u, :]).then_inc(sem["a_bn"], 1)
            if t == 2 and lagged(it, s, 6):
                q = (s // TPS + 1) % 2
                bb = b - 1
                wait_apart(dve, sem["a_bn"], TPS * (bb + 1))
                for u in range(TPS):
                    nc.vector.bn_aggr(mv[q][:, u, :], st[q][:, u, :]).then_inc(sem["a_var"], 1)
            if t == 1 and lagged(it, s, 9):
                bb = b - 2
                dve.wait_ge(sem["a_logit_ps"], bb + 1)
                logits = p_g[:, 0:64].rearrange("p (t e) -> p t e", t=TPS)
                nc.vector.tensor_reduce(lmax[:, :], logits, AX, ALU.max).then_inc(sem["a_lmax"], 1)
                dve.wait_ge(sem["a_lmax"], bb + 1)
                wait(dve, sem["a_gate_exp"], bb)
                nc.vector.tensor_tensor(lsub[:, :, :], logits,
                                        lmax[:, :].rearrange("p (t a) -> p t a", a=1).to_broadcast([P, TPS, E0]),
                                        ALU.subtract).then_inc(sem["a_lsub"], 1)
                dve.wait_ge(sem["a_lsub"], bb + 1)
                nc.vector.scalar_tensor_tensor(first[:, :, :], lsub[:, :, :], 0.0, rev[:, :, :], ALU.is_ge, ALU.mult)\
                    .then_inc(sem["a_first"], 1)
                dve.wait_ge(sem["a_first"], bb + 1)
                nc.vector.tensor_reduce(rmx[:, :], first[:, :, :], AX, ALU.max).then_inc(sem["a_rmx"], 1)
                dve.wait_ge(sem["a_rmx"], bb + 1)
                nc.vector.tensor_tensor(onehot[:, :, :], rev[:, :, :],
                                        rmx[:, :].rearrange("p (t a) -> p t a", a=1).to_broadcast([P, TPS, E0]),
                                        ALU.is_equal).then_inc(sem["a_onehot"], 1)
            if t == 2 and lagged(it, s, 10):
                bb, q = b - 2, par
                valid, rank, off, inside, total, gprob = (g[:, i, :] for i in range(6))
                dve.wait_ge(sem["a_rank_ps"], bb + 1)
                nc.vector.tensor_tensor(ranked[:, :, :], p_g[:, 64:128].rearrange("p (t e) -> p t e", t=TPS),
                                        onehot[:, :, :], ALU.mult).then_inc(sem["a_ranked"], 1)
                nc.vector.tensor_reduce(batch_n[:, :], onehot[:, :, :].rearrange("p t e -> p e t"), AX, ALU.add)\
                    .then_inc(sem["a_batch_n"], 1)
                dve.wait_ge(sem["a_gate_exp"], bb + 1)
                nc.vector.tensor_reduce(total, lexp[:, :, :], AX, ALU.add).then_inc(sem["a_total"], 1)
                dve.wait_ge(sem["a_ranked"], bb + 1)
                nc.vector.tensor_reduce(rank, ranked[:, :, :], AX, ALU.add).then_inc(sem["a_rank"], 1)
                dve.wait_ge(sem["a_batch_n"], bb + 1)
                nc.vector.tensor_tensor(seen[:, :], seen[:, :], batch_n[:, :], ALU.add)
                dve.wait_ge(sem["a_total"], bb + 1)
                nc.vector.reciprocal(gprob, total).then_inc(sem["a_gprob"], 1)
                dve.wait_ge(sem["a_rank"], bb + 1)
                nc.vector.tensor_scalar(valid, rank, float(CAP), None, ALU.is_lt).then_inc(sem["a_valid"], 1)
                nc.vector.scalar_tensor_tensor(off, rmx[:, :], -float(CAP), rank, ALU.mult, ALU.add)\
                    .then_inc(sem["a_valid"], 1)
                dve.wait_ge(sem["a_valid"], 2 * (bb + 1))
                nc.vector.tensor_tensor(inside, off, valid, ALU.mult).then_inc(sem["a_inside"], 1)
                if not isinstance(it, int) or bb >= 2:
                    dve.wait_ge(sem[f"a_scatter_out{q}"], 64 * (it - 1))
                    dve.wait_ge(sem[f"a_meta_out{q}"], 32 * (it - 1))
                dve.wait_ge(sem["a_gprob"], bb + 1)
                nc.vector.tensor_tensor(gweight[q][:, :], gprob, valid, ALU.mult)
                dve.wait_ge(sem["a_inside"], bb + 1)
                nc.vector.tensor_scalar(slot[q][:, :], inside, float(SLOTS), None, ALU.add).then_inc(sem["a_slot"], 1)
        steps(dve, body, 2, 11)

    @block.gpsimd
    def _(pool):
        pool.wait_ge(sem["a_const_in"], 16 * 11)

        def body(it, s):
            t, par = s % TPS, (s // TPS) % 2
            n = UNROLL * it + s
            b = 2 * it + par
            if lagged(it, s, 1):
                pool.wait_ge(sem["a_rinv"], n)
                e = prob[(s - 1) % TPS][:, :, :]
                nc.gpsimd.tensor_tensor(e, e, rinv[(s - 1) % TPS][:, :].rearrange("p (h a) -> p h a", a=1)
                                        .to_broadcast([P, H0, WIN]), ALU.mult).then_inc(sem["a_norm"], 1)
            if t == 1 and lagged(it, s, 1):
                pool.wait_ge(sem[f"a_x_in{par}"], 16 * (it + 1))
                nc.gpsimd.tensor_tensor(x[par][:, :, :], x[par][:, :, :],
                                        bproj[:, :].rearrange("p (a c) -> p a c", a=1).to_broadcast([P, TPS, C]),
                                        ALU.add).then_inc(sem["a_xb"], 1)
            if t == 3 and lagged(it, s, 11):
                bb, q = b - 2, par
                pool.wait_ge(sem["a_slot"], bb + 1)
                wait_apart(pool, sem["a_y"], TPS * (bb + 1))
                if isinstance(it, int) and bb == 0:
                    pool.wait_ge(sem["slots_zeroed"], 16 * (SLOTS // (P * 10) + 1))
                for u in range(TPS):
                    pool.indirect_dma_start(dram["slots"], bass.IndirectOffsetOnAxis(slot[q][:, u:u + 1], 0),
                                            y[q][:, u, :], None, bounds_check=SLOTS - 1, oob_is_err=False)\
                        .then_inc(sem[f"a_scatter_out{q}"], 16)
        steps(pool, body, 2, 11)
        for q in range(2):
            pool.wait_ge(sem[f"a_scatter_out{q}"], 64 * NSEQ // 2)


def phase_experts0(nc, dram, const, sem, ctx):
    def sb(name, shape, dt=F32):
        return ctx.enter_context(nc.sbuf_tensor("b_" + name, shape, dt))

    def ps(name):
        return ctx.enter_context(nc.psum_tensor("b_ps_" + name, [P, 512], F32))

    FC = F0 // P
    HALF = CAP // 2
    ident = const["ident"]
    xs = [sb(f"xs{i}", [P, NCAP, C]) for i in range(2)]
    w1 = [sb(f"w1{i}", [P, F0]) for i in range(2)]
    w2 = [sb(f"w2{i}", [P, FC, C]) for i in range(2)]
    xsT = [sb(f"xsT{i}", [P, CAP]) for i in range(2)]
    hT = [sb(f"hT{i}", [P, FC, CAP]) for i in range(2)]
    ys = [sb(f"ys{i}", [P, NCAP, C]) for i in range(2)]
    p_x = [ps("x0"), ps("x1")]
    p_h = [ps(f"h{i}") for i in range(4)]
    p_y = [ps("y0"), ps("y1")]
    slots = dram["slots"].rearrange("(e t p) c -> e p t c", p=P, t=NCAP)
    yslots = dram["yslots"][0:SLOTS, :].rearrange("(e t p) c -> e p t c", p=P, t=NCAP)
    w2_rows = dram["w2_0"].rearrange("e (k p) c -> e p k c", p=P)
    units = [(k, half) for k in range(FC) for half in range(2)]
    NU = len(units)
    block = ctx.enter_context(nc.Block())

    def turns(eng, body):
        for par in range(2):
            body(0, par, par == 0, False)
        with eng.Fori(1, E0 // 2 - 1) as it:
            for par in range(2):
                body(it, par, False, False)
        for par in range(2):
            body(E0 // 2 - 1, par, False, par == 1)

    @block.sync
    def _(sp):
        def load(e, par):
            sp.dma_start(xs[par][:, :, :], slots[e]).then_inc(sem[f"b_xs_in{par}"], 16)
            sp.dma_start(w1[par][:, :], dram["w1_0"][e]).then_inc(sem[f"b_w1_in{par}"], 16)
            sp.dma_start(w2[par][:, :, :], w2_rows[e]).then_inc(sem[f"b_w2_in{par}"], 16)

        load(0, 0)

        def body(it, par, first, last):
            e = 2 * it + par
            if not last:
                wait(sp, sem["b_y_ps"], e)
                load(e + 1, 1 - par)
            wait(sp, sem["b_ys_sb"], 2 * e + 2)
            sp.dma_start(yslots[e], ys[par][:, :, :]).then_inc(sem[f"b_ys_out{par}"], 16)
        turns(sp, body)
        for par in range(2):
            sp.wait_ge(sem[f"b_ys_out{par}"], 16 * E0 // 2)

    @block.tensor
    def _(pe):
        def turn_rows(e, par, rounds):
            pe.wait_ge(sem[f"b_xs_in{par}"], 16 * rounds)
            wait(pe, sem["b_xsT_sb"], 2 * e)
            for t in range(NCAP):
                last = nc.tensor.transpose(p_x[t // 4][:, P * (t % 4):P * (t % 4) + P], xs[par][:, t, :], ident[:, :])
                if t in (3, NCAP - 1):
                    last.then_inc(sem["b_xsT_ps"], 1)

        turn_rows(0, 0, 1)

        def body(it, par, first, last):
            e = 2 * it + par
            pe.wait_ge(sem["b_xsT_sb"], 2 * e + 2)
            pe.wait_ge(sem[f"b_w1_in{par}"], 16 * (it + 1))
            for u, (k, half) in enumerate(units):
                wait(pe, sem["b_gelu"], NU * e + u - 3)
                nc.tensor.matmul(p_h[u % 4][:, 0:HALF], w1[par][:, P * k:P * k + P],
                                 xsT[par][:, HALF * half:HALF * half + HALF], start=True, stop=True)\
                    .then_inc(sem["b_h_ps"], 1)
            if not last:
                turn_rows(e + 1, 1 - par, it + 1 + par)
            pe.wait_ge(sem[f"b_w2_in{par}"], 16 * (it + 1))
            pe.wait_ge(sem["b_gelu"], NU * (e + 1))
            wait(pe, sem["b_ys_sb"], 2 * e)
            for t in range(NCAP):
                for k in range(FC):
                    m = nc.tensor.matmul(p_y[t // 4][:, P * (t % 4):P * (t % 4) + P], hT[par][:, k, P * t:P * t + P],
                                         w2[par][:, k, :], start=(k == 0), stop=(k == FC - 1), skip_group_check=True)
            m.then_inc(sem["b_y_ps"], 1)
        turns(pe, body)

    @block.scalar
    def _(act):
        def body(it, par, first, last):
            e = 2 * it + par
            wait(act, sem["b_y_ps"], e - 1)
            for u, (k, half) in enumerate(units):
                act.wait_ge(sem["b_h_ps"], NU * e + u + 1)
                nc.scalar.activation(hT[par][:, k, HALF * half:HALF * half + HALF], p_h[u % 4][:, 0:HALF],
                                     ACT.Gelu_apprx_tanh).then_inc(sem["b_gelu"], 1)
        turns(act, body)

    @block.vector
    def _(dve):
        def xsT_out(e, par):
            wait(dve, sem["b_h_ps"], NU * (e - 1))
            dve.wait_ge(sem["b_xsT_ps"], 2 * e + 1)
            nc.vector.tensor_copy(xsT[par][:, 0:512], p_x[0][:, :]).then_inc(sem["b_xsT_sb"], 1)
            dve.wait_ge(sem["b_xsT_ps"], 2 * e + 2)
            nc.vector.tensor_copy(xsT[par][:, 512:CAP], p_x[1][:, 0:CAP - 512]).then_inc(sem["b_xsT_sb"], 1)

        xsT_out(0, 0)

        def body(it, par, first, last):
            e = 2 * it + par
            if not last:
                xsT_out(e + 1, 1 - par)
            wait(dve, sem[f"b_ys_out{par}"], 16 * it)
            dve.wait_ge(sem["b_y_ps"], e + 1)
            nc.vector.tensor_copy(ys[par][:, 0:4, :].rearrange("p t c -> p (t c)"), p_y[0][:, :]).then_inc(sem["b_ys_sb"], 1)
            nc.vector.tensor_copy(ys[par][:, 4, :], p_y[1][:, 0:C]).then_inc(sem["b_ys_sb"], 1)
        turns(dve, body)


def phase_attention1(nc, dram, const, sem, ctx):
    def sb(name, shape, dt=F32):
        return ctx.enter_context(nc.sbuf_tensor("c_" + name, shape, dt))

    def ps(name):
        return ctx.enter_context(nc.psum_tensor("c_ps_" + name, [P, 512], F32))

    ident, eps = const["ident"], const["eps"]
    wqk, wv = sb("wqk", [P, C]), sb("wv", [P, C])
    causal_f, causal16, ident16 = sb("causal_f", [P, P]), sb("causal16", [P, P], BF16), sb("ident16", [P, P], BF16)
    x1 = [sb(f"x1{i}", [P, TPS, C]) for i in range(2)]
    slot = [sb(f"slot{i}", [P, TPS], U32) for i in range(2)]
    weight = [sb(f"weight{i}", [P, TPS]) for i in range(2)]
    moe = [sb(f"moe{i}", [P, TPS, C]) for i in range(2)]
    res1 = sb("res1", [P, TPS, C])
    x2 = [sb(f"x2{i}", [P, TPS, C]) for i in range(2)]
    x2T = sb("x2T", [P, SEQ])
    qT = [sb(f"qT{i}", [DQ, SEQ]) for i in range(2)]
    kT = [sb(f"kT{i}", [DQ, SEQ]) for i in range(2)]
    v = [sb(f"v{i}", [P, TPS, C]) for i in range(2)]
    prob = [sb(f"prob{i}", [P, SEQ]) for i in range(TPS)]
    probT = [sb(f"probT{i}", [P, TPS, P]) for i in range(2)]
    mx = [sb(f"mx{i}", [P, 1]) for i in range(2)]
    nmx = [sb(f"nmx{i}", [P, 1]) for i in range(2)]
    sm = [sb(f"sm{i}", [P, 1]) for i in range(TPS)]
    rinv = [sb(f"rinv{i}", [P, 1]) for i in range(2)]
    res2 = [sb(f"res2{i}", [P, TPS, C]) for i in range(2)]
    x3 = [sb(f"x3{i}", [P, TPS, C]) for i in range(2)]
    st = [sb(f"st{i}", [P, TPS, 6]) for i in range(2)]
    mv = [sb(f"mv{i}", [P, TPS, 2]) for i in range(2)]
    ln = [sb(f"ln{i}", [P, 5, TPS]) for i in range(2)]
    p_x, p_qk, p_v, p_o = (ps(n) for n in ("x", "qk", "v", "o"))
    p_s = [ps(f"s{i}") for i in range(2)]
    p_pt, p_g = ps("pt"), ps("g")
    gate_w, bias = sb("gate_w", [P, E1]), sb("bias", [P, TPS, E1])
    rev, base = sb("rev", [P, TPS, E1]), sb("base", [P, TPS, E1])
    tri_f, tri16, ones16 = sb("tri_f", [P, P]), sb("tri16", [P, P], BF16), sb("ones16", [P, P], BF16)
    zeros = sb("zeros", [P, 2 * C])
    x3T = sb("x3T", [P, SEQ])
    z, ez, e1p, score, hit, score2, hit2, at, at1, at2 = (sb(f"gate{i}", [P, TPS, E1]) for i in range(10))
    hot1, hot2, hot = (sb(n, [P, TPS, E1], BF16) for n in ("hot1", "hot2", "hot"))
    seen, batch_n = const["seen"], sb("batch_n", [P, E1])
    rowf = sb("rowf", [P, 2, TPS])
    top = sb("top", [P, 2, TPS])
    who = sb("who", [P, 2, TPS])
    total = sb("total", [P, 2, TPS])
    place = [sb(f"place{i}", [P, 2, TPS], U32) for i in range(2)]
    share = [sb(f"share{i}", [P, 2, TPS]) for i in range(2)]
    x1_rows = dram["x1"].rearrange("(b t p) c -> b p t c", p=P, t=TPS)
    x3_rows = dram["x3"].rearrange("(b t p) c -> b p t c", p=P, t=TPS)
    block = ctx.enter_context(nc.Block())

    def rows_of(eng, body):
        for it in (-1, 0, 1, 2):
            for s in range(UNROLL):
                body(it, s)
        with eng.Fori(3, NT // UNROLL - 1) as it:
            for s in range(UNROLL):
                body(it, s)
        for s in range(UNROLL + 14):
            body(NT // UNROLL - 1 + s // UNROLL, s % UNROLL)

    @block.sync
    def _(sp):
        for dst, src in ((wqk, dram["wqk1"]), (wv, dram["wv1"]), (causal_f, dram["causal"])):
            sp.dma_start(dst[:, :], src).then_inc(sem["c_const_in"], 16)
        sp.dma_start(gate_w[:, :], dram["gate1T"]).then_inc(sem["c_const_in"], 16)
        sp.dma_start(tri_f[:, :], dram["before"]).then_inc(sem["c_const_in"], 16)
        for dst, src in ((bias, dram["balance"]), (rev, dram["rev1"]), (base, dram["region1"])):
            sp.dma_start(dst[:, :, :].rearrange("p t e -> p (t e)"), src).then_inc(sem["c_const_in"], 16)
        sp.wait_ge(sem["c_zero"], 1)
        spare = dram["xs1"].rearrange("(k t p) c -> k p t c", p=P, t=2)
        for k in range(SPARE1):
            sp.dma_start(spare[E1 * REGION1 + k], zeros[:, :].rearrange("p (t c) -> p t c", t=2)).then_inc(sem["c_spare"], 16)

        def body(it, s):
            t, par = s % TPS, (s // TPS) % 2
            b = 2 * it + par
            if t == 0 and lagged(it, s, -8):
                wait_apart(sp, sem["c_gathered"], b + 1)
                wait(sp, sem["c_res1"], TPS * (b + 1))
                sp.dma_start(slot[par][:, :], dram["slot_of"][b + 2]).then_inc(sem[f"c_slot_in{par}"], 16)
                sp.dma_start(weight[par][:, :], dram["weight_of"][b + 2]).then_inc(sem[f"c_x1_in{par}"], 16)
                sp.dma_start(x1[par][:, :, :], x1_rows[b + 2]).then_inc(sem[f"c_x1_in{par}"], 16)
            if t == 3 and lagged(it, s, 7):
                bb, q = b - 1, 1 - par
                sp.wait_ge(sem["c_x3"], TPS * (bb + 1))
                sp.dma_start(x3_rows[bb], x3[q][:, :, :]).then_inc(sem[f"c_x3_out{q}"], 16)
            if t == 1 and lagged(it, s, 13):
                bb, q = b - 3, 1 - par
                sp.wait_ge(sem["c_place"], 2 * (bb + 1))
                sp.dma_start(dram["place_of"][bb], place[q][:, :, :]).then_inc(sem[f"c_meta_out{q}"], 16)
                sp.dma_start(dram["share_of"][bb], share[q][:, :, :]).then_inc(sem[f"c_meta_out{q}"], 16)
        rows_of(sp, body)
        for q in range(2):
            sp.wait_ge(sem[f"c_x3_out{q}"], 16 * NSEQ // 2)
            sp.wait_ge(sem[f"c_meta_out{q}"], 32 * NSEQ // 2)
        sp.wait_ge(sem["c_spare"], 16 * SPARE1)

    @block.gpsimd
    def _(pool):
        def body(it, s):
            t, par = s % TPS, (s // TPS) % 2
            b = 2 * it + par
            if t == 1 and lagged(it, s, -7):
                pool.wait_ge(sem[f"c_slot_in{par}"], 16 * (it + 2))
                wait_apart(pool, sem["c_res1"], TPS * (b + 1))
                for u in range(TPS):
                    pool.indirect_dma_start(moe[par][:, u, :], None, dram["yslots"],
                                            bass.IndirectOffsetOnAxis(slot[par][:, u:u + 1], 0))\
                        .then_inc(sem[f"c_moe_in{par}"], 16)
                pool.wait_ge(sem[f"c_moe_in{par}"], 64 * (it + 2))
                pool.sem_inc(sem["c_gathered"], 1)
            if t == 1 and lagged(it, s, 13):
                bb, q = b - 3, 1 - par
                pool.wait_ge(sem["c_place"], 2 * (bb + 1))
                wait_apart(pool, sem["c_x3"], TPS * (bb + 1))
                for k in range(2):
                    for u in range(TPS):
                        pool.indirect_dma_start(dram["xs1"], bass.IndirectOffsetOnAxis(place[q][:, k, u:u + 1], 0),
                                                x3[q][:, u, :], None).then_inc(sem[f"c_scatter_out{q}"], 16)
        rows_of(pool, body)
        for q in range(2):
            pool.wait_ge(sem[f"c_scatter_out{q}"], 128 * NSEQ // 2)

    @block.tensor
    def _(pe):
        pe.wait_ge(sem["c_const_in"], 16 * 8)
        pe.wait_ge(sem["c_setup"], 4)

        def body(it, s):
            t, par = s % TPS, (s // TPS) % 2
            n = UNROLL * it + s
            b = 2 * it + par
            if lagged(it, s, 2):
                u = (s - 2) % TPS
                pe.wait_ge(sem["c_exp"], n - 1)
                wait(pe, sem["c_pt_sb"], n - 2)
                for c in range(u + 1):
                    last = nc.tensor.transpose(p_pt[:, P * c:P * c + P], prob[u][:, P * c:P * c + P], ident[:, :])
                last.then_inc(sem["c_pt_ps"], 1)
            if lagged(it, s, 0):
                if t == 0:
                    pe.wait_ge(sem["c_k_sb"], b + 1)
                wait(pe, sem["c_exp"], n - 1)
                nc.tensor.matmul(p_s[s % 2][:, 0:P * (t + 1)], qT[par][:, P * t:P * t + P], kT[par][:, 0:P * (t + 1)],
                                 start=True, stop=False, skip_group_check=True)
                nc.tensor.matmul(p_s[s % 2][:, P * t:P * t + P], ident16[:, :], causal16[:, :], start=False, stop=True,
                                 skip_group_check=True).then_inc(sem["c_s_ps"], 1)
            if t == 2 and lagged(it, s, -2):
                pe.wait_ge(sem["c_x2"], TPS * (b + 2))
                wait(pe, sem["c_x2T_sb"], b + 1)
                for u in range(TPS):
                    last = nc.tensor.transpose(p_x[:, P * u:P * u + P], x2[1 - par][:, u, :], ident[:, :])
                last.then_inc(sem["c_x2T_ps"], 1)
            if t == 3 and lagged(it, s, -1):
                pe.wait_ge(sem["c_x2T_sb"], b + 2)
                wait(pe, sem["c_k_sb"], b + 1)
                nc.tensor.matmul(p_qk[:, :], wqk[:, :], x2T[:, :], start=True, stop=True).then_inc(sem["c_qk_ps"], 1)
                wait(pe, sem["c_v_sb"], b + 1)
                for u in range(TPS):
                    last = nc.tensor.matmul(p_v[:, P * u:P * u + P], x2T[:, P * u:P * u + P], wv[:, :],
                                            start=True, stop=True, skip_group_check=True)
                last.then_inc(sem["c_v_ps"], 1)
            if lagged(it, s, 2):
                u, q = (s - 2) % TPS, ((s - 2) // TPS) % 2
                pe.wait_ge(sem["c_pt_sb"], n - 1)
                pe.wait_ge(sem["c_v_sb"], (b if t >= 2 else b - 1) + 1)
                wait(pe, sem["c_res2"], n - 2)
                for c in range(u + 1):
                    last = nc.tensor.matmul(p_o[:, 0:C], probT[s % 2][:, c, :], v[q][:, c, :],
                                            start=(c == 0), stop=(c == u))
                last.then_inc(sem["c_o_ps"], 1)
            if t == 0 and lagged(it, s, 8):
                bb, q = b - 2, par
                pe.wait_ge(sem["c_x3"], TPS * (bb + 1))
                wait(pe, sem["c_at"], bb)
                for u in range(TPS):
                    last = nc.tensor.transpose(p_g[:, P * u:P * u + P], x3[q][:, u, :], ident[:, :])
                last.then_inc(sem["c_x3T_ps"], 1)
            if t == 1 and lagged(it, s, 9):
                bb = b - 2
                pe.wait_ge(sem["c_x3T_sb"], bb + 1)
                for u in range(TPS):
                    last = nc.tensor.matmul(p_g[:, E1 * u:E1 * u + E1], x3T[:, P * u:P * u + P], gate_w[:, :],
                                            start=(u == 0), stop=(u == TPS - 1), skip_group_check=True)
                last.then_inc(sem["c_logit_ps"], 1)
            if t == 3 and lagged(it, s, 11):
                bb = b - 2
                pe.wait_ge(sem["c_hot"], bb + 1)
                out = p_g[:, 64:64 + TPS * E1]
                nc.tensor.matmul(out, ones16[:, :], seen[:, :].rearrange("p (a e) -> p a e", a=1).to_broadcast([P, TPS, E1]),
                                 start=True, stop=False, skip_group_check=True)
                nc.tensor.matmul(out, tri16[:, :], hot[:, :, :], start=False, stop=False, skip_group_check=True)
                for u in range(TPS - 1):
                    last = nc.tensor.matmul(out[:, E1 * (u + 1):TPS * E1], ones16[:, :],
                                            hot[:, u:u + 1, :].to_broadcast([P, TPS - 1 - u, E1]),
                                            start=False, stop=(u == TPS - 2), skip_group_check=True)
                last.then_inc(sem["c_rank_ps"], 1)
        rows_of(pe, body)

    @block.scalar
    def _(act):
        nc.scalar.preload_act_table_set("natural_log_exp_and_others")

        def body(it, s):
            t, par = s % TPS, (s // TPS) % 2
            n = UNROLL * it + s
            b = 2 * it + par
            if lagged(it, s, 2):
                u = (s - 2) % TPS
                act.wait_ge(sem["c_pt_ps"], n - 1)
                wait(act, sem["c_o_ps"], n - 3)
                nc.scalar.copy(probT[s % 2][:, 0:u + 1, :].rearrange("p a b -> p (a b)"), p_pt[:, 0:P * (u + 1)])\
                    .then_inc(sem["c_pt_sb"], 1)
            if lagged(it, s, 0):
                act.wait_ge(sem["c_nmax"], n + 1)
                wait(act, sem["c_pt_ps"], n - 3)
                wait(act, sem["c_rinv"], n - 3)
                nc.scalar.activation(prob[t][:, 0:P * (t + 1)], p_s[s % 2][:, 0:P * (t + 1)], ACT.Exp,
                                     bias=nmx[s % 2][:, 0:1], scale=float(DQ) ** -0.5,
                                     accum_out=sm[t][:, 0:1]).then_inc(sem["c_exp"], 1)
            if t == 0 and lagged(it, s, -4):
                act.wait_ge(sem["c_var1"], TPS * (b + 2))
                nc.scalar.activation(ln[0][:, 0, :], mv[0][:, :, 1], ACT.Ln, bias=eps[:, 0:1]).then_inc(sem["c_ln1"], 1)
                act.wait_ge(sem["c_ln1"], b + 2)
                nc.scalar.activation(ln[0][:, 1, :], ln[0][:, 0, :], ACT.Exp, scale=-0.5).then_inc(sem["c_guess1"], 1)
            if t == 1 and lagged(it, s, 5):
                bb = b - 1
                act.wait_ge(sem["c_var2"], TPS * (bb + 1))
                nc.scalar.activation(ln[1][:, 0, :], mv[1][:, :, 1], ACT.Ln, bias=eps[:, 0:1]).then_inc(sem["c_ln2"], 1)
                act.wait_ge(sem["c_ln2"], bb + 1)
                nc.scalar.activation(ln[1][:, 1, :], ln[1][:, 0, :], ACT.Exp, scale=-0.5).then_inc(sem["c_guess2"], 1)
            if t == 2 and lagged(it, s, -2):
                act.wait_ge(sem["c_x2T_ps"], b + 2)
                wait(act, sem["c_v_ps"], b + 1)
                nc.scalar.copy(x2T[:, :], p_x[:, :]).then_inc(sem["c_x2T_sb"], 1)
            if t == 0 and lagged(it, s, 8):
                bb = b - 2
                act.wait_ge(sem["c_x3T_ps"], bb + 1)
                wait(act, sem["c_logit_ps"], bb)
                nc.scalar.copy(x3T[:, :], p_g[:, :]).then_inc(sem["c_x3T_sb"], 1)
            if t == 1 and lagged(it, s, 9):
                bb = b - 2
                act.wait_ge(sem["c_z"], bb + 1)
                wait(act, sem["c_e1p"], bb)
                nc.scalar.activation(ez[:, :, :], z[:, :, :], ACT.Exp, scale=-1.0).then_inc(sem["c_ez"], 1)
            if t == 3 and lagged(it, s, -1):
                act.wait_ge(sem["c_qk_ps"], b + 2)
                wait(act, sem["c_s_ps"], TPS * b)
                nc.scalar.copy(qT[1 - par][:, :], p_qk[0:DQ, :]).then_inc(sem["c_q_sb"], 1)
                nc.scalar.copy(kT[1 - par][:, :], p_qk[DQ:P, :]).then_inc(sem["c_k_sb"], 1)
        rows_of(act, body)

    @block.vector
    def _(dve):
        dve.wait_ge(sem["c_const_in"], 16 * 8)
        nc.vector.memset(zeros[:, :], 0.0).then_inc(sem["c_zero"], 1)
        nc.vector.memset(seen[:, :], 0.0)
        nc.vector.memset(ones16[:, :], 1.0).then_inc(sem["c_setup"], 1)
        nc.vector.tensor_copy(tri16[:, :], tri_f[:, :]).then_inc(sem["c_setup"], 1)
        nc.vector.tensor_copy(causal16[:, :], causal_f[:, :]).then_inc(sem["c_setup"], 1)
        nc.vector.tensor_copy(ident16[:, :], ident[:, :]).then_inc(sem["c_setup"], 1)

        def newton(k, count, norm):
            var, guess, u, w, rstd = mv[k][:, :, 1], ln[k][:, 1, :], ln[k][:, 2, :], ln[k][:, 3, :], ln[k][:, 4, :]
            done = sem[f"c_newton{k + 1}"]
            dve.wait_ge(sem[f"c_guess{k + 1}"], count + 1)
            nc.vector.scalar_tensor_tensor(u, var, EPS, guess, ALU.add, ALU.mult).then_inc(done, 1)
            dve.wait_ge(done, 4 * count + 1)
            nc.vector.tensor_tensor(w, u, guess, ALU.mult).then_inc(done, 1)
            dve.wait_ge(done, 4 * count + 2)
            nc.vector.tensor_scalar(u, w, -0.5, 1.5, ALU.mult, ALU.add).then_inc(done, 1)
            dve.wait_ge(done, 4 * count + 3)
            nc.vector.tensor_tensor(rstd, u, guess, ALU.mult).then_inc(done, 1)
            dve.wait_ge(done, 4 * count + 4)

        def body(it, s):
            t, par = s % TPS, (s // TPS) % 2
            n = UNROLL * it + s
            b = 2 * it + par
            if lagged(it, s, 0):
                dve.wait_ge(sem["c_s_ps"], n + 1)
                nc.vector.tensor_reduce(mx[s % 2][:, :], p_s[s % 2][:, 0:P * (t + 1)], AX, ALU.max).then_inc(sem["c_max"], 1)
                dve.wait_ge(sem["c_max"], n + 1)
                wait(dve, sem["c_exp"], n - 1)
                nc.vector.tensor_scalar(nmx[s % 2][:, :], mx[s % 2][:, :], -float(DQ) ** -0.5, None, ALU.mult)\
                    .then_inc(sem["c_nmax"], 1)
            if lagged(it, s, 1):
                dve.wait_ge(sem["c_exp"], n)
                nc.vector.reciprocal(rinv[(s - 1) % 2][:, :], sm[(s - 1) % TPS][:, :]).then_inc(sem["c_rinv"], 1)
            if lagged(it, s, 2):
                u, q = (s - 2) % TPS, ((s - 2) // TPS) % 2
                bb = b if t >= 2 else b - 1
                dve.wait_ge(sem["c_o_ps"], n - 1)
                dve.wait_ge(sem["c_rinv"], n - 1)
                nc.vector.scalar_tensor_tensor(res2[q][:, u, :], p_o[:, 0:C], rinv[s % 2][:, 0:1], x2[q][:, u, :],
                                               ALU.mult, ALU.add).then_inc(sem["c_res2"], 1)
                dve.wait_ge(sem["c_res2"], n - 1)
                nc.vector.bn_stats(st[1][:, u, :], res2[q][:, u, :]).then_inc(sem["c_bn2"], 1)
            if t == 1 and lagged(it, s, 5):
                bb = b - 1
                wait_apart(dve, sem["c_bn2"], TPS * (bb + 1))
                for u in range(TPS):
                    nc.vector.bn_aggr(mv[1][:, u, :], st[1][:, u, :]).then_inc(sem["c_var2"], 1)
            if t == 3 and lagged(it, s, 7):
                bb, q = b - 1, 1 - par
                newton(1, bb, None)
                if not isinstance(it, int) or bb >= 2:
                    dve.wait_ge(sem[f"c_x3_out{q}"], 16 * (it if q == 0 else it - 1))
                    dve.wait_ge(sem[f"c_scatter_out{q}"], 128 * (it if q == 0 else it - 1))
                    dve.wait_ge(sem["c_x3T_ps"], bb - 1)
                for u in range(TPS):
                    nc.vector.tensor_scalar(x3[q][:, u, :], res2[q][:, u, :], mv[1][:, u, 0:1], ln[1][:, 4, u:u + 1],
                                            ALU.subtract, ALU.mult).then_inc(sem["c_x3"], 1)
            if t == 0 and lagged(it, s, -4):
                q = 1 - par
                dve.wait_ge(sem[f"c_x1_in{q}"], 32 * (it + 1 + par))
                dve.wait_ge(sem[f"c_moe_in{q}"], 64 * (it + 1 + par))
                for u in range(TPS):
                    nc.vector.scalar_tensor_tensor(res1[:, u, :], moe[q][:, u, :], weight[q][:, u:u + 1], x1[q][:, u, :],
                                                   ALU.mult, ALU.add).then_inc(sem["c_res1"], 1)
                dve.wait_ge(sem["c_res1"], TPS * (b + 2))
                for u in range(TPS):
                    nc.vector.bn_stats(st[0][:, u, :], res1[:, u, :]).then_inc(sem["c_bn1"], 1)
                wait_apart(dve, sem["c_bn1"], TPS * (b + 2))
                for u in range(TPS):
                    nc.vector.bn_aggr(mv[0][:, u, :], st[0][:, u, :]).then_inc(sem["c_var1"], 1)
            if t == 1 and lagged(it, s, -3):
                q = 1 - par
                newton(0, b + 1, None)
                wait(dve, sem["c_x2T_ps"], b)
                for u in range(TPS):
                    nc.vector.tensor_scalar(x2[q][:, u, :], res1[:, u, :], mv[0][:, u, 0:1], ln[0][:, 4, u:u + 1],
                                            ALU.subtract, ALU.mult).then_inc(sem["c_x2"], 1)
            if t == 3 and lagged(it, s, -1):
                dve.wait_ge(sem["c_v_ps"], b + 2)
                wait(dve, sem["c_o_ps"], TPS * b)
                nc.vector.tensor_copy(v[1 - par][:, :, :].rearrange("p t c -> p (t c)"), p_v[:, :]).then_inc(sem["c_v_sb"], 1)
            def spread(a):
                return a.rearrange("p (t a) -> p t a", a=1).to_broadcast([P, TPS, E1])

            def chain(done):
                dve.wait_ge(sem[done], b - 1)

            if t == 1 and lagged(it, s, 9):
                dve.wait_ge(sem["c_logit_ps"], b - 1)
                wait(dve, sem["c_ez"], b - 2)
                nc.vector.tensor_tensor(z[:, :, :], p_g[:, 0:TPS * E1].rearrange("p (t e) -> p t e", t=TPS), bias[:, :, :],
                                        ALU.add).then_inc(sem["c_z"], 1)
            if t == 2 and lagged(it, s, 10):
                chain("c_ez")
                nc.vector.tensor_scalar(e1p[:, :, :], ez[:, :, :], 1.0, None, ALU.add).then_inc(sem["c_e1p"], 1)
                chain("c_e1p")
                nc.vector.reciprocal(score[:, :, :], e1p[:, :, :]).then_inc(sem["c_score"], 1)
                chain("c_score")
                nc.vector.tensor_reduce(top[:, 0, :], score[:, :, :], AX, ALU.max).then_inc(sem["c_top1"], 1)
                chain("c_top1")
                nc.vector.tensor_tensor(hit[:, :, :], score[:, :, :], spread(top[:, 0, :]), ALU.is_ge).then_inc(sem["c_ge1"], 1)
                chain("c_ge1")
                nc.vector.tensor_tensor(hit2[:, :, :], hit[:, :, :], rev[:, :, :], ALU.mult).then_inc(sem["c_hit1"], 1)
                chain("c_hit1")
                nc.vector.tensor_reduce(who[:, 0, :], hit2[:, :, :], AX, ALU.max).then_inc(sem["c_who1"], 1)
                chain("c_who1")
                nc.vector.tensor_tensor(hot1[:, :, :], rev[:, :, :], spread(who[:, 0, :]), ALU.is_equal).then_inc(sem["c_hot1"], 1)
                chain("c_hot1")
                nc.vector.scalar_tensor_tensor(score2[:, :, :], hot1[:, :, :], -2.0, score[:, :, :], ALU.mult, ALU.add)                    .then_inc(sem["c_score2"], 1)
                chain("c_score2")
                nc.vector.tensor_reduce(top[:, 1, :], score2[:, :, :], AX, ALU.max).then_inc(sem["c_top2"], 1)
                chain("c_top2")
                nc.vector.tensor_tensor(hit[:, :, :], score2[:, :, :], spread(top[:, 1, :]), ALU.is_ge).then_inc(sem["c_ge2"], 1)
                chain("c_ge2")
                nc.vector.tensor_tensor(hit2[:, :, :], hit[:, :, :], rev[:, :, :], ALU.mult).then_inc(sem["c_hit2"], 1)
                chain("c_hit2")
                nc.vector.tensor_reduce(who[:, 1, :], hit2[:, :, :], AX, ALU.max).then_inc(sem["c_who2"], 1)
                chain("c_who2")
                nc.vector.tensor_tensor(hot2[:, :, :], rev[:, :, :], spread(who[:, 1, :]), ALU.is_equal).then_inc(sem["c_hot2"], 1)
                chain("c_hot2")
                wait(dve, sem["c_rank_ps"], b - 2)
                nc.vector.tensor_tensor(hot[:, :, :], hot1[:, :, :], hot2[:, :, :], ALU.add).then_inc(sem["c_hot"], 1)
            if t == 0 and lagged(it, s, 12):
                bb, q = b - 3, 1 - par

                def chain(done):
                    dve.wait_ge(sem[done], bb + 1)
                chain("c_rank_ps")
                nc.vector.tensor_tensor(at[:, :, :], p_g[:, 64:64 + TPS * E1].rearrange("p (t e) -> p t e", t=TPS),
                                        base[:, :, :], ALU.add).then_inc(sem["c_at"], 1)
                nc.vector.tensor_reduce(batch_n[:, :], hot[:, :, :].rearrange("p t e -> p e t"), AX, ALU.add)                    .then_inc(sem["c_batch_n"], 1)
                nc.vector.scalar_tensor_tensor(total[:, 0, :], top[:, 0, :], 1e-6, top[:, 1, :], ALU.add, ALU.add)                    .then_inc(sem["c_total"], 1)
                chain("c_at")
                nc.vector.tensor_tensor(at1[:, :, :], at[:, :, :], hot1[:, :, :], ALU.mult).then_inc(sem["c_at1"], 1)
                nc.vector.tensor_tensor(at2[:, :, :], at[:, :, :], hot2[:, :, :], ALU.mult).then_inc(sem["c_at2"], 1)
                chain("c_batch_n")
                nc.vector.tensor_tensor(seen[:, :], seen[:, :], batch_n[:, :], ALU.add).then_inc(sem["c_seen"], 1)
                chain("c_total")
                nc.vector.reciprocal(total[:, 1, :], total[:, 0, :]).then_inc(sem["c_rtotal"], 1)
                chain("c_at1")
                nc.vector.tensor_reduce(rowf[:, 0, :], at1[:, :, :], AX, ALU.add)
                chain("c_at2")
                nc.vector.tensor_reduce(rowf[:, 1, :], at2[:, :, :], AX, ALU.add).then_inc(sem["c_rowf"], 1)
                if not isinstance(it, int) or bb >= 2:
                    dve.wait_ge(sem[f"c_scatter_out{q}"], 128 * (it - 1 if q == 0 else it - 2))
                    dve.wait_ge(sem[f"c_meta_out{q}"], 32 * (it - 1 if q == 0 else it - 2))
                chain("c_rowf")
                nc.vector.tensor_copy(place[q][:, :, :], rowf[:, :, :]).then_inc(sem["c_place"], 1)
                chain("c_rtotal")
                for k in range(2):
                    last = nc.vector.tensor_tensor(share[q][:, k, :], top[:, k, :], total[:, 1, :], ALU.mult)
                last.then_inc(sem["c_place"], 1)
        rows_of(dve, body)


def phase_experts1(nc, dram, const, sem, ctx):
    def sb(name, shape, dt=F32):
        return ctx.enter_context(nc.sbuf_tensor("d_" + name, shape, dt))

    def ps(name):
        return ctx.enter_context(nc.psum_tensor("d_ps_" + name, [P, 512], F32))

    ident, seen = const["ident"], const["seen"]
    U, T, FC = 4, 2, F1 // P
    NB = REGION1 - 1
    ones16 = sb("ones16", [P, P], BF16)
    zeros = sb("zeros", [P, T, C])
    starts, up_to, row_number = sb("starts", [P, E1, NB]), sb("up_to", [P, E1, E1]), sb("row_number", [P, 1])
    base = sb("base", [P, E1])
    count, full, blocks = sb("count", [P, E1]), sb("full", [P, E1, NB]), sb("blocks", [P, E1])
    part, cum, before, before_n = sb("part", [P, E1, E1]), sb("cum", [P, E1]), sb("before", [P, E1]), sb("before_n", [P, E1])
    expert, first_of, local, known = (sb(n, [P, 1]) for n in ("expert", "first_of", "local", "known"))
    table = sb("table", [P, 2], U32)
    table_row = sb("table_row", [1, P, 2], U32)
    tails = sb("tails", [P, E1], U32)
    xs = [sb(f"xs{i}", [P, T, C]) for i in range(U)]
    w12 = [sb(f"w12{i}", [P, 2, F1]) for i in range(U)]
    xsT = [sb(f"xsT{i}", [P, BLK1]) for i in range(2)]
    hT = [sb(f"hT{i}", [P, FC, BLK1]) for i in range(2)]
    ys = [sb(f"ys{i}", [P, T, C]) for i in range(U)]
    p_x = [ps("x0"), ps("x1")]
    p_h = [ps(f"h{i}") for i in range(4)]
    p_y = [ps("y0"), ps("y1")]
    xs_blocks = dram["xs1"].rearrange("(k t p) c -> k p t c", p=P, t=T)
    ys_blocks = dram["ys1"].rearrange("(k t p) c -> k p t c", p=P, t=T)
    NBLOCKS = E1 * REGION1 + SPARE1
    block = ctx.enter_context(nc.Block())

    def live(it, s, lag):
        return not isinstance(it, int) or 0 <= U * it + s - lag < TILES1

    def turns(eng, body):
        for it in (-1, 0, 1):
            for s in range(U):
                body(it, s)
        with eng.Fori(2, TILES1 // U - 1) as it:
            for s in range(U):
                body(it, s)
        for s in range(U + 3):
            body(TILES1 // U - 1 + s // U, s % U)

    @block.sync
    def _(sp):
        sp.dma_start(starts[:, :, :].rearrange("p a b -> p (a b)"), dram["block_starts"]).then_inc(sem["d_const_in"], 16)
        sp.dma_start(up_to[:, :, :].rearrange("p a b -> p (a b)"), dram["up_to"]).then_inc(sem["d_const_in"], 16)
        sp.dma_start(row_number[:, :], dram["row_number"]).then_inc(sem["d_const_in"], 16)
        sp.dma_start(base[:, :], dram["region1"].rearrange("p (t e) -> p t e", e=E1)[:, 0, :], ).then_inc(sem["d_const_in"], 16)
        sp.wait_ge(sem["d_table"], 2)
        sp.dma_start(dram["tile_table"], table[:, :]).then_inc(sem["d_table_out"], 16)
        sp.wait_ge(sem["d_table_out"], 16)
        sp.dma_start(table_row[:, :, :], dram["tile_table"].rearrange("(a p) k -> a p k", a=1)).then_inc(sem["d_table_in"], 16)
        sp.wait_ge(sem["d_tails"], 1)
        for e in range(E1):
            row = sp.value_load(tails[0:1, e:e + 1], min_val=e * REGION1 * BLK1, max_val=(e + 1) * REGION1 * BLK1 - BLK1)
            sp.dma_start(dram["xs1"][bass.ds(row, BLK1), :].rearrange("(t p) c -> p t c", p=P), zeros[:, :, :])\
                .then_inc(sem["d_tails_out"], 16)
        sp.wait_ge(sem["d_tails_out"], 16 * E1)
        sp.wait_ge(sem["d_table_in"], 16)

        def body(it, s):
            n = U * it + s
            if live(it, s, -3):
                q = (s + 3) % U
                wait(sp, sem["d_y_ps"], n)
                i = n + 3
                blk = sp.value_load(table_row[0:1, bass.ds(i, 1), 0], min_val=0, max_val=NBLOCKS - 1)
                exp = sp.value_load(table_row[0:1, bass.ds(i, 1), 1], min_val=0, max_val=E1 - 1)
                sp.dma_start(xs[q][:, :, :], xs_blocks[blk]).then_inc(sem[f"d_xs_in{q}"], 16)
                sp.dma_start(w12[q][:, :, :].rearrange("p a b -> p (a b)"), dram["w12_1"][exp]).then_inc(sem[f"d_w_in{q}"], 16)
            if live(it, s, 2):
                q = (s - 2) % U
                sp.wait_ge(sem["d_ys_sb"], n - 1)
                sp.dma_start(ys_blocks[n - 2], ys[q][:, :, :]).then_inc(sem[f"d_ys_out{q}"], 16)
        turns(sp, body)
        for q in range(U):
            sp.wait_ge(sem[f"d_ys_out{q}"], 16 * TILES1 // U)

    @block.tensor
    def _(pe):
        pe.wait_ge(sem["d_ones"], 1)
        nc.tensor.matmul(p_y[0][:, 0:E1], ones16[:, :], seen[:, :], start=True, stop=True).then_inc(sem["d_count_ps"], 1)
        pe.wait_ge(sem["d_count"], 1)

        def body(it, s):
            n = U * it + s
            if live(it, s, -1):
                q = (s + 1) % U
                pe.wait_ge(sem[f"d_xs_in{q}"], 16 * (it + 1 + (s + 1) // U))
                wait(pe, sem["d_xsT_sb"], n)
                for t in range(T):
                    last = nc.tensor.transpose(p_x[(s + 1) % 2][:, P * t:P * t + P], xs[q][:, t, :], ident[:, :])
                last.then_inc(sem["d_xsT_ps"], 1)
            if live(it, s, 0):
                pe.wait_ge(sem["d_xsT_sb"], n + 1)
                pe.wait_ge(sem[f"d_w_in{s}"], 16 * (it + 1))
                for k in range(FC):
                    wait(pe, sem["d_silu"], 2 * n + k - 3)
                    nc.tensor.matmul(p_h[2 * (s % 2) + k][:, 0:BLK1], w12[s][:, 0, P * k:P * k + P], xsT[s % 2][:, :],
                                     start=True, stop=True).then_inc(sem["d_h_ps"], 1)
            if live(it, s, 1):
                q = (s - 1) % U
                pe.wait_ge(sem["d_silu"], 2 * n)
                wait(pe, sem["d_ys_sb"], n - 2)
                for t in range(T):
                    for k in range(FC):
                        last = nc.tensor.matmul(p_y[q % 2][:, P * t:P * t + P], hT[q % 2][:, k, P * t:P * t + P],
                                                w12[q][:, 1, C * k:C * k + C], start=(k == 0), stop=(k == FC - 1),
                                                skip_group_check=True)
                last.then_inc(sem["d_y_ps"], 1)
        turns(pe, body)

    @block.scalar
    def _(act):
        def body(it, s):
            n = U * it + s
            if live(it, s, 0):
                wait(act, sem["d_y_ps"], n - 1)
                for k in range(FC):
                    act.wait_ge(sem["d_h_ps"], 2 * n + k + 1)
                    nc.scalar.activation(hT[s % 2][:, k, :], p_h[2 * (s % 2) + k][:, 0:BLK1], ACT.Silu)\
                        .then_inc(sem["d_silu"], 1)
        turns(act, body)

    @block.vector
    def _(dve):
        def spread(a, n):
            return a.rearrange("p (e a) -> p e a", a=1).to_broadcast([P, E1, n])

        step = [0]

        def then(ins):
            step[0] += 1
            ins.then_inc(sem["d_plan"], 1)
            dve.wait_ge(sem["d_plan"], step[0])

        nc.vector.memset(ones16[:, :], 1.0).then_inc(sem["d_ones"], 1)
        nc.vector.memset(zeros[:, :, :], 0.0)
        dve.wait_ge(sem["d_count_ps"], 1)
        nc.vector.tensor_copy(count[:, :], p_y[0][:, 0:E1]).then_inc(sem["d_count"], 1)
        dve.wait_ge(sem["d_count"], 1)
        dve.wait_ge(sem["d_const_in"], 16 * 4)
        nc.vector.tensor_tensor(tails[:, :], count[:, :], base[:, :], ALU.add).then_inc(sem["d_tails"], 1)
        then(nc.vector.tensor_tensor(full[:, :, :], starts[:, :, :], spread(count[:, :], NB), ALU.is_lt))
        then(nc.vector.tensor_reduce(blocks[:, :], full[:, :, :], AX, ALU.add))
        then(nc.vector.tensor_tensor(part[:, :, :], up_to[:, :, :],
                                     blocks[:, :].rearrange("p (a e) -> p a e", a=1).to_broadcast([P, E1, E1]), ALU.mult))
        then(nc.vector.tensor_reduce(cum[:, :], part[:, :, :], AX, ALU.add))
        nc.vector.memset(const["shift"][:, 0:1], 0.0)
        nc.vector.tensor_scalar(const["shift"][:, 1:E1], blocks[:, 0:E1 - 1], float(BLK1), -float(REGION1 * BLK1),
                                ALU.mult, ALU.add)
        then(nc.vector.tensor_scalar(before[:, :], cum[:, :], row_number[:, 0:1], None, ALU.is_le))
        then(nc.vector.tensor_reduce(expert[:, :], before[:, :], AX, ALU.add))
        then(nc.vector.tensor_tensor(before_n[:, :], before[:, :], blocks[:, :], ALU.mult))
        then(nc.vector.tensor_reduce(first_of[:, :], before_n[:, :], AX, ALU.add))
        then(nc.vector.tensor_tensor(local[:, :], row_number[:, :], first_of[:, :], ALU.subtract))
        then(nc.vector.tensor_scalar(known[:, :], local[:, :], float(NBLOCKS - 1), None, ALU.min))
        nc.vector.tensor_scalar(table[:, 1:2], expert[:, :], float(E1 - 1), None, ALU.min).then_inc(sem["d_table"], 1)
        then(nc.vector.tensor_scalar(local[:, :], expert[:, :], float(REGION1), known[:, 0:1], ALU.mult, ALU.add))
        nc.vector.tensor_scalar(table[:, 0:1], local[:, :], float(NBLOCKS - 1), None, ALU.min).then_inc(sem["d_table"], 1)

        def body(it, s):
            n = U * it + s
            if live(it, s, -1):
                dve.wait_ge(sem["d_xsT_ps"], n + 2)
                wait(dve, sem["d_h_ps"], 2 * n)
                nc.vector.tensor_copy(xsT[(s + 1) % 2][:, :], p_x[(s + 1) % 2][:, 0:BLK1]).then_inc(sem["d_xsT_sb"], 1)
            if live(it, s, 1):
                q = (s - 1) % U
                dve.wait_ge(sem["d_y_ps"], n)
                if not isinstance(it, int) or n - 1 >= U:
                    dve.wait_ge(sem[f"d_ys_out{q}"], 16 * (it if s >= 1 else it - 1))
                nc.vector.tensor_copy(ys[q][:, :, :].rearrange("p t c -> p (t c)"), p_y[q % 2][:, 0:BLK1])\
                    .then_inc(sem["d_ys_sb"], 1)
        turns(dve, body)


def phase_combine1(nc, dram, const, sem, ctx):
    def sb(name, shape, dt=F32):
        return ctx.enter_context(nc.sbuf_tensor("e_" + name, shape, dt))

    eps = const["eps"]
    NB = 2
    x3 = [sb(f"x3{i}", [P, TPS, C]) for i in range(NB)]
    place = [sb(f"place{i}", [P, 2, TPS], U32) for i in range(NB)]
    share = [sb(f"share{i}", [P, 2, TPS]) for i in range(NB)]
    got = [sb(f"got{i}", [P, 2, TPS, C]) for i in range(NB)]
    one = sb("one", [P, TPS, C])
    base = sb("base", [P, E1])
    rowf, row2 = sb("rowf", [P, 2 * TPS]), sb("shifts", [P, 2 * TPS])
    past, moved = sb("past", [P, 2 * TPS, E1]), sb("moved", [P, 2 * TPS, E1])
    row = [sb(f"row{i}", [P, 2 * TPS], U32) for i in range(NB)]
    res = [sb(f"res{i}", [P, TPS, C]) for i in range(NB)]
    y = [sb(f"y{i}", [P, TPS, C]) for i in range(NB)]
    st = [sb(f"st{i}", [P, TPS, 6]) for i in range(NB)]
    mv = [sb(f"mv{i}", [P, TPS, 2]) for i in range(NB)]
    ln = [sb(f"ln{i}", [P, 5, TPS]) for i in range(NB)]
    x3_rows = dram["x3"].rearrange("(b t p) c -> b p t c", p=P, t=TPS)
    out_rows = dram["out"].rearrange("b (t p) c -> b p t c", p=P)
    block = ctx.enter_context(nc.Block())

    def live(it, s, lag):
        return not isinstance(it, int) or 0 <= NB * it + s - lag < NSEQ

    def turns(eng, body):
        for it in (-1, 0, 1):
            for s in range(NB):
                body(it, s)
        with eng.Fori(2, NSEQ // NB - 1) as it:
            for s in range(NB):
                body(it, s)
        for s in range(NB + 3):
            body(NSEQ // NB - 1 + s // NB, s % NB)

    @block.sync
    def _(sp):
        sp.dma_start(base[:, :], dram["region1"].rearrange("p (t e) -> p t e", e=E1)[:, 0, :]).then_inc(sem["e_base_in"], 16)

        def body(it, s):
            b = NB * it + s
            if live(it, s, -2):
                q = (s + 2) % NB
                wait(sp, sem["e_res"], TPS * (b + 3 - NB))
                sp.dma_start(place[q][:, :, :], dram["place_of"][b + 2]).then_inc(sem[f"e_place_in{q}"], 16)
                sp.dma_start(share[q][:, :, :], dram["share_of"][b + 2]).then_inc(sem[f"e_x3_in{q}"], 16)
                sp.dma_start(x3[q][:, :, :], x3_rows[b + 2]).then_inc(sem[f"e_x3_in{q}"], 16)
            if live(it, s, 2):
                q = (s - 2) % NB
                sp.wait_ge(sem["e_y"], TPS * (b - 1))
                sp.dma_start(out_rows[b - 2], y[q][:, :, :]).then_inc(sem[f"e_out{q}"], 16)
        turns(sp, body)
        for q in range(NB):
            sp.wait_ge(sem[f"e_out{q}"], 16 * NSEQ // NB)

    @block.gpsimd
    def _(pool):
        def body(it, s):
            b = NB * it + s
            if live(it, s, 0):
                pool.wait_ge(sem["e_row"], b + 1)
                wait_apart(pool, sem["e_res"], TPS * (b - NB + 1))
                for k in range(2):
                    for u in range(TPS):
                        pool.indirect_dma_start(got[s][:, k, u, :], None, dram["ys1"],
                                                bass.IndirectOffsetOnAxis(row[s][:, TPS * k + u:TPS * k + u + 1], 0))\
                            .then_inc(sem[f"e_got_in{s}"], 16)
        turns(pool, body)

    @block.scalar
    def _(act):
        nc.scalar.preload_act_table_set("natural_log_exp_and_others")

        def body(it, s):
            b = NB * it + s
            if live(it, s, 1):
                q = (s - 1) % NB
                act.wait_ge(sem["e_var"], TPS * b)
                nc.scalar.activation(ln[q][:, 0, :], mv[q][:, :, 1], ACT.Ln, bias=eps[:, 0:1]).then_inc(sem["e_ln"], 1)
                act.wait_ge(sem["e_ln"], b)
                nc.scalar.activation(ln[q][:, 1, :], ln[q][:, 0, :], ACT.Exp, scale=-0.5).then_inc(sem["e_guess"], 1)
        turns(act, body)

    @block.vector
    def _(dve):
        dve.wait_ge(sem["e_base_in"], 16)

        def body(it, s):
            b = NB * it + s
            if live(it, s, -1):
                q, c = (s + 1) % NB, b + 1
                dve.wait_ge(sem[f"e_place_in{q}"], 16 * (it + 1 + (s + 1) // NB))
                wait(dve, sem["e_row"], c)
                nc.vector.tensor_copy(rowf[:, :], place[q][:, :, :].rearrange("p k t -> p (k t)")).then_inc(sem["e_rowf"], 1)
                dve.wait_ge(sem["e_rowf"], c + 1)
                nc.vector.tensor_tensor(past[:, :, :],
                                        rowf[:, :].rearrange("p (n a) -> p n a", a=1).to_broadcast([P, 2 * TPS, E1]),
                                        base[:, :].rearrange("p (a e) -> p a e", a=1).to_broadcast([P, 2 * TPS, E1]),
                                        ALU.is_ge).then_inc(sem["e_past"], 1)
                dve.wait_ge(sem["e_past"], c + 1)
                nc.vector.tensor_tensor(moved[:, :, :], past[:, :, :],
                                        const["shift"][:, :].rearrange("p (a e) -> p a e", a=1)
                                        .to_broadcast([P, 2 * TPS, E1]), ALU.mult).then_inc(sem["e_moved"], 1)
                dve.wait_ge(sem["e_moved"], c + 1)
                nc.vector.tensor_reduce(row2[:, :], moved[:, :, :], AX, ALU.add).then_inc(sem["e_row2"], 1)
                dve.wait_ge(sem["e_row2"], c + 1)
                nc.vector.tensor_tensor(row[q][:, :], rowf[:, :], row2[:, :], ALU.add).then_inc(sem["e_row"], 1)
            if live(it, s, 0):
                dve.wait_ge(sem[f"e_x3_in{s}"], 32 * (it + 1))
                dve.wait_ge(sem[f"e_got_in{s}"], 16 * 2 * TPS * (it + 1))
                for u in range(TPS):
                    nc.vector.scalar_tensor_tensor(one[:, u, :], got[s][:, 0, u, :], share[s][:, 0, u:u + 1], x3[s][:, u, :],
                                                   ALU.mult, ALU.add).then_inc(sem["e_one"], 1)
                for u in range(TPS):
                    dve.wait_ge(sem["e_one"], TPS * b + u + 1)
                    nc.vector.scalar_tensor_tensor(res[s][:, u, :], got[s][:, 1, u, :], share[s][:, 1, u:u + 1], one[:, u, :],
                                                   ALU.mult, ALU.add).then_inc(sem["e_res"], 1)
                for u in range(TPS):
                    dve.wait_ge(sem["e_res"], TPS * b + u + 1)
                    nc.vector.bn_stats(st[s][:, u, :], res[s][:, u, :]).then_inc(sem["e_bn"], 1)
                for u in range(TPS):
                    wait_apart(dve, sem["e_bn"], TPS * b + u + 1)
                    nc.vector.bn_aggr(mv[s][:, u, :], st[s][:, u, :]).then_inc(sem["e_var"], 1)
            if live(it, s, 1):
                q, c = (s - 1) % NB, b - 1
                var, guess, u1, w, rstd = mv[q][:, :, 1], ln[q][:, 1, :], ln[q][:, 2, :], ln[q][:, 3, :], ln[q][:, 4, :]
                done = sem["e_newton"]
                dve.wait_ge(sem["e_guess"], b)
                nc.vector.scalar_tensor_tensor(u1, var, EPS, guess, ALU.add, ALU.mult).then_inc(done, 1)
                dve.wait_ge(done, 4 * c + 1)
                nc.vector.tensor_tensor(w, u1, guess, ALU.mult).then_inc(done, 1)
                dve.wait_ge(done, 4 * c + 2)
                nc.vector.tensor_scalar(u1, w, -0.5, 1.5, ALU.mult, ALU.add).then_inc(done, 1)
                dve.wait_ge(done, 4 * c + 3)
                nc.vector.tensor_tensor(rstd, u1, guess, ALU.mult).then_inc(done, 1)
                dve.wait_ge(done, 4 * c + 4)
                if not isinstance(it, int) or c >= NB:
                    dve.wait_ge(sem[f"e_out{q}"], 16 * (it if s >= 1 else it - 1))
                for u in range(TPS):
                    nc.vector.tensor_scalar(y[q][:, u, :], res[q][:, u, :], mv[q][:, u, 0:1], ln[q][:, 4, u:u + 1],
                                            ALU.subtract, ALU.mult).then_inc(sem["e_y"], 1)
        turns(dve, body)


PHASES = (phase_attention0, phase_experts0, phase_attention1, phase_experts1, phase_combine1)


class Semaphores(dict):

    def __init__(self, nc):
        self.nc = nc

    def __missing__(self, name):
        self[name] = self.nc.alloc_semaphore(name=name)
        return self[name]


def build(nc, dram, phases=PHASES):
    assert TILES1 >= 2 * NT * P // BLK1 + E1 - 1
    with ExitStack() as ctx:
        const = {"eps": ctx.enter_context(nc.sbuf_tensor("eps", [P, 1], F32)),
                 "ident": ctx.enter_context(nc.sbuf_tensor("ident", [P, P], F32)),
                 "seen": ctx.enter_context(nc.sbuf_tensor("seen", [P, E1], BF16)),
                 "shift": ctx.enter_context(nc.sbuf_tensor("shift", [P, E1], F32))}
        for phase in phases:
            sem = Semaphores(nc)
            with ExitStack() as of_phase:
                phase(nc, dram, const, sem, of_phase)
            nc.clear_and_free_semaphores(list(sem.values()))
            nc.all_engine_barrier()


SCRATCH = {"x1": ((NT * P, C), F32), "slots": ((SLOTS, C), F32), "yslots": ((SLOTS + 1, C), F32),
           "slot_of": ((NSEQ, P, TPS), U32), "weight_of": ((NSEQ, P, TPS), F32), "x3": ((NT * P, C), F32),
           "xs1": (((E1 * REGION1 + SPARE1) * BLK1, C), F32), "ys1": ((TILES1 * BLK1, C), F32),
           "place_of": ((NSEQ, P, 2 * TPS), U32), "share_of": ((NSEQ, P, 2 * TPS), F32),
           "tile_table": ((P, 2), U32)}


def laid_out(i):
    import numpy as np
    c = np.ascontiguousarray
    w = {k: np.asarray(v) for k, v in i.items()}
    x = w["L0_attn_x"]
    wqkv = w["L0_attn_w_qkv"]
    wv = wqkv[2 * C:].reshape(4, 2, D0, C)
    i_q, k = np.arange(P)[:, None] % QB, np.arange(WIN)[None, :]
    band = (k > i_q) & (k < i_q + 2 * BAND)
    masks = [band, band & (k >= BAND), band & (k < WIN - BAND)]
    tok = np.arange(P)
    return {
        "x": c(x), "xT": c(x.transpose(0, 2, 1)),
        "wqkvT": c(wqkv[:2 * C].T), "wv_by_parity": c(wv.transpose(3, 1, 0, 2).reshape(C, C)),
        "wprojT": c(w["L0_attn_w_proj"].T), "bqkv": c(w["L0_attn_b_qkv"].reshape(3, C).T),
        "bproj": c(np.broadcast_to(w["L0_attn_b_proj"], (P, C))),
        "gate0T": c(w["L0_ffn_gate_w"].T),
        "w1_0": c(w["L0_ffn_w1"]), "w2_0": c(w["L0_ffn_w2"]),
        "wqk1": c(np.concatenate([w["L1_attn_Wq"], w["L1_attn_Wk"]], 1)), "wv1": c(w["L1_attn_Wv"]),
        "gate1T": c(w["L1_ffn_gate_w"].T),
        "balance": c(np.broadcast_to(np.tile(w["L1_ffn_balance_bias"], TPS), (P, TPS * E1))),
        "w12_1": c(np.concatenate([w["L1_ffn_w1"].transpose(0, 2, 1),
                                   w["L1_ffn_w2"].reshape(E1, C, F1 // P, P).transpose(0, 3, 2, 1).reshape(E1, P, F1)], 2)),
        "band_mask": c(np.concatenate([np.where(m, 0, -1e30) for m in masks], 1).astype(np.float32)),
        "causal": np.where(tok[None, :] <= tok[:, None], 0, -1e30).astype(np.float32),
        "before": (tok[:, None] < tok[None, :]).astype(np.float32),
        "ident": np.eye(P, dtype=np.float32),
        "rev1": c(np.broadcast_to(np.tile(E1 - np.arange(E1), TPS), (P, TPS * E1)).astype(np.float32)),
        "region1": c(np.broadcast_to(np.tile(np.arange(E1) * REGION1 * BLK1, TPS), (P, TPS * E1)).astype(np.float32)),
        "block_starts": c(np.broadcast_to(np.tile(np.arange(REGION1 - 1) * BLK1, E1), (P, E1 * (REGION1 - 1))).astype(np.float32)),
        "up_to": c(np.broadcast_to(np.tri(E1).reshape(-1), (P, E1 * E1)).astype(np.float32)),
        "row_number": c(tok[:, None].astype(np.float32)),
        "rev": c(np.broadcast_to(np.tile(E0 - np.arange(E0), TPS), (P, TPS * E0)).astype(np.float32)),
    }


def kernel(**inputs):
    import numpy as np
    import concourse.bacc as bacc
    from concourse.bass_utils import run_bass_kernel_spmd

    arrays = laid_out(inputs)
    nc = bacc.Bacc("TRN2", target_bir_lowering=False, num_devices=1)
    dram = {n: nc.dram_tensor("in_" + n, a.shape, mybir.dt.from_np(a.dtype), kind="ExternalInput").ap()
            for n, a in arrays.items()}
    for n, (shape, dt) in SCRATCH.items():
        dram[n] = nc.dram_tensor("scratch_" + n, shape, dt, kind="Internal").ap()
    dram["out"] = nc.dram_tensor("out_0", (NSEQ, SEQ, C), F32, kind="ExternalOutput").ap()
    build(nc, dram)
    r = run_bass_kernel_spmd(nc, [{"in_" + n: a for n, a in arrays.items()}], core_ids=[0])
    return np.asarray(r.results[0]["out_0"])
```

```python
from contextlib import ExitStack

import concourse.bass as bass
from concourse import mybir

F32 = mybir.dt.float32
BF16 = mybir.dt.bfloat16
U32 = mybir.dt.uint32
ALU = mybir.AluOpType
ACT = mybir.ActivationFunctionType
AX = mybir.AxisListType.X

P = 128
SEQ = 512
NSEQ = 16
TPS = SEQ // P
NT = NSEQ * TPS
C = 128
EPS = 1e-5

H0, D0, BAND = 8, 16, 16
QB = 32
WIN = QB + 2 * BAND
NBLK = P // QB
PAD = BAND
SEQP = SEQ + 2 * PAD

E0, F0 = 16, 512
CAP = 640
SLOTS = E0 * CAP
NCAP = CAP // P
ROW0 = C + 1

DQ = 64
E1, F1 = 8, 256

BLK1 = 2 * P
REGION1 = NT * P // BLK1 + 1
SPARE1 = E1
ROW1 = C + 2
TILES1 = 72

UNROLL = 2 * TPS


def wait(eng, sem, n):
    if not (isinstance(n, int) and n <= 0):
        eng.wait_ge(sem, n)


def wait_apart(eng, sem, n):
    if not isinstance(n, int):
        n = eng.to_reg(n)
        eng.wait_ge(sem, 1)
        eng.wait_ge(sem, n)
    elif n > 0:
        eng.wait_ge(sem, n)


def lagged(it, s, lag, total=NT):
    return not isinstance(it, int) or 0 <= UNROLL * it + s - lag < total


def steps(eng, body, peel, lag):
    for it in range(peel):
        for s in range(UNROLL):
            body(it, s)
    with eng.Fori(peel, NT // UNROLL - 1) as it:
        for s in range(UNROLL):
            body(it, s)
    for s in range(UNROLL + lag + 1):
        body(NT // UNROLL - 1 + s // UNROLL, s % UNROLL)


def phase_attention0(nc, dram, const, sem, ctx):
    def sb(name, shape, dt=F32):
        return ctx.enter_context(nc.sbuf_tensor("a_" + name, shape, dt))

    def ps(name, shape=(P, 512)):
        return ctx.enter_context(nc.psum_tensor("a_ps_" + name, list(shape), F32))

    wq, wk, wv, wp = (sb(n, [P, C]) for n in ("wq", "wk", "wv", "wp"))
    bqkv = sb("bqkv", [P, 3])
    bproj = sb("bproj", [P, C])
    gate_w = sb("gate_w", [P, E0])
    maskf = sb("maskf", [P, 3 * WIN])
    mask = sb("mask", [P, 3, WIN], BF16)
    ident16 = sb("ident16", [P, P], BF16)
    ones16 = sb("ones16", [P, P], BF16)
    tri_f = sb("tri_f", [P, P])
    tri16 = sb("tri16", [P, P], BF16)
    rev = sb("rev", [P, TPS, E0])
    zeros = sb("zeros", [P, 10 * ROW0])
    token_of = sb("token_of", [P, 2, TPS])

    x = [sb(f"x{i}", [P, TPS, C]) for i in range(2)]
    xT = [sb(f"xT{i}", [P, SEQP]) for i in range(2)]
    kT = sb("kT", [P, SEQ])
    kexp = [sb(f"kexp{i}", [P, H0, SEQP]) for i in range(2)]
    qT = [sb(f"qT{i}", [P, SEQ]) for i in range(2)]
    vexp = [sb(f"vexp{i}", [P, NBLK, 4, 32]) for i in range(TPS)]
    prob = [sb(f"prob{i}", [P, H0, WIN]) for i in range(TPS)]
    probT = [sb(f"probT{i}", [P, 4, P]) for i in range(2)]
    attT = [sb(f"attT{i}", [P, P]) for i in range(2)]
    mx = [sb(f"mx{i}", [P, H0]) for i in range(2)]
    sm = [sb(f"sm{i}", [P, H0]) for i in range(2)]
    rinv = [sb(f"rinv{i}", [P, H0]) for i in range(TPS)]
    res = [sb(f"res{i}", [P, TPS, C]) for i in range(2)]
    y = [sb(f"y{i}", [P, TPS, ROW0]) for i in range(2)]
    yT = sb("yT", [P, SEQ])
    st = [sb(f"st{i}", [P, TPS, 6]) for i in range(2)]
    ln = [sb(f"ln{i}", [P, 6, TPS]) for i in range(2)]
    mv = [sb(f"mv{i}", [P, TPS, 2]) for i in range(2)]
    lmax = sb("lmax", [P, TPS])
    lsub = sb("lsub", [P, TPS, E0])
    lexp = sb("lexp", [P, TPS, E0])
    first = sb("first", [P, TPS, E0])
    rmx = sb("rmx", [P, TPS])
    onehot = sb("onehot", [P, TPS, E0], BF16)
    ranked = sb("ranked", [P, TPS, E0])
    seen = sb("seen", [P, E0], BF16)
    batch_n = sb("batch_n", [P, E0])
    g = sb("g", [P, 6, TPS])
    gweight = [sb(f"gweight{i}", [P, TPS]) for i in range(2)]
    slot = [sb(f"slot{i}", [P, TPS], U32) for i in range(2)]

    p_q, p_k, p_v, p_pt, p_ap, p_g = (ps(n) for n in ("q", "k", "v", "pt", "ap", "g"))
    p_s = [ps(f"s{i}") for i in range(2)]
    p_av, p_pj = p_ap[:, 0:P], p_ap[:, P:P + C]
    eps, ident = const["eps"], const["ident"]

    block = ctx.enter_context(nc.Block())
    x_rows = dram["x"].rearrange("b (t p) c -> b p t c", p=P)
    x1_rows = dram["x1"].rearrange("(b t p) c -> b p t c", p=P, t=TPS)

    @block.sync
    def _(sp):
        def load_xT(b, par):
            sp.dma_start(xT[par][:, PAD:PAD + SEQ], dram["xT"][b]).then_inc(sem[f"a_xT_in{par}"], 16)

        def spread_keys(par):
            for h in range(H0):
                rows = slice(D0 * h, D0 * h + D0)
                sp.dma_start(kexp[par][rows, h, PAD:PAD + SEQ], kT[rows, :]).then_inc(sem[f"a_kexp_in{par}"], 16)

        for dst, src in ((wq, dram["wqkvT"][:, 0:C]), (wk, dram["wqkvT"][:, C:2 * C]),
                         (wv, dram["wv_by_parity"]), (wp, dram["wprojT"]), (bqkv, dram["bqkv"]),
                         (maskf, dram["band_mask"]), (tri_f, dram["before"]), (gate_w, dram["gate0T"])):
            sp.dma_start(dst[:, :], src).then_inc(sem["a_const_in"], 16)
        sp.dma_start(ident[:, :], dram["ident"]).then_inc(sem["a_const_in"], 16)
        sp.dma_start(rev[:, :, :], dram["rev"].rearrange("p (t e) -> p t e", e=E0)).then_inc(sem["a_const_in"], 16)
        sp.dma_start(bproj[:, :], dram["bproj"]).then_inc(sem["a_const_in"], 16)
        sp.dma_start(token_of[:, :, :], dram["token_of"].rearrange("p (q t) -> p q t", q=2)).then_inc(sem["a_const_in"], 16)
        sp.wait_ge(sem["a_zero"], 1)
        moe_flat = dram["moe"].rearrange("(n p r) c -> n p (r c)", p=P, r=8)
        slots_flat = dram["slots"].rearrange("(n p r) c -> n p (r c)", p=P, r=10)
        load_xT(0, 0)
        sp.dma_start(x[0][:, :, :], x_rows[0]).then_inc(sem["a_x_in0"], 16)
        for n in range(SLOTS // (P * 10)):
            sp.dma_start(slots_flat[n], zeros[:, :]).then_inc(sem["slots_zeroed"], 16)
        for n in range(NT // 8):
            sp.dma_start(moe_flat[n], zeros[:, 0:8 * C]).then_inc(sem["slots_zeroed"], 16)

        sp.wait_ge(sem["a_k_sb"], 1)
        spread_keys(0)

        def body(it, s):
            t, par = s % TPS, (s // TPS) % 2
            b = 2 * it + par
            if t == 0 and lagged(it, s, -4):
                wait(sp, sem["a_v_ps"], TPS * b)
                load_xT(b + 1, 1 - par)
            if t == 1 and lagged(it, s, -3):
                wait(sp, sem["a_k_sb"], b + 2)
                wait(sp, sem["a_s_ps"], TPS * b)
                spread_keys(1 - par)
            if t == 3 and lagged(it, s, -1):
                wait(sp, sem["a_res"], TPS * b)
                sp.dma_start(x[1 - par][:, :, :], x_rows[b + 1]).then_inc(sem[f"a_x_in{1 - par}"], 16)
            if t == 2 and lagged(it, s, 10):
                q = par
                bb = b - 2
                sp.wait_ge(sem["a_y"], TPS * (bb + 1))
                sp.dma_start(x1_rows[bb], y[q][:, :, 0:C]).then_inc(sem[f"a_y_out{q}"], 16)
            if t == 1 and lagged(it, s, 13):
                q = 1 - par
                bb = b - 3
                sp.wait_ge(sem["a_slot"], bb + 1)
                sp.dma_start(dram["slot_of"][bb], slot[q][:, :]).then_inc(sem[f"a_meta_out{q}"], 16)
                sp.dma_start(dram["weight_of"][bb], gweight[q][:, :]).then_inc(sem[f"a_meta_out{q}"], 16)
        steps(sp, body, 3, 15)
        for q in range(2):
            sp.wait_ge(sem[f"a_y_out{q}"], 16 * NSEQ // 2)
            sp.wait_ge(sem[f"a_meta_out{q}"], 32 * NSEQ // 2)

    @block.tensor
    def _(pe):
        def project(out, w, par, done):
            nc.tensor.matmul(out[:, :], w[:, :], xT[par][:, PAD:PAD + SEQ], start=True, stop=True).then_inc(done, 1)

        pe.wait_ge(sem["a_const_in"], 16 * 12)
        pe.wait_ge(sem["a_setup"], 1)
        pe.wait_ge(sem["a_xT_in0"], 16)
        project(p_k, wk, 0, sem["a_k_ps"])
        project(p_q, wq, 0, sem["a_q_ps"])

        def body(it, s):
            t, par = s % TPS, (s // TPS) % 2
            n = UNROLL * it + s
            b = 2 * it + par
            if lagged(it, s, 0):
                wait(pe, sem["a_v_sb"], n)
                for j in range(NBLK):
                    for odd in range(2):
                        last = nc.tensor.matmul(p_v[64 * odd:64 * odd + 64, 64 * j:64 * j + 64],
                                                xT[par][:, P * t + QB * j:P * t + QB * j + WIN],
                                                wv[:, 64 * odd:64 * odd + 64], start=True, stop=True, skip_group_check=True)
                last.then_inc(sem["a_v_ps"], 1)
            if t == 1 and lagged(it, s, -3):
                pe.wait_ge(sem["a_k_sb"], b + 1)
                pe.wait_ge(sem[f"a_xT_in{1 - par}"], 16 * (it + 1 + par))
                project(p_k, wk, 1 - par, sem["a_k_ps"])
            if t == 2 and lagged(it, s, -2):
                pe.wait_ge(sem["a_q_sb"], b + 1)
                project(p_q, wq, 1 - par, sem["a_q_ps"])
            if lagged(it, s, 0):
                if t == 0:
                    pe.wait_ge(sem["a_q_sb"], b + 1)
                    pe.wait_ge(sem[f"a_kexp_in{par}"], 16 * H0 * (it + 1))
                wait(pe, sem["a_sub"], n - 1)
                out = p_s[s % 2]
                edge = 1 if t == 0 else 2 if t == TPS - 1 else 0
                for j in range(NBLK):
                    m = edge if (t == 0 and j == 0) or (t == TPS - 1 and j == NBLK - 1) else 0
                    q = slice(QB * j, QB * j + QB)
                    nc.tensor.matmul(out[q, :], ident16[:, q], mask[:, m:m + 1, :].to_broadcast([P, H0, WIN]),
                                     start=True, stop=False, skip_group_check=True)
                for j in range(NBLK):
                    q = slice(QB * j, QB * j + QB)
                    last = nc.tensor.matmul(out[q, :], qT[par][:, P * t + QB * j:P * t + QB * j + QB],
                                            kexp[par][:, :, P * t + QB * j:P * t + QB * j + WIN], start=False, stop=True,
                                            skip_group_check=True)
                last.then_inc(sem["a_s_ps"], 1)
            if lagged(it, s, 3):
                pe.wait_ge(sem["a_pt_sb"], n - 2)
                pe.wait_ge(sem["a_v_sb"], n - 2)
                wait(pe, sem["a_res"], n - 3)
                for j in range(NBLK):
                    for hp in range(4):
                        last = nc.tensor.matmul(p_av[32 * hp:32 * hp + 32, QB * j:QB * j + QB],
                                                vexp[(s - 3) % TPS][:, j, hp, :],
                                                probT[(s - 3) % 2][:, hp, QB * j:QB * j + QB], start=True, stop=True,
                                                skip_group_check=True)
                last.then_inc(sem["a_av_ps"], 1)
            if lagged(it, s, 2):
                pe.wait_ge(sem["a_norm"], n - 1)
                wait(pe, sem["a_pt_sb"], n - 2)
                for hp in range(4):
                    last = nc.tensor.transpose(p_pt[:, hp * P:hp * P + P], prob[(s - 2) % TPS][:, 2 * hp:2 * hp + 2, :]
                                               .rearrange("p a b -> p (a b)"),
                                               ident[:, :])
                last.then_inc(sem["a_pt_ps"], 1)
            if t == 2 and lagged(it, s, 10):
                bb = b - 2
                pe.wait_ge(sem["a_y"], TPS * (bb + 1))
                wait(pe, sem["a_slot"], bb)
                for u in range(TPS):
                    last = nc.tensor.transpose(p_g[:, P * u:P * u + P], y[par][:, u, 0:C], ident[:, :])
                last.then_inc(sem["a_yT_ps"], 1)
            if t == 3 and lagged(it, s, 11):
                bb = b - 2
                pe.wait_ge(sem["a_yT_sb"], bb + 1)
                for u in range(TPS):
                    last = nc.tensor.matmul(p_g[:, E0 * u:E0 * u + E0], yT[:, P * u:P * u + P], gate_w[:, :],
                                            start=(u == 0), stop=(u == TPS - 1), skip_group_check=True)
                last.then_inc(sem["a_logit_ps"], 1)
            if t == 0 and lagged(it, s, 12):
                bb = b - 3
                pe.wait_ge(sem["a_onehot"], bb + 1)
                out = p_g[:, 64:128]
                nc.tensor.matmul(out, ones16[:, :], seen[:, :].rearrange("p (a e) -> p a e", a=1).to_broadcast([P, TPS, E0]),
                                 start=True, stop=False, skip_group_check=True)
                nc.tensor.matmul(out, tri16[:, :], onehot[:, :, :], start=False, stop=False, skip_group_check=True)
                for u in range(TPS - 1):
                    last = nc.tensor.matmul(out[:, E0 * (u + 1):64], ones16[:, :],
                                            onehot[:, u:u + 1, :].to_broadcast([P, TPS - 1 - u, E0]),
                                            start=False, stop=(u == TPS - 2), skip_group_check=True)
                last.then_inc(sem["a_rank_ps"], 1)
            if lagged(it, s, 3):
                pe.wait_ge(sem["a_att_sb"], n - 2)
                nc.tensor.matmul(p_pj, attT[(s - 3) % 2][:, :], wp[:, :], start=True, stop=True)\
                    .then_inc(sem["a_pj_ps"], 1)
        steps(pe, body, 3, 15)

    @block.scalar
    def _(act):
        nc.scalar.preload_act_table_set("natural_log_exp_and_others")

        def k_out(value, par_of_old, old):
            act.wait_ge(sem["a_k_ps"], value)
            if old is not None:
                act.wait_ge(sem[f"a_kexp_in{par_of_old}"], old)
            nc.scalar.activation(kT[:, :], p_k[:, :], ACT.Identity, bias=bqkv[:, 1:2]).then_inc(sem["a_k_sb"], 1)

        def q_out(value, par, used):
            act.wait_ge(sem["a_q_ps"], value)
            wait(act, sem["a_s_ps"], used)
            nc.scalar.activation(qT[par][:, :], p_q[:, :], ACT.Identity, bias=bqkv[:, 0:1]).then_inc(sem["a_q_sb"], 1)

        act.wait_ge(sem["a_const_in"], 16 * 12)
        k_out(1, 0, None)
        q_out(1, 0, 0)

        def body(it, s):
            t, par = s % TPS, (s // TPS) % 2
            n = UNROLL * it + s
            b = 2 * it + par
            if lagged(it, s, 0):
                act.wait_ge(sem["a_v_ps"], n + 1)
                wait(act, sem["a_av_ps"], n - 3)
                for odd in range(2):
                    rows = slice(64 * odd, 64 * odd + 64)
                    nc.scalar.copy(vexp[t][rows, :, :, 16 * odd:16 * odd + 16],
                                   p_v[rows, 0:256].rearrange("p (j h d) -> p j h d", j=NBLK, h=4))\
                        .then_inc(sem["a_v_half"] if odd == 0 else sem["a_v_sb"], 1)
            if lagged(it, s, 3):
                act.wait_ge(sem["a_av_ps"], n - 2)
                wait(act, sem["a_pj_ps"], n - 4)
                nc.scalar.activation(attT[(s - 3) % 2][:, :], p_av, ACT.Identity, bias=bqkv[:, 2:3])\
                    .then_inc(sem["a_att_sb"], 1)
            if t == 1 and lagged(it, s, -3):
                k_out(b + 2, par, 16 * H0 * (it + 1))
            if t == 2 and lagged(it, s, -2):
                q_out(b + 2, 1 - par, TPS * b)
            if lagged(it, s, 2):
                act.wait_ge(sem["a_pt_ps"], n - 1)
                wait(act, sem["a_av_ps"], n - 3)
                nc.scalar.copy(probT[(s - 2) % 2][:, :, :].rearrange("p a b -> p (a b)"), p_pt[:, :]).then_inc(sem["a_pt_sb"], 1)
            if t == 3 and lagged(it, s, 7):
                q = (s // TPS + 1) % 2
                bb = b - 1
                act.wait_ge(sem["a_var"], TPS * (bb + 1))
                nc.scalar.activation(ln[q][:, 0, :], mv[q][:, :, 1], ACT.Ln, bias=eps[:, 0:1]).then_inc(sem["a_ln"], 1)
                act.wait_ge(sem["a_ln"], bb + 1)
                nc.scalar.activation(ln[q][:, 1, :], ln[q][:, 0, :], ACT.Exp, scale=-0.5).then_inc(sem["a_guess"], 1)
            for due in range(2):
                if t == due and lagged(it, s, 8 + due):
                    q, bb = par, b - 2
                    if due == 0:
                        act.wait_ge(sem["a_shift"], bb + 1)
                        if not isinstance(it, int) or bb >= 2:
                            act.wait_ge(sem[f"a_scatter_out{q}"], 64 * (it - 1))
                            act.wait_ge(sem[f"a_y_out{q}"], 16 * (it - 1))
                            act.wait_ge(sem["a_yT_ps"], bb - 1)
                    for u in (2 * due, 2 * due + 1):
                        nc.scalar.activation(y[q][:, u, 0:C], res[q][:, u, :], ACT.Identity, bias=ln[q][:, 4, u:u + 1],
                                             scale=ln[q][:, 5, u:u + 1]).then_inc(sem["a_y"], 1)
            if lagged(it, s, 0):
                act.wait_ge(sem["a_sub"], n + 1)
                e = prob[t][:, :, :].rearrange("p a b -> p (a b)")
                nc.scalar.activation(e, e, ACT.Exp, scale=float(C) ** -0.5).then_inc(sem["a_exp"], 1)
            if t == 2 and lagged(it, s, 10):
                bb = b - 2
                act.wait_ge(sem["a_yT_ps"], bb + 1)
                wait(act, sem["a_logit_ps"], bb)
                nc.scalar.copy(yT[:, :], p_g[:, :]).then_inc(sem["a_yT_sb"], 1)
            if t == 3 and lagged(it, s, 11):
                bb = b - 2
                act.wait_ge(sem["a_lsub"], bb + 1)
                wait(act, sem["a_slot"], bb)
                nc.scalar.activation(lexp[:, :, :], lsub[:, :, :], ACT.Exp).then_inc(sem["a_gate_exp"], 1)
        steps(act, body, 3, 15)

    @block.vector
    def _(dve):
        nc.vector.memset(zeros[:, :], 0.0).then_inc(sem["a_zero"], 1)
        nc.vector.memset(eps[:, :], EPS)
        nc.vector.memset(ones16[:, :], 1.0)
        nc.vector.memset(seen[:, :], 0.0)
        for q in range(2):
            nc.vector.memset(kexp[q][:, :, :], 0.0)
            nc.vector.memset(xT[q][:, 0:PAD], 0.0)
            nc.vector.memset(xT[q][:, PAD + SEQ:SEQP], 0.0)
        for t in range(TPS):
            nc.vector.memset(vexp[t][:, :, :, :], 0.0)
        dve.wait_ge(sem["a_const_in"], 16 * 12)
        nc.vector.tensor_copy(mask[:, :, :].rearrange("p a b -> p (a b)"), maskf[:, :])
        nc.vector.tensor_copy(tri16[:, :], tri_f[:, :])
        for q in range(2):
            nc.vector.tensor_scalar(y[q][:, :, C], token_of[:, q, :], -float(NT * P), None, ALU.add)
        nc.vector.tensor_copy(ident16[:, :], ident[:, :]).then_inc(sem["a_setup"], 1)

        def body(it, s):
            t, par = s % TPS, (s // TPS) % 2
            n = UNROLL * it + s
            b = 2 * it + par
            if lagged(it, s, 0):
                dve.wait_ge(sem["a_s_ps"], n + 1)
                scores = p_s[s % 2][:, :].rearrange("p (h k) -> p h k", h=H0)
                nc.vector.tensor_reduce(mx[s % 2][:, :], scores, AX, ALU.max).then_inc(sem["a_max"], 1)
            if lagged(it, s, 0):
                wait(dve, sem["a_pt_ps"], n - 3)
                dve.wait_ge(sem["a_max"], n + 1)
                nc.vector.tensor_tensor(prob[t][:, :, :], scores,
                                        mx[s % 2][:, :].rearrange("p (h a) -> p h a", a=1).to_broadcast([P, H0, WIN]),
                                        ALU.subtract).then_inc(sem["a_sub"], 1)
            if lagged(it, s, 3):
                u, q = (s - 3) % TPS, ((s - 3) // TPS) % 2
                bb = b if t == 3 else b - 1
                dve.wait_ge(sem["a_pj_ps"], n - 2)
                dve.wait_ge(sem["a_xb"], bb + 1)
                wait(dve, sem["a_y"], TPS * (bb - 1))
                nc.vector.tensor_tensor(res[q][:, u, :], x[q][:, u, :], p_pj, ALU.add).then_inc(sem["a_res"], 1)
            if t == 3 and lagged(it, s, 11):
                bb = b - 2
                dve.wait_ge(sem["a_logit_ps"], bb + 1)
                logits = p_g[:, 0:64].rearrange("p (t e) -> p t e", t=TPS)
                nc.vector.tensor_reduce(lmax[:, :], logits, AX, ALU.max).then_inc(sem["a_lmax"], 1)
                dve.wait_ge(sem["a_lmax"], bb + 1)
                wait(dve, sem["a_gate_exp"], bb)
                nc.vector.tensor_tensor(lsub[:, :, :], logits,
                                        lmax[:, :].rearrange("p (t a) -> p t a", a=1).to_broadcast([P, TPS, E0]),
                                        ALU.subtract).then_inc(sem["a_lsub"], 1)
                dve.wait_ge(sem["a_lsub"], bb + 1)
                nc.vector.scalar_tensor_tensor(first[:, :, :], lsub[:, :, :], 0.0, rev[:, :, :], ALU.is_ge, ALU.mult)\
                    .then_inc(sem["a_first"], 1)
                dve.wait_ge(sem["a_first"], bb + 1)
                nc.vector.tensor_reduce(rmx[:, :], first[:, :, :], AX, ALU.max).then_inc(sem["a_rmx"], 1)
                dve.wait_ge(sem["a_rmx"], bb + 1)
                nc.vector.tensor_tensor(onehot[:, :, :], rev[:, :, :],
                                        rmx[:, :].rearrange("p (t a) -> p t a", a=1).to_broadcast([P, TPS, E0]),
                                        ALU.is_equal).then_inc(sem["a_onehot"], 1)
            if t == 0 and lagged(it, s, 12):
                bb, q = b - 3, 1 - par
                valid, rank, off, inside, total, gprob = (g[:, i, :] for i in range(6))
                dve.wait_ge(sem["a_rank_ps"], bb + 1)
                nc.vector.tensor_tensor(ranked[:, :, :], p_g[:, 64:128].rearrange("p (t e) -> p t e", t=TPS),
                                        onehot[:, :, :], ALU.mult).then_inc(sem["a_ranked"], 1)
                nc.vector.tensor_reduce(batch_n[:, :], onehot[:, :, :].rearrange("p t e -> p e t"), AX, ALU.add)\
                    .then_inc(sem["a_batch_n"], 1)
                dve.wait_ge(sem["a_gate_exp"], bb + 1)
                nc.vector.tensor_reduce(total, lexp[:, :, :], AX, ALU.add).then_inc(sem["a_total"], 1)
                dve.wait_ge(sem["a_ranked"], bb + 1)
                nc.vector.tensor_reduce(rank, ranked[:, :, :], AX, ALU.add).then_inc(sem["a_rank"], 1)
                dve.wait_ge(sem["a_batch_n"], bb + 1)
                nc.vector.tensor_tensor(seen[:, :], seen[:, :], batch_n[:, :], ALU.add)
                dve.wait_ge(sem["a_total"], bb + 1)
                nc.vector.reciprocal(gprob, total).then_inc(sem["a_gprob"], 1)
                dve.wait_ge(sem["a_rank"], bb + 1)
                nc.vector.tensor_scalar(valid, rank, float(CAP), None, ALU.is_lt).then_inc(sem["a_valid"], 1)
                nc.vector.scalar_tensor_tensor(off, rmx[:, :], -float(CAP), rank, ALU.mult, ALU.add)\
                    .then_inc(sem["a_valid"], 1)
                dve.wait_ge(sem["a_valid"], 2 * (bb + 1))
                nc.vector.tensor_tensor(inside, off, valid, ALU.mult).then_inc(sem["a_inside"], 1)
                if not isinstance(it, int) or bb >= 2:
                    dve.wait_ge(sem[f"a_scatter_out{q}"], 64 * (it - 1 if q == 0 else it - 2))
                    dve.wait_ge(sem[f"a_meta_out{q}"], 32 * (it - 1 if q == 0 else it - 2))
                    nc.vector.tensor_scalar(y[q][:, :, C], y[q][:, :, C], float(2 * SEQ), None, ALU.add)
                dve.wait_ge(sem["a_gprob"], bb + 1)
                nc.vector.tensor_tensor(gweight[q][:, :], gprob, valid, ALU.mult)
                dve.wait_ge(sem["a_inside"], bb + 1)
                nc.vector.tensor_scalar(slot[q][:, :], inside, float(SLOTS), None, ALU.add).then_inc(sem["a_slot"], 1)
            if lagged(it, s, 0):
                dve.wait_ge(sem["a_exp"], n + 1)
                nc.vector.tensor_reduce(sm[s % 2][:, :], prob[t][:, :, :], AX, ALU.add).then_inc(sem["a_sum"], 1)
            if lagged(it, s, 3):
                u, q = (s - 3) % TPS, ((s - 3) // TPS) % 2
                dve.wait_ge(sem["a_res"], n - 2)
                nc.vector.bn_stats(st[q][:, u, :], res[q][:, u, :]).then_inc(sem["a_bn"], 1)
            if lagged(it, s, 3):
                u, q = (s - 3) % TPS, ((s - 3) // TPS) % 2
                wait_apart(dve, sem["a_bn"], n - 2)
                nc.vector.bn_aggr(mv[q][:, u, :], st[q][:, u, :]).then_inc(sem["a_var"], 1)
            if lagged(it, s, 0):
                wait(dve, sem["a_norm"], n - 3)
                dve.wait_ge(sem["a_sum"], n + 1)
                nc.vector.reciprocal(rinv[t][:, :], sm[s % 2][:, :]).then_inc(sem["a_rinv"], 1)
            if t == 3 and lagged(it, s, 7):
                q, bb = 1 - par, b - 1
                var, guess, half, square, rstd = mv[q][:, :, 1], ln[q][:, 1, :], ln[q][:, 2, :], ln[q][:, 3, :], ln[q][:, 5, :]
                shift = ln[q][:, 4, :]
                dve.wait_ge(sem["a_guess"], bb + 1)
                nc.vector.scalar_tensor_tensor(half, var, EPS, guess, ALU.add, ALU.mult).then_inc(sem["a_newton"], 1)
                dve.wait_ge(sem["a_newton"], 3 * bb + 1)
                nc.vector.tensor_tensor(square, half, guess, ALU.mult).then_inc(sem["a_newton"], 1)
                dve.wait_ge(sem["a_newton"], 3 * bb + 2)
                nc.vector.tensor_scalar(half, square, -0.5, 1.5, ALU.mult, ALU.add).then_inc(sem["a_newton"], 1)
                dve.wait_ge(sem["a_newton"], 3 * bb + 3)
                nc.vector.tensor_tensor(rstd, half, guess, ALU.mult).then_inc(sem["a_rstd"], 1)
                dve.wait_ge(sem["a_rstd"], bb + 1)
                nc.vector.scalar_tensor_tensor(shift, mv[q][:, :, 0], -1.0, rstd, ALU.mult, ALU.mult)\
                    .then_inc(sem["a_shift"], 1)
        steps(dve, body, 3, 15)

    @block.gpsimd
    def _(pool):
        pool.wait_ge(sem["a_const_in"], 16 * 12)

        def body(it, s):
            t, par = s % TPS, (s // TPS) % 2
            n = UNROLL * it + s
            b = 2 * it + par
            if lagged(it, s, 0):
                pool.wait_ge(sem["a_rinv"], n + 1)
                e = prob[t][:, :, :]
                nc.gpsimd.tensor_tensor(e, e, rinv[t][:, :].rearrange("p (h a) -> p h a", a=1)
                                        .to_broadcast([P, H0, WIN]), ALU.mult).then_inc(sem["a_norm"], 1)
            if t == 0 and lagged(it, s, 0):
                pool.wait_ge(sem[f"a_x_in{par}"], 16 * (it + 1))
                nc.gpsimd.tensor_tensor(x[par][:, :, :], x[par][:, :, :],
                                        bproj[:, :].rearrange("p (a c) -> p a c", a=1).to_broadcast([P, TPS, C]),
                                        ALU.add).then_inc(sem["a_xb"], 1)
            for due, which in ((1, (0, 1)), (2, (2, 3))):
                if t == due and lagged(it, s, 12 + due):
                    bb, q = b - 3, 1 - par
                    if due == 1:
                        pool.wait_ge(sem["a_slot"], bb + 1)
                        wait_apart(pool, sem["a_y"], TPS * (bb + 1))
                        if isinstance(it, int) and bb == 0:
                            pool.wait_ge(sem["slots_zeroed"], 16 * (SLOTS // (P * 10) + NT // 8))
                    for u in which:
                        pool.indirect_dma_start(dram["slots"], bass.IndirectOffsetOnAxis(slot[q][:, u:u + 1], 0),
                                                y[q][:, u, :], None, bounds_check=SLOTS - 1, oob_is_err=False)\
                            .then_inc(sem[f"a_scatter_out{q}"], 16)
        steps(pool, body, 3, 15)
        for q in range(2):
            pool.wait_ge(sem[f"a_scatter_out{q}"], 64 * NSEQ // 2)


def phase_experts0(nc, dram, const, sem, ctx):
    def sb(name, shape, dt=F32):
        return ctx.enter_context(nc.sbuf_tensor("b_" + name, shape, dt))

    def ps(name):
        return ctx.enter_context(nc.psum_tensor("b_ps_" + name, [P, 512], F32))

    FC = F0 // P
    HALF = CAP // 2
    ident = const["ident"]
    xs = [sb(f"xs{i}", [P, NCAP, ROW0]) for i in range(2)]
    w1 = [sb(f"w1{i}", [P, F0]) for i in range(2)]
    w2 = [sb(f"w2{i}", [P, FC, C]) for i in range(2)]
    xsT = [sb(f"xsT{i}", [P, CAP]) for i in range(2)]
    hT = [sb(f"hT{i}", [P, FC, CAP]) for i in range(2)]
    ys = [sb(f"ys{i}", [P, NCAP, C]) for i in range(2)]
    token = [sb(f"token{i}", [P, NCAP], U32) for i in range(2)]
    p_x = [ps("x0"), ps("x1")]
    p_h = [ps(f"h{i}") for i in range(4)]
    p_y = [ps("y0"), ps("y1")]
    slots = dram["slots"].rearrange("(e t p) c -> e p t c", p=P, t=NCAP)
    w2_rows = dram["w2_0"].rearrange("e (k p) c -> e p k c", p=P)
    units = [(k, half) for k in range(FC) for half in range(2)]
    NU = len(units)
    block = ctx.enter_context(nc.Block())

    def turns(eng, body):
        for par in range(2):
            body(0, par, par == 0, False)
        with eng.Fori(1, E0 // 2 - 1) as it:
            for par in range(2):
                body(it, par, False, False)
        for par in range(2):
            body(E0 // 2 - 1, par, False, par == 1)

    @block.sync
    def _(sp):
        def load(e, par):
            sp.dma_start(xs[par][:, :, :], slots[e]).then_inc(sem[f"b_xs_in{par}"], 16)
            sp.dma_start(w1[par][:, :], dram["w1_0"][e]).then_inc(sem[f"b_w1_in{par}"], 16)
            sp.dma_start(w2[par][:, :, :], w2_rows[e]).then_inc(sem[f"b_w2_in{par}"], 16)

        load(0, 0)

        def body(it, par, first, last):
            e = 2 * it + par
            if not last:
                wait(sp, sem["b_y_ps"], e)
                wait(sp, sem["b_token"], e)
                load(e + 1, 1 - par)
        turns(sp, body)

    @block.gpsimd
    def _(pool):
        def body(it, par, first, last):
            e = 2 * it + par
            pool.wait_ge(sem["b_token"], e + 1)
            wait_apart(pool, sem["b_ys_sb"], 2 * e + 2)
            for t in range(NCAP):
                pool.indirect_dma_start(dram["moe"], bass.IndirectOffsetOnAxis(token[par][:, t:t + 1], 0),
                                        ys[par][:, t, :], None, bounds_check=NT * P - 1, oob_is_err=False)\
                    .then_inc(sem[f"b_ys_out{par}"], 16)
        turns(pool, body)
        for par in range(2):
            pool.wait_ge(sem[f"b_ys_out{par}"], 16 * NCAP * E0 // 2)

    @block.tensor
    def _(pe):
        def turn_rows(e, par, rounds):
            pe.wait_ge(sem[f"b_xs_in{par}"], 16 * rounds)
            wait(pe, sem["b_xsT_sb"], 2 * e)
            for t in range(NCAP):
                last = nc.tensor.transpose(p_x[t // 4][:, P * (t % 4):P * (t % 4) + P], xs[par][:, t, 0:C], ident[:, :])
                if t in (3, NCAP - 1):
                    last.then_inc(sem["b_xsT_ps"], 1)

        turn_rows(0, 0, 1)

        def body(it, par, first, last):
            e = 2 * it + par
            pe.wait_ge(sem["b_xsT_sb"], 2 * e + 2)
            pe.wait_ge(sem[f"b_w1_in{par}"], 16 * (it + 1))
            for u, (k, half) in enumerate(units):
                wait(pe, sem["b_gelu"], NU * e + u - 3)
                nc.tensor.matmul(p_h[u % 4][:, 0:HALF], w1[par][:, P * k:P * k + P],
                                 xsT[par][:, HALF * half:HALF * half + HALF], start=True, stop=True)\
                    .then_inc(sem["b_h_ps"], 1)
            if not last:
                turn_rows(e + 1, 1 - par, it + 1 + par)
            pe.wait_ge(sem[f"b_w2_in{par}"], 16 * (it + 1))
            pe.wait_ge(sem["b_gelu"], NU * (e + 1))
            wait(pe, sem["b_ys_sb"], 2 * e)
            for t in range(NCAP):
                for k in range(FC):
                    m = nc.tensor.matmul(p_y[t // 4][:, P * (t % 4):P * (t % 4) + P], hT[par][:, k, P * t:P * t + P],
                                         w2[par][:, k, :], start=(k == 0), stop=(k == FC - 1), skip_group_check=True)
            m.then_inc(sem["b_y_ps"], 1)
        turns(pe, body)

    @block.scalar
    def _(act):
        def body(it, par, first, last):
            e = 2 * it + par
            wait(act, sem["b_y_ps"], e - 1)
            for u, (k, half) in enumerate(units):
                act.wait_ge(sem["b_h_ps"], NU * e + u + 1)
                nc.scalar.activation(hT[par][:, k, HALF * half:HALF * half + HALF], p_h[u % 4][:, 0:HALF],
                                     ACT.Gelu_apprx_tanh).then_inc(sem["b_gelu"], 1)
        turns(act, body)

    @block.vector
    def _(dve):
        def xsT_out(e, par):
            wait(dve, sem["b_h_ps"], NU * (e - 1))
            dve.wait_ge(sem["b_xsT_ps"], 2 * e + 1)
            nc.vector.tensor_copy(xsT[par][:, 0:512], p_x[0][:, :]).then_inc(sem["b_xsT_sb"], 1)
            dve.wait_ge(sem["b_xsT_ps"], 2 * e + 2)
            nc.vector.tensor_copy(xsT[par][:, 512:CAP], p_x[1][:, 0:CAP - 512]).then_inc(sem["b_xsT_sb"], 1)

        xsT_out(0, 0)

        def body(it, par, first, last):
            e = 2 * it + par
            if not last:
                xsT_out(e + 1, 1 - par)
            wait(dve, sem[f"b_ys_out{par}"], 16 * NCAP * it)
            dve.wait_ge(sem[f"b_xs_in{par}"], 16 * (it + 1))
            nc.vector.tensor_scalar(token[par][:, :], xs[par][:, :, C], float(NT * P), None, ALU.add)\
                .then_inc(sem["b_token"], 1)
            dve.wait_ge(sem["b_y_ps"], e + 1)
            nc.vector.tensor_copy(ys[par][:, 0:4, :].rearrange("p t c -> p (t c)"), p_y[0][:, :]).then_inc(sem["b_ys_sb"], 1)
            nc.vector.tensor_copy(ys[par][:, 4, :], p_y[1][:, 0:C]).then_inc(sem["b_ys_sb"], 1)
        turns(dve, body)


def phase_attention1(nc, dram, const, sem, ctx):
    def sb(name, shape, dt=F32):
        return ctx.enter_context(nc.sbuf_tensor("c_" + name, shape, dt))

    def ps(name):
        return ctx.enter_context(nc.psum_tensor("c_ps_" + name, [P, 512], F32))

    ident, eps = const["ident"], const["eps"]
    wqk, wv = sb("wqk", [P, C]), sb("wv", [P, C])
    causal_f, causal16, ident16 = sb("causal_f", [P, P]), sb("causal16", [P, P], BF16), sb("ident16", [P, P], BF16)
    x1 = [sb(f"x1{i}", [P, TPS, C]) for i in range(2)]
    weight = [sb(f"weight{i}", [P, TPS]) for i in range(2)]
    moe = [sb(f"moe{i}", [P, TPS, C]) for i in range(2)]
    res1 = sb("res1", [P, TPS, C])
    x2 = [sb(f"x2{i}", [P, TPS, C]) for i in range(2)]
    x2T = sb("x2T", [P, SEQ])
    qT = [sb(f"qT{i}", [DQ, SEQ]) for i in range(2)]
    kT = [sb(f"kT{i}", [DQ, SEQ]) for i in range(2)]
    v = [sb(f"v{i}", [P, TPS, C]) for i in range(2)]
    prob = [sb(f"prob{i}", [P, SEQ]) for i in range(TPS)]
    probT = [sb(f"probT{i}", [P, TPS, P]) for i in range(2)]
    nmx = [sb(f"nmx{i}", [P, 1]) for i in range(2)]
    sm = [sb(f"sm{i}", [P, 1]) for i in range(TPS)]
    rinv = [sb(f"rinv{i}", [P, 1]) for i in range(2)]
    res2 = [sb(f"res2{i}", [P, TPS, C]) for i in range(2)]
    x3 = [sb(f"x3{i}", [P, TPS, ROW1]) for i in range(2)]
    st = [sb(f"st{i}", [P, TPS, 6]) for i in range(2)]
    mv = [sb(f"mv{i}", [P, TPS, 2]) for i in range(2)]
    ln = [sb(f"ln{i}", [P, 6, TPS]) for i in range(2)]
    p_x, p_qk, p_v, p_o = (ps(n) for n in ("x", "qk", "v", "o"))
    p_s = [ps(f"s{i}") for i in range(2)]
    p_pt, p_g = ps("pt"), ps("g")
    gate_w, bias = sb("gate_w", [P, E1]), sb("bias", [P, TPS, E1])
    rev, base = sb("rev", [P, TPS, E1]), sb("base", [P, TPS, E1])
    tri_f, tri16, ones16 = sb("tri_f", [P, P]), sb("tri16", [P, P], BF16), sb("ones16", [P, P], BF16)
    zeros = sb("zeros", [P, 2 * ROW1])
    x3T = sb("x3T", [P, SEQ])
    z, ez, e1p, score, hit, score2, hit2, at, at1, at2 = (sb(f"gate{i}", [P, TPS, E1]) for i in range(10))
    hot1, hot2, hot = (sb(n, [P, TPS, E1], BF16) for n in ("hot1", "hot2", "hot"))
    seen, batch_n = const["seen"], sb("batch_n", [P, E1])
    token_of = sb("token_of", [P, 2, TPS])
    top = sb("top", [P, 2, TPS])
    who = sb("who", [P, 2, TPS])
    total = sb("total", [P, 2, TPS])
    place = [sb(f"place{i}", [P, 2, TPS], U32) for i in range(2)]
    share = [sb(f"share{i}", [P, 2, TPS]) for i in range(2)]
    x1_rows = dram["x1"].rearrange("(b t p) c -> b p t c", p=P, t=TPS)
    moe_rows = dram["moe"].rearrange("(b t p) c -> b p t c", p=P, t=TPS)
    x3_rows = dram["x3"].rearrange("(b t p) c -> b p t c", p=P, t=TPS)
    block = ctx.enter_context(nc.Block())

    def rows_of(eng, body):
        for it in (-1, 0, 1, 2):
            for s in range(UNROLL):
                body(it, s)
        with eng.Fori(3, NT // UNROLL - 1) as it:
            for s in range(UNROLL):
                body(it, s)
        for s in range(UNROLL + 13):
            body(NT // UNROLL - 1 + s // UNROLL, s % UNROLL)

    @block.sync
    def _(sp):
        for dst, src in ((wqk, dram["wqk1"]), (wv, dram["wv1"]), (causal_f, dram["causal"])):
            sp.dma_start(dst[:, :], src).then_inc(sem["c_const_in"], 16)
        sp.dma_start(gate_w[:, :], dram["gate1T"]).then_inc(sem["c_const_in"], 16)
        sp.dma_start(tri_f[:, :], dram["before"]).then_inc(sem["c_const_in"], 16)
        for dst, src in ((bias, dram["balance"]), (rev, dram["rev1"]), (base, dram["region1"])):
            sp.dma_start(dst[:, :, :].rearrange("p t e -> p (t e)"), src).then_inc(sem["c_const_in"], 16)
        sp.dma_start(token_of[:, :, :], dram["token_of"].rearrange("p (q t) -> p q t", q=2)).then_inc(sem["c_const_in"], 16)
        sp.wait_ge(sem["c_zero"], 1)
        spare = dram["xs1"].rearrange("(k t p) c -> k p t c", p=P, t=2)
        for k in range(SPARE1):
            sp.dma_start(spare[E1 * REGION1 + k], zeros[:, :].rearrange("p (t c) -> p t c", t=2)).then_inc(sem["c_spare"], 16)

        def body(it, s):
            t, par = s % TPS, (s // TPS) % 2
            b = 2 * it + par
            if t == 0 and lagged(it, s, 8):
                bb, q = b - 2, par
                sp.wait_ge(sem["c_x3"], TPS * (bb + 1))
                sp.dma_start(x3_rows[bb], x3[q][:, :, 0:C]).then_inc(sem[f"c_x3_out{q}"], 16)
            if t == 0 and lagged(it, s, 12):
                bb, q = b - 3, 1 - par
                sp.wait_ge(sem["c_place"], bb + 1)
                sp.dma_start(dram["share_of"][bb], share[q][:, :, :]).then_inc(sem[f"c_meta_out{q}"], 16)
            if t == 0 and lagged(it, s, -8):
                wait(sp, sem["c_res1"], TPS * (b + 1))
                sp.dma_start(weight[par][:, :], dram["weight_of"][b + 2]).then_inc(sem[f"c_x1_in{par}"], 16)
                sp.dma_start(x1[par][:, :, :], x1_rows[b + 2]).then_inc(sem[f"c_x1_in{par}"], 16)
                sp.dma_start(moe[par][:, :, :], moe_rows[b + 2]).then_inc(sem[f"c_x1_in{par}"], 16)
        rows_of(sp, body)
        for q in range(2):
            sp.wait_ge(sem[f"c_x3_out{q}"], 16 * NSEQ // 2)
            sp.wait_ge(sem[f"c_meta_out{q}"], 16 * NSEQ // 2)
        sp.wait_ge(sem["c_spare"], 16 * SPARE1)

    @block.gpsimd
    def _(pool):
        def body(it, s):
            t, par = s % TPS, (s // TPS) % 2
            b = 2 * it + par
            if t == 0 and lagged(it, s, 12):
                bb, q = b - 3, 1 - par
                wait_apart(pool, sem["c_place"], bb + 1)
                for k in range(2):
                    for u in range(TPS):
                        pool.indirect_dma_start(dram["xs1"], bass.IndirectOffsetOnAxis(place[q][:, k, u:u + 1], 0),
                                                x3[q][:, u, :], None).then_inc(sem[f"c_scatter_out{q}"], 16)
        rows_of(pool, body)
        for q in range(2):
            pool.wait_ge(sem[f"c_scatter_out{q}"], 128 * NSEQ // 2)

    @block.tensor
    def _(pe):
        pe.wait_ge(sem["c_const_in"], 16 * 9)
        pe.wait_ge(sem["c_setup"], 5)

        def body(it, s):
            t, par = s % TPS, (s // TPS) % 2
            n = UNROLL * it + s
            b = 2 * it + par
            if lagged(it, s, 2):
                u = (s - 2) % TPS
                pe.wait_ge(sem["c_exp"], n - 1)
                wait(pe, sem["c_pt_sb"], n - 2)
                for c in range(u + 1):
                    last = nc.tensor.transpose(p_pt[:, P * c:P * c + P], prob[u][:, P * c:P * c + P], ident[:, :])
                last.then_inc(sem["c_pt_ps"], 1)
            def times_values(when):
                if lagged(it, s, 2) and t in when:
                    u, q = (s - 2) % TPS, ((s - 2) // TPS) % 2
                    pe.wait_ge(sem["c_pt_sb"], n - 1)
                    pe.wait_ge(sem["c_v_sb"], (b if t >= 2 else b - 1) + 1)
                    wait(pe, sem["c_res2"], n - 2)
                    for c in range(u + 1):
                        last = nc.tensor.matmul(p_o[:, 0:C], probT[s % 2][:, c, :], v[q][:, c, :],
                                                start=(c == 0), stop=(c == u))
                    last.then_inc(sem["c_o_ps"], 1)

            times_values((0,))
            if lagged(it, s, 0):
                if t == 0:
                    pe.wait_ge(sem["c_k_sb"], b + 1)
                wait(pe, sem["c_exp"], n - 1)
                nc.tensor.matmul(p_s[s % 2][:, 0:P * (t + 1)], qT[par][:, P * t:P * t + P], kT[par][:, 0:P * (t + 1)],
                                 start=True, stop=False, skip_group_check=True)
                nc.tensor.matmul(p_s[s % 2][:, P * t:P * t + P], ident16[:, :], causal16[:, :], start=False, stop=True,
                                 skip_group_check=True).then_inc(sem["c_s_ps"], 1)
            if t == 1 and lagged(it, s, 9):
                bb = b - 2
                pe.wait_ge(sem["c_x3T_sb"], bb + 1)
                for u in range(TPS):
                    last = nc.tensor.matmul(p_g[:, E1 * u:E1 * u + E1], x3T[:, P * u:P * u + P], gate_w[:, :],
                                            start=(u == 0), stop=(u == TPS - 1), skip_group_check=True)
                last.then_inc(sem["c_logit_ps"], 1)
            times_values((1, 2, 3))
            if t == 3 and lagged(it, s, 11):
                bb = b - 2
                pe.wait_ge(sem["c_hot"], bb + 1)
                out = p_g[:, 64:64 + TPS * E1]
                nc.tensor.matmul(out, ones16[:, :], seen[:, :].rearrange("p (a e) -> p a e", a=1).to_broadcast([P, TPS, E1]),
                                 start=True, stop=False, skip_group_check=True)
                nc.tensor.matmul(out, tri16[:, :], hot[:, :, :], start=False, stop=False, skip_group_check=True)
                for u in range(TPS - 1):
                    last = nc.tensor.matmul(out[:, E1 * (u + 1):TPS * E1], ones16[:, :],
                                            hot[:, u:u + 1, :].to_broadcast([P, TPS - 1 - u, E1]),
                                            start=False, stop=(u == TPS - 2), skip_group_check=True)
                last.then_inc(sem["c_rank_ps"], 1)
            if t == 0 and lagged(it, s, 8):
                bb, q = b - 2, par
                pe.wait_ge(sem["c_x3"], TPS * (bb + 1))
                wait(pe, sem["c_at"], bb)
                for u in range(TPS):
                    last = nc.tensor.transpose(p_g[:, P * u:P * u + P], x3[q][:, u, 0:C], ident[:, :])
                last.then_inc(sem["c_x3T_ps"], 1)
            if t == 2 and lagged(it, s, -2):
                pe.wait_ge(sem["c_x2"], TPS * (b + 2))
                wait(pe, sem["c_x2T_sb"], b + 1)
                for u in range(TPS):
                    last = nc.tensor.transpose(p_x[:, P * u:P * u + P], x2[1 - par][:, u, :], ident[:, :])
                last.then_inc(sem["c_x2T_ps"], 1)
            if t == 3 and lagged(it, s, -1):
                pe.wait_ge(sem["c_x2T_sb"], b + 2)
                wait(pe, sem["c_k_sb"], b + 1)
                nc.tensor.matmul(p_qk[:, :], wqk[:, :], x2T[:, :], start=True, stop=True).then_inc(sem["c_qk_ps"], 1)
                wait(pe, sem["c_v_sb"], b + 1)
                for u in range(TPS):
                    last = nc.tensor.matmul(p_v[:, P * u:P * u + P], x2T[:, P * u:P * u + P], wv[:, :],
                                            start=True, stop=True, skip_group_check=True)
                last.then_inc(sem["c_v_ps"], 1)
        rows_of(pe, body)

    @block.scalar
    def _(act):
        nc.scalar.preload_act_table_set("natural_log_exp_and_others")

        def guess(k, count):
            act.wait_ge(sem[f"c_var{k + 1}"], TPS * count)
            nc.scalar.activation(ln[k][:, 0, :], mv[k][:, :, 1], ACT.Ln, bias=eps[:, 0:1]).then_inc(sem[f"c_ln{k + 1}"], 1)
            act.wait_ge(sem[f"c_ln{k + 1}"], count)
            nc.scalar.activation(ln[k][:, 1, :], ln[k][:, 0, :], ACT.Exp, scale=-0.5).then_inc(sem[f"c_guess{k + 1}"], 1)

        def body(it, s):
            t, par = s % TPS, (s // TPS) % 2
            n = UNROLL * it + s
            b = 2 * it + par
            if lagged(it, s, 2):
                u = (s - 2) % TPS
                act.wait_ge(sem["c_pt_ps"], n - 1)
                wait(act, sem["c_o_ps"], n - 3)
                nc.scalar.copy(probT[s % 2][:, 0:u + 1, :].rearrange("p a b -> p (a b)"), p_pt[:, 0:P * (u + 1)])\
                    .then_inc(sem["c_pt_sb"], 1)
            if t == 2 and lagged(it, s, 6):
                guess(1, b)
            if t == 1 and lagged(it, s, -3):
                guess(0, b + 2)
            if t == 0 and lagged(it, s, 0):
                act.wait_ge(sem["c_qk_ps"], b + 1)
                wait(act, sem["c_s_ps"], TPS * (b - 1))
                nc.scalar.activation(qT[par][:, :], p_qk[0:DQ, :], ACT.Identity, scale=float(DQ) ** -0.5)\
                    .then_inc(sem["c_q_sb"], 1)
                nc.scalar.copy(kT[par][:, :], p_qk[DQ:P, :]).then_inc(sem["c_k_sb"], 1)
            if t == 2 and lagged(it, s, -2):
                for u in (2, 3):
                    nc.scalar.activation(x2[1 - par][:, u, :], res1[:, u, :], ACT.Identity, bias=ln[0][:, 5, u:u + 1],
                                         scale=ln[0][:, 4, u:u + 1]).then_inc(sem["c_x2"], 1)
            if lagged(it, s, 0):
                act.wait_ge(sem["c_nmax"], n + 1)
                wait(act, sem["c_pt_ps"], n - 3)
                wait(act, sem["c_rinv"], n - 3)
                nc.scalar.activation(prob[t][:, 0:P * (t + 1)], p_s[s % 2][:, 0:P * (t + 1)], ACT.Exp,
                                     bias=nmx[s % 2][:, 0:1], accum_out=sm[t][:, 0:1]).then_inc(sem["c_exp"], 1)
            if t == 1 and lagged(it, s, 9):
                bb = b - 2
                act.wait_ge(sem["c_z"], bb + 1)
                wait(act, sem["c_e1p"], bb)
                nc.scalar.activation(ez[:, :, :], z[:, :, :], ACT.Exp, scale=-1.0).then_inc(sem["c_ez"], 1)
            if t == 1 and lagged(it, s, -3):
                act.wait_ge(sem["c_shift1"], b + 2)
                wait(act, sem["c_x2T_ps"], b)
                wait(act, sem["c_res2"], TPS * b)
                for u in (0, 1):
                    nc.scalar.activation(x2[1 - par][:, u, :], res1[:, u, :], ACT.Identity, bias=ln[0][:, 5, u:u + 1],
                                         scale=ln[0][:, 4, u:u + 1]).then_inc(sem["c_x2"], 1)
            if t == 3 and lagged(it, s, 7):
                bb, q = b - 1, 1 - par
                act.wait_ge(sem["c_shift2"], bb + 1)
                if not isinstance(it, int) or bb >= 2:
                    act.wait_ge(sem[f"c_x3_out{q}"], 16 * (it if q == 0 else it - 1))
                    act.wait_ge(sem[f"c_scatter_out{q}"], 128 * (it if q == 0 else it - 1))
                    act.wait_ge(sem["c_x3T_ps"], bb - 1)
                for u in range(TPS):
                    nc.scalar.activation(x3[q][:, u, 0:C], res2[q][:, u, :], ACT.Identity, bias=ln[1][:, 5, u:u + 1],
                                         scale=ln[1][:, 4, u:u + 1]).then_inc(sem["c_x3"], 1)
            if t == 0 and lagged(it, s, 8):
                bb = b - 2
                act.wait_ge(sem["c_x3T_ps"], bb + 1)
                wait(act, sem["c_logit_ps"], bb)
                nc.scalar.copy(x3T[:, :], p_g[:, :]).then_inc(sem["c_x3T_sb"], 1)
            if t == 0 and lagged(it, s, 0):
                act.wait_ge(sem["c_v_ps"], b + 1)
                wait(act, sem["c_o_ps"], TPS * (b - 1))
                nc.scalar.copy(v[par][:, :, :].rearrange("p t c -> p (t c)"), p_v[:, :]).then_inc(sem["c_v_sb"], 1)
            if t == 2 and lagged(it, s, -2):
                act.wait_ge(sem["c_x2T_ps"], b + 2)
                wait(act, sem["c_v_ps"], b + 1)
                nc.scalar.copy(x2T[:, :], p_x[:, :]).then_inc(sem["c_x2T_sb"], 1)
        rows_of(act, body)

    @block.vector
    def _(dve):
        dve.wait_ge(sem["c_const_in"], 16 * 9)
        nc.vector.memset(zeros[:, :], 0.0).then_inc(sem["c_zero"], 1)
        nc.vector.memset(seen[:, :], 0.0)
        nc.vector.memset(ones16[:, :], 1.0).then_inc(sem["c_setup"], 1)
        nc.vector.tensor_copy(tri16[:, :], tri_f[:, :]).then_inc(sem["c_setup"], 1)
        nc.vector.tensor_copy(causal16[:, :], causal_f[:, :]).then_inc(sem["c_setup"], 1)
        nc.vector.tensor_copy(ident16[:, :], ident[:, :]).then_inc(sem["c_setup"], 1)
        for q in range(2):
            last = nc.vector.tensor_scalar(x3[q][:, :, C], token_of[:, q, :], -2.0 * NT * P, None, ALU.add)
        last.then_inc(sem["c_setup"], 1)

        def newton(k, count, i):
            mean, var = mv[k][:, :, 0], mv[k][:, :, 1]
            _, first, half, square, rstd, shift = (ln[k][:, r, :] for r in range(6))
            done = sem[f"c_newton{k + 1}"]
            if i == 0:
                dve.wait_ge(sem[f"c_guess{k + 1}"], count + 1)
                nc.vector.scalar_tensor_tensor(half, var, EPS, first, ALU.add, ALU.mult).then_inc(done, 1)
            if i == 1:
                dve.wait_ge(done, 4 * count + 1)
                nc.vector.tensor_tensor(square, half, first, ALU.mult).then_inc(done, 1)
            if i == 2:
                dve.wait_ge(done, 4 * count + 2)
                nc.vector.tensor_scalar(half, square, -0.5, 1.5, ALU.mult, ALU.add).then_inc(done, 1)
            if i == 3:
                dve.wait_ge(done, 4 * count + 3)
                nc.vector.tensor_tensor(rstd, half, first, ALU.mult).then_inc(done, 1)
            if i == 4:
                dve.wait_ge(done, 4 * count + 4)
                nc.vector.scalar_tensor_tensor(shift, mean, -1.0, rstd, ALU.mult, ALU.mult)\
                    .then_inc(sem[f"c_shift{k + 1}"], 1)

        def spread(a):
            return a.rearrange("p (t a) -> p t a", a=1).to_broadcast([P, TPS, E1])

        def body(it, s):
            t, par = s % TPS, (s // TPS) % 2
            n = UNROLL * it + s
            b = 2 * it + par
            ln1 = t == 1 and lagged(it, s, -3)
            ln2 = t == 2 and lagged(it, s, 6)
            gate1, gate2, gate3 = (t == k and lagged(it, s, 8 + k) for k in (1, 2, 3))

            def between(i):
                if ln1:
                    newton(0, b + 1, i)
                if ln2:
                    newton(1, b - 1, i)

            if lagged(it, s, 1):
                dve.wait_ge(sem["c_exp"], n)
                nc.vector.reciprocal(rinv[(s - 1) % 2][:, :], sm[(s - 1) % TPS][:, :]).then_inc(sem["c_rinv"], 1)
            between(0)
            if gate1:
                dve.wait_ge(sem["c_logit_ps"], b - 1)
                wait(dve, sem["c_ez"], b - 2)
                nc.vector.tensor_tensor(z[:, :, :], p_g[:, 0:TPS * E1].rearrange("p (t e) -> p t e", t=TPS), bias[:, :, :],
                                        ALU.add).then_inc(sem["c_z"], 1)
            if gate2:
                dve.wait_ge(sem["c_hot1"], b - 1)
                nc.vector.scalar_tensor_tensor(score2[:, :, :], hot1[:, :, :], -2.0, score[:, :, :], ALU.mult, ALU.add)\
                    .then_inc(sem["c_score2"], 1)
            if t == 0 and lagged(it, s, -4):
                q = 1 - par
                dve.wait_ge(sem[f"c_x1_in{q}"], 48 * (it + 1 + par))
                wait(dve, sem["c_x2"], TPS * (b + 1))
                for u in range(TPS):
                    nc.vector.scalar_tensor_tensor(res1[:, u, :], moe[q][:, u, :], weight[q][:, u:u + 1], x1[q][:, u, :],
                                                   ALU.mult, ALU.add).then_inc(sem["c_res1"], 1)
            between(1)
            if gate2:
                dve.wait_ge(sem["c_score2"], b - 1)
                nc.vector.tensor_reduce(top[:, 1, :], score2[:, :, :], AX, ALU.max).then_inc(sem["c_top2"], 1)
            between(2)
            between(3)
            if lagged(it, s, 0):
                dve.wait_ge(sem["c_s_ps"], n + 1)
                wait(dve, sem["c_exp"], n - 1)
                nc.vector.tensor_reduce(nmx[s % 2][:, :], p_s[s % 2][:, 0:P * (t + 1)], AX, ALU.max, negate=True)\
                    .then_inc(sem["c_nmax"], 1)
            if t == 0 and lagged(it, s, -4):
                dve.wait_ge(sem["c_res1"], TPS * (b + 2))
                for u in range(TPS):
                    nc.vector.bn_stats(st[0][:, u, :], res1[:, u, :]).then_inc(sem["c_bn1"], 1)
            if gate2:
                dve.wait_ge(sem["c_top2"], b - 1)
                nc.vector.tensor_tensor(hit[:, :, :], score2[:, :, :], spread(top[:, 1, :]), ALU.is_ge).then_inc(sem["c_ge2"], 1)
            between(4)
            if lagged(it, s, 2):
                u, q = (s - 2) % TPS, ((s - 2) // TPS) % 2
                bb = b if t >= 2 else b - 1
                dve.wait_ge(sem["c_o_ps"], n - 1)
                dve.wait_ge(sem["c_rinv"], n - 1)
                wait(dve, sem["c_x3"], TPS * (bb - 1))
                nc.vector.scalar_tensor_tensor(res2[q][:, u, :], p_o[:, 0:C], rinv[s % 2][:, 0:1], x2[q][:, u, :],
                                               ALU.mult, ALU.add).then_inc(sem["c_res2"], 1)
            if gate2:
                dve.wait_ge(sem["c_ge2"], b - 1)
                nc.vector.tensor_tensor(hit2[:, :, :], hit[:, :, :], rev[:, :, :], ALU.mult).then_inc(sem["c_hit2"], 1)
            if lagged(it, s, 2):
                dve.wait_ge(sem["c_res2"], n - 1)
                nc.vector.bn_stats(st[1][:, (s - 2) % TPS, :], res2[((s - 2) // TPS) % 2][:, (s - 2) % TPS, :]).then_inc(sem["c_bn2"], 1)
            if t == 0 and lagged(it, s, -4):
                wait_apart(dve, sem["c_bn1"], TPS * (b + 2))
                for u in range(TPS):
                    nc.vector.bn_aggr(mv[0][:, u, :], st[0][:, u, :]).then_inc(sem["c_var1"], 1)
            if lagged(it, s, 2):
                if ln2:
                    wait_apart(dve, sem["c_shift2"], b)
                wait_apart(dve, sem["c_bn2"], n - 1)
                u = (s - 2) % TPS
                nc.vector.bn_aggr(mv[1][:, u, :], st[1][:, u, :]).then_inc(sem["c_var2"], 1)
            if gate1:
                dve.wait_ge(sem["c_ez"], b - 1)
                nc.vector.tensor_scalar(e1p[:, :, :], ez[:, :, :], 1.0, None, ALU.add).then_inc(sem["c_e1p"], 1)
                dve.wait_ge(sem["c_e1p"], b - 1)
                nc.vector.reciprocal(score[:, :, :], e1p[:, :, :]).then_inc(sem["c_score"], 1)
                dve.wait_ge(sem["c_score"], b - 1)
                nc.vector.tensor_reduce(top[:, 0, :], score[:, :, :], AX, ALU.max).then_inc(sem["c_top1"], 1)
                dve.wait_ge(sem["c_top1"], b - 1)
                nc.vector.tensor_tensor(hit[:, :, :], score[:, :, :], spread(top[:, 0, :]), ALU.is_ge).then_inc(sem["c_ge1"], 1)
                dve.wait_ge(sem["c_ge1"], b - 1)
                nc.vector.tensor_tensor(hit2[:, :, :], hit[:, :, :], rev[:, :, :], ALU.mult).then_inc(sem["c_hit1"], 1)
                dve.wait_ge(sem["c_hit1"], b - 1)
                nc.vector.tensor_reduce(who[:, 0, :], hit2[:, :, :], AX, ALU.max).then_inc(sem["c_who1"], 1)
                dve.wait_ge(sem["c_who1"], b - 1)
                nc.vector.tensor_tensor(hot1[:, :, :], rev[:, :, :], spread(who[:, 0, :]), ALU.is_equal).then_inc(sem["c_hot1"], 1)
            if gate2:
                dve.wait_ge(sem["c_hit2"], b - 1)
                nc.vector.tensor_reduce(who[:, 1, :], hit2[:, :, :], AX, ALU.max).then_inc(sem["c_who2"], 1)
                dve.wait_ge(sem["c_who2"], b - 1)
                nc.vector.tensor_tensor(hot2[:, :, :], rev[:, :, :], spread(who[:, 1, :]), ALU.is_equal).then_inc(sem["c_hot2"], 1)
                dve.wait_ge(sem["c_hot2"], b - 1)
                wait(dve, sem["c_rank_ps"], b - 2)
                nc.vector.tensor_tensor(hot[:, :, :], hot1[:, :, :], hot2[:, :, :], ALU.add).then_inc(sem["c_hot"], 1)
            if gate3:
                bb, q = b - 2, par
                dve.wait_ge(sem["c_rank_ps"], bb + 1)
                nc.vector.tensor_tensor(at[:, :, :], p_g[:, 64:64 + TPS * E1].rearrange("p (t e) -> p t e", t=TPS),
                                        base[:, :, :], ALU.add).then_inc(sem["c_at"], 1)
                nc.vector.tensor_reduce(batch_n[:, :], hot[:, :, :].rearrange("p t e -> p e t"), AX, ALU.add)\
                    .then_inc(sem["c_batch_n"], 1)
                nc.vector.scalar_tensor_tensor(total[:, 0, :], top[:, 0, :], 1e-6, top[:, 1, :], ALU.add, ALU.add)\
                    .then_inc(sem["c_total"], 1)
                dve.wait_ge(sem["c_at"], bb + 1)
                nc.vector.tensor_tensor(at1[:, :, :], at[:, :, :], hot1[:, :, :], ALU.mult).then_inc(sem["c_at1"], 1)
                nc.vector.tensor_tensor(at2[:, :, :], at[:, :, :], hot2[:, :, :], ALU.mult).then_inc(sem["c_at2"], 1)
                dve.wait_ge(sem["c_batch_n"], bb + 1)
                nc.vector.tensor_tensor(seen[:, :], seen[:, :], batch_n[:, :], ALU.add).then_inc(sem["c_seen"], 1)
                dve.wait_ge(sem["c_total"], bb + 1)
                nc.vector.reciprocal(total[:, 1, :], total[:, 0, :]).then_inc(sem["c_rtotal"], 1)
                if not isinstance(it, int) or bb >= 2:
                    dve.wait_ge(sem[f"c_scatter_out{q}"], 128 * (it - 1))
                    dve.wait_ge(sem[f"c_meta_out{q}"], 16 * (it - 1))
                    nc.vector.tensor_scalar(x3[q][:, :, C], x3[q][:, :, C], float(2 * SEQ), None, ALU.add)
                nc.vector.tensor_copy(x3[q][:, :, C + 1], who[:, 0, :])
                with nc.allow_low_precision(reason="sums of one whole number and zeros, in float32 inside"):
                    dve.wait_ge(sem["c_at1"], bb + 1)
                    nc.vector.tensor_reduce(place[q][:, 0, :], at1[:, :, :], AX, ALU.add)
                    dve.wait_ge(sem["c_at2"], bb + 1)
                    nc.vector.tensor_reduce(place[q][:, 1, :], at2[:, :, :], AX, ALU.add)
                dve.wait_ge(sem["c_rtotal"], bb + 1)
                for k in range(2):
                    last = nc.vector.tensor_tensor(share[q][:, k, :], top[:, k, :], total[:, 1, :], ALU.mult)
                last.then_inc(sem["c_place"], 1)
        rows_of(dve, body)


def phase_experts1(nc, dram, const, sem, ctx):
    def sb(name, shape, dt=F32):
        return ctx.enter_context(nc.sbuf_tensor("d_" + name, shape, dt))

    def ps(name):
        return ctx.enter_context(nc.psum_tensor("d_ps_" + name, [P, 512], F32))

    ident, seen = const["ident"], const["seen"]
    U, T, FC = 4, 2, F1 // P
    NB = REGION1 - 1
    ones16 = sb("ones16", [P, P], BF16)
    zeros = sb("zeros", [P, T, ROW1])
    starts, up_to, row_number = sb("starts", [P, E1, NB]), sb("up_to", [P, E1, E1]), sb("row_number", [P, 1])
    tile_number, ended = sb("tile_number", [P, TILES1]), sb("ended", [P, TILES1, E1])
    own = sb("own", [P, TILES1])
    base = sb("base", [P, E1])
    count, full, blocks = sb("count", [P, E1]), sb("full", [P, E1, NB]), sb("blocks", [P, E1])
    part, cum, before, before_n = sb("part", [P, E1, E1]), sb("cum", [P, E1]), sb("before", [P, E1]), sb("before_n", [P, E1])
    expert, first_of, local, known = (sb(n, [P, 1]) for n in ("expert", "first_of", "local", "known"))
    table = sb("table", [P, 2], U32)
    table_row = sb("table_row", [1, P, 2], U32)
    tails = sb("tails", [P, E1], U32)
    xs = [sb(f"xs{i}", [P, T, ROW1]) for i in range(U)]
    second = [sb(f"second{i}", [P, T]) for i in range(U)]
    dest = [sb(f"dest{i}", [P, T], U32) for i in range(U)]
    w12 = [sb(f"w12{i}", [P, 2, F1]) for i in range(U)]
    xsT = [sb(f"xsT{i}", [P, BLK1]) for i in range(2)]
    hT = [sb(f"hT{i}", [P, FC, BLK1]) for i in range(2)]
    ys = [sb(f"ys{i}", [P, T, C]) for i in range(U)]
    p_x = [ps("x0"), ps("x1")]
    p_h = [ps(f"h{i}") for i in range(4)]
    p_y = [ps("y0"), ps("y1")]
    xs_blocks = dram["xs1"].rearrange("(k t p) c -> k p t c", p=P, t=T)
    NBLOCKS = E1 * REGION1 + SPARE1
    block = ctx.enter_context(nc.Block())

    def live(it, s, lag):
        return not isinstance(it, int) or 0 <= U * it + s - lag < TILES1

    def turns(eng, body):
        for it in (-1, 0, 1):
            for s in range(U):
                body(it, s)
        with eng.Fori(2, TILES1 // U - 1) as it:
            for s in range(U):
                body(it, s)
        for s in range(U + 3):
            body(TILES1 // U - 1 + s // U, s % U)

    @block.sync
    def _(sp):
        sp.dma_start(starts[:, :, :].rearrange("p a b -> p (a b)"), dram["block_starts"]).then_inc(sem["d_const_in"], 16)
        sp.dma_start(up_to[:, :, :].rearrange("p a b -> p (a b)"), dram["up_to"]).then_inc(sem["d_const_in"], 16)
        sp.dma_start(row_number[:, :], dram["row_number"]).then_inc(sem["d_const_in"], 16)
        sp.dma_start(tile_number[:, :], dram["tile_number"]).then_inc(sem["d_const_in"], 16)
        sp.dma_start(base[:, :], dram["region1"].rearrange("p (t e) -> p t e", e=E1)[:, 0, :], ).then_inc(sem["d_const_in"], 16)
        sp.wait_ge(sem["d_table"], 2)
        sp.dma_start(dram["tile_table"], table[:, :]).then_inc(sem["d_table_out"], 16)
        sp.wait_ge(sem["d_table_out"], 16)
        sp.dma_start(table_row[:, :, :], dram["tile_table"].rearrange("(a p) k -> a p k", a=1)).then_inc(sem["d_table_in"], 16)
        sp.wait_ge(sem["d_tails"], 1)
        for e in range(E1):
            row = sp.value_load(tails[0:1, e:e + 1], min_val=e * REGION1 * BLK1, max_val=(e + 1) * REGION1 * BLK1 - BLK1)
            sp.dma_start(dram["xs1"][bass.ds(row, BLK1), :].rearrange("(t p) c -> p t c", p=P), zeros[:, :, :])\
                .then_inc(sem["d_tails_out"], 16)
        sp.wait_ge(sem["d_tails_out"], 16 * E1)
        sp.wait_ge(sem["d_table_in"], 16)

        def body(it, s):
            n = U * it + s
            if live(it, s, -3):
                q = (s + 3) % U
                wait(sp, sem["d_y_ps"], n)
                wait(sp, sem["d_dest"], n)
                i = n + 3
                blk = sp.value_load(table_row[0:1, bass.ds(i, 1), 0], min_val=0, max_val=NBLOCKS - 1)
                exp = sp.value_load(table_row[0:1, bass.ds(i, 1), 1], min_val=0, max_val=E1 - 1)
                sp.dma_start(xs[q][:, :, :], xs_blocks[blk]).then_inc(sem[f"d_xs_in{q}"], 16)
                sp.dma_start(w12[q][:, :, :].rearrange("p a b -> p (a b)"), dram["w12_1"][exp]).then_inc(sem[f"d_w_in{q}"], 16)
        turns(sp, body)

    @block.gpsimd
    def _(pool):
        def body(it, s):
            n = U * it + s
            if live(it, s, 2):
                q = (s - 2) % U
                wait_apart(pool, sem["d_dest"], n - 1)
                for t in range(T):
                    pool.indirect_dma_start(dram["told"], bass.IndirectOffsetOnAxis(dest[q][:, t:t + 1], 0),
                                            ys[q][:, t, :], None, bounds_check=2 * NT * P - 1, oob_is_err=False)\
                        .then_inc(sem[f"d_ys_out{q}"], 16)
        turns(pool, body)
        for q in range(U):
            pool.wait_ge(sem[f"d_ys_out{q}"], 16 * T * TILES1 // U)

    @block.tensor
    def _(pe):
        pe.wait_ge(sem["d_ones"], 1)
        nc.tensor.matmul(p_y[0][:, 0:E1], ones16[:, :], seen[:, :], start=True, stop=True).then_inc(sem["d_count_ps"], 1)
        pe.wait_ge(sem["d_count"], 1)

        def body(it, s):
            n = U * it + s
            if live(it, s, -1):
                q = (s + 1) % U
                pe.wait_ge(sem[f"d_xs_in{q}"], 16 * (it + 1 + (s + 1) // U))
                wait(pe, sem["d_xsT_sb"], n)
                for t in range(T):
                    last = nc.tensor.transpose(p_x[(s + 1) % 2][:, P * t:P * t + P], xs[q][:, t, 0:C], ident[:, :])
                last.then_inc(sem["d_xsT_ps"], 1)
            if live(it, s, 0):
                pe.wait_ge(sem["d_xsT_sb"], n + 1)
                pe.wait_ge(sem[f"d_w_in{s}"], 16 * (it + 1))
                for k in range(FC):
                    wait(pe, sem["d_silu"], 2 * n + k - 3)
                    nc.tensor.matmul(p_h[2 * (s % 2) + k][:, 0:BLK1], w12[s][:, 0, P * k:P * k + P], xsT[s % 2][:, :],
                                     start=True, stop=True).then_inc(sem["d_h_ps"], 1)
            if live(it, s, 1):
                q = (s - 1) % U
                pe.wait_ge(sem["d_silu"], 2 * n)
                wait(pe, sem["d_ys_sb"], n - 2)
                for t in range(T):
                    for k in range(FC):
                        last = nc.tensor.matmul(p_y[q % 2][:, P * t:P * t + P], hT[q % 2][:, k, P * t:P * t + P],
                                                w12[q][:, 1, C * k:C * k + C], start=(k == 0), stop=(k == FC - 1),
                                                skip_group_check=True)
                last.then_inc(sem["d_y_ps"], 1)
        turns(pe, body)

    @block.scalar
    def _(act):
        def body(it, s):
            n = U * it + s
            if live(it, s, 0):
                wait(act, sem["d_y_ps"], n - 1)
                for k in range(FC):
                    act.wait_ge(sem["d_h_ps"], 2 * n + k + 1)
                    nc.scalar.activation(hT[s % 2][:, k, :], p_h[2 * (s % 2) + k][:, 0:BLK1], ACT.Silu)\
                        .then_inc(sem["d_silu"], 1)
        turns(act, body)

    @block.vector
    def _(dve):
        def spread(a, n):
            return a.rearrange("p (e a) -> p e a", a=1).to_broadcast([P, E1, n])

        step = [0]

        def then(ins):
            step[0] += 1
            ins.then_inc(sem["d_plan"], 1)
            dve.wait_ge(sem["d_plan"], step[0])

        nc.vector.memset(ones16[:, :], 1.0).then_inc(sem["d_ones"], 1)
        nc.vector.memset(zeros[:, :, :], 0.0)
        dve.wait_ge(sem["d_count_ps"], 1)
        nc.vector.tensor_copy(count[:, :], p_y[0][:, 0:E1]).then_inc(sem["d_count"], 1)
        dve.wait_ge(sem["d_count"], 1)
        dve.wait_ge(sem["d_const_in"], 16 * 5)
        nc.vector.tensor_tensor(tails[:, :], count[:, :], base[:, :], ALU.add).then_inc(sem["d_tails"], 1)
        then(nc.vector.tensor_tensor(full[:, :, :], starts[:, :, :], spread(count[:, :], NB), ALU.is_lt))
        then(nc.vector.tensor_reduce(blocks[:, :], full[:, :, :], AX, ALU.add))
        then(nc.vector.tensor_tensor(part[:, :, :], up_to[:, :, :],
                                     blocks[:, :].rearrange("p (a e) -> p a e", a=1).to_broadcast([P, E1, E1]), ALU.mult))
        then(nc.vector.tensor_reduce(cum[:, :], part[:, :, :], AX, ALU.add))
        then(nc.vector.tensor_scalar(before[:, :], cum[:, :], row_number[:, 0:1], None, ALU.is_le))
        then(nc.vector.tensor_reduce(expert[:, :], before[:, :], AX, ALU.add))
        then(nc.vector.tensor_tensor(before_n[:, :], before[:, :], blocks[:, :], ALU.mult))
        then(nc.vector.tensor_reduce(first_of[:, :], before_n[:, :], AX, ALU.add))
        then(nc.vector.tensor_tensor(local[:, :], row_number[:, :], first_of[:, :], ALU.subtract))
        then(nc.vector.tensor_scalar(known[:, :], local[:, :], float(NBLOCKS - 1), None, ALU.min))
        nc.vector.tensor_scalar(table[:, 1:2], expert[:, :], float(E1 - 1), None, ALU.min).then_inc(sem["d_table"], 1)
        then(nc.vector.tensor_scalar(local[:, :], expert[:, :], float(REGION1), known[:, 0:1], ALU.mult, ALU.add))
        nc.vector.tensor_scalar(table[:, 0:1], local[:, :], float(NBLOCKS - 1), None, ALU.min).then_inc(sem["d_table"], 1)
        then(nc.vector.tensor_tensor(ended[:, :, :], tile_number[:, :].rearrange("p (n a) -> p n a", a=1)
                                     .to_broadcast([P, TILES1, E1]),
                                     cum[:, :].rearrange("p (a e) -> p a e", a=1).to_broadcast([P, TILES1, E1]), ALU.is_ge))
        then(nc.vector.tensor_reduce(own[:, :], ended[:, :, :], AX, ALU.add))
        then(nc.vector.tensor_scalar(own[:, :], own[:, :], -1.0, float(E1), ALU.mult, ALU.add))

        def body(it, s):
            n = U * it + s
            if live(it, s, -1):
                dve.wait_ge(sem["d_xsT_ps"], n + 2)
                wait(dve, sem["d_h_ps"], 2 * n)
                nc.vector.tensor_copy(xsT[(s + 1) % 2][:, :], p_x[(s + 1) % 2][:, 0:BLK1]).then_inc(sem["d_xsT_sb"], 1)
            if live(it, s, 1):
                q = (s - 1) % U
                dve.wait_ge(sem["d_y_ps"], n)
                if not isinstance(it, int) or n - 1 >= U:
                    dve.wait_ge(sem[f"d_ys_out{q}"], 16 * T * (it if s >= 1 else it - 1))
                nc.vector.tensor_copy(ys[q][:, :, :].rearrange("p t c -> p (t c)"), p_y[q % 2][:, 0:BLK1])\
                    .then_inc(sem["d_ys_sb"], 1)
                nc.vector.tensor_scalar(second[q][:, :], xs[q][:, :, C + 1], own[:, bass.ds(n - 1, 1)], float(NT * P),
                                        ALU.not_equal, ALU.mult).then_inc(sem["d_second"], 1)
                dve.wait_ge(sem["d_second"], n)
                nc.vector.scalar_tensor_tensor(dest[q][:, :], xs[q][:, :, C], 2.0 * NT * P, second[q][:, :], ALU.add, ALU.add)\
                    .then_inc(sem["d_dest"], 1)
        turns(dve, body)


def phase_combine1(nc, dram, const, sem, ctx):
    def sb(name, shape, dt=F32):
        return ctx.enter_context(nc.sbuf_tensor("e_" + name, shape, dt))

    eps = const["eps"]
    NB = 4
    x3 = [sb(f"x3{i}", [P, TPS, C]) for i in range(NB)]
    share = [sb(f"share{i}", [P, 2, TPS]) for i in range(NB)]
    told = [sb(f"told{i}", [P, 2, TPS, C]) for i in range(NB)]
    one = sb("one", [P, TPS, C])
    res = [sb(f"res{i}", [P, TPS, C]) for i in range(NB)]
    y = [sb(f"y{i}", [P, TPS, C]) for i in range(NB)]
    st = [sb(f"st{i}", [P, TPS, 6]) for i in range(NB)]
    mv = [sb(f"mv{i}", [P, TPS, 2]) for i in range(NB)]
    ln = [sb(f"ln{i}", [P, 6, TPS]) for i in range(NB)]
    x3_rows = dram["x3"].rearrange("(b t p) c -> b p t c", p=P, t=TPS)
    told_rows = dram["told"].rearrange("(k b t p) c -> k b p t c", p=P, t=TPS, k=2)
    out_rows = dram["out"].rearrange("b (t p) c -> b p t c", p=P)
    block = ctx.enter_context(nc.Block())

    def live(it, s, lag):
        return not isinstance(it, int) or 0 <= NB * it + s - lag < NSEQ

    def turns(eng, body):
        for it in (-1, 0, 1):
            for s in range(NB):
                body(it, s)
        with eng.Fori(2, NSEQ // NB - 1) as it:
            for s in range(NB):
                body(it, s)
        for s in range(NB + 3):
            body(NSEQ // NB - 1 + s // NB, s % NB)

    @block.sync
    def _(sp):
        def body(it, s):
            b = NB * it + s
            if live(it, s, -3):
                q = (s + 3) % NB
                wait(sp, sem["e_res"], TPS * b)
                arrived = sem[f"e_in{q}"]
                sp.dma_start(share[q][:, :, :], dram["share_of"][b + 3]).then_inc(arrived, 16)
                sp.dma_start(x3[q][:, :, :], x3_rows[b + 3]).then_inc(arrived, 16)
                for k in range(2):
                    sp.dma_start(told[q][:, k, :, :], told_rows[k][b + 3]).then_inc(arrived, 16)
        turns(sp, body)

    @block.scalar
    def _(act):
        nc.scalar.preload_act_table_set("natural_log_exp_and_others")

        def body(it, s):
            b = NB * it + s
            if live(it, s, 0):
                act.wait_ge(sem["e_var"], TPS * (b + 1))
                nc.scalar.activation(ln[s][:, 0, :], mv[s][:, :, 1], ACT.Ln, bias=eps[:, 0:1]).then_inc(sem["e_ln"], 1)
                act.wait_ge(sem["e_ln"], b + 1)
                nc.scalar.activation(ln[s][:, 1, :], ln[s][:, 0, :], ACT.Exp, scale=-0.5).then_inc(sem["e_guess"], 1)
            if live(it, s, 1):
                q = (s - 1) % NB
                act.wait_ge(sem["e_shift"], b)
                if not isinstance(it, int) or b - 1 >= NB:
                    act.wait_ge(sem[f"e_out{q}"], 16 * (it if s >= 1 else it - 1))
                for u in range(TPS):
                    nc.scalar.activation(y[q][:, u, :], res[q][:, u, :], ACT.Identity, bias=ln[q][:, 5, u:u + 1],
                                         scale=ln[q][:, 4, u:u + 1]).then_inc(sem["e_y"], 1)
                act.wait_ge(sem["e_y"], TPS * b)
                nc.scalar.dma_start(out_rows[b - 1], y[q][:, :, :]).then_inc(sem[f"e_out{q}"], 16)
        turns(act, body)
        for q in range(NB):
            act.wait_ge(sem[f"e_out{q}"], 16 * NSEQ // NB)

    @block.vector
    def _(dve):
        def body(it, s):
            b = NB * it + s
            q, c = (s - 1) % NB, b - 1
            mean, var = mv[q][:, :, 0], mv[q][:, :, 1]
            _, first, half, square, rstd, shift = (ln[q][:, r, :] for r in range(6))
            done = sem["e_newton"]
            if live(it, s, 0):
                dve.wait_ge(sem[f"e_in{s}"], 64 * (it + 1))
                for u in range(TPS):
                    nc.vector.scalar_tensor_tensor(one[:, u, :], told[s][:, 0, u, :], share[s][:, 0, u:u + 1], x3[s][:, u, :],
                                                   ALU.mult, ALU.add).then_inc(sem["e_one"], 1)
            if live(it, s, 1):
                dve.wait_ge(sem["e_guess"], b)
                nc.vector.scalar_tensor_tensor(half, var, EPS, first, ALU.add, ALU.mult).then_inc(done, 1)
            if live(it, s, 0):
                if not isinstance(it, int) or b >= NB:
                    dve.wait_ge(sem["e_y"], TPS * (b - NB + 1))
                for u in range(TPS):
                    dve.wait_ge(sem["e_one"], TPS * b + u + 1)
                    nc.vector.scalar_tensor_tensor(res[s][:, u, :], told[s][:, 1, u, :], share[s][:, 1, u:u + 1], one[:, u, :],
                                                   ALU.mult, ALU.add).then_inc(sem["e_res"], 1)
            if live(it, s, 1):
                dve.wait_ge(done, 4 * c + 1)
                nc.vector.tensor_tensor(square, half, first, ALU.mult).then_inc(done, 1)
            if live(it, s, 0):
                for u in range(2):
                    dve.wait_ge(sem["e_res"], TPS * b + u + 1)
                    nc.vector.bn_stats(st[s][:, u, :], res[s][:, u, :]).then_inc(sem["e_bn"], 1)
            if live(it, s, 1):
                dve.wait_ge(done, 4 * c + 2)
                nc.vector.tensor_scalar(half, square, -0.5, 1.5, ALU.mult, ALU.add).then_inc(done, 1)
            if live(it, s, 0):
                for u in range(2, TPS):
                    dve.wait_ge(sem["e_res"], TPS * b + u + 1)
                    nc.vector.bn_stats(st[s][:, u, :], res[s][:, u, :]).then_inc(sem["e_bn"], 1)
            if live(it, s, 1):
                dve.wait_ge(done, 4 * c + 3)
                nc.vector.tensor_tensor(rstd, half, first, ALU.mult).then_inc(done, 1)
            if live(it, s, 0):
                wait_apart(dve, sem["e_bn"], TPS * (b + 1))
                for u in range(TPS):
                    nc.vector.bn_aggr(mv[s][:, u, :], st[s][:, u, :]).then_inc(sem["e_var"], 1)
            if live(it, s, 1):
                dve.wait_ge(done, 4 * c + 4)
                nc.vector.scalar_tensor_tensor(shift, mean, -1.0, rstd, ALU.mult, ALU.mult).then_inc(sem["e_shift"], 1)
        turns(dve, body)


PHASES = (phase_attention0, phase_experts0, phase_attention1, phase_experts1, phase_combine1)


class Semaphores(dict):

    def __init__(self, nc):
        self.nc = nc

    def __missing__(self, name):
        self[name] = self.nc.alloc_semaphore(name=name)
        return self[name]


def build(nc, dram, phases=PHASES):
    assert TILES1 >= 2 * NT * P // BLK1 + E1 - 1
    with ExitStack() as ctx:
        const = {"eps": ctx.enter_context(nc.sbuf_tensor("eps", [P, 1], F32)),
                 "ident": ctx.enter_context(nc.sbuf_tensor("ident", [P, P], F32)),
                 "seen": ctx.enter_context(nc.sbuf_tensor("seen", [P, E1], BF16))}
        for phase in phases:
            sem = Semaphores(nc)
            with ExitStack() as of_phase:
                phase(nc, dram, const, sem, of_phase)
            nc.clear_and_free_semaphores(list(sem.values()))
            nc.all_engine_barrier()


SCRATCH = {"x1": ((NT * P, C), F32), "slots": ((SLOTS, ROW0), F32), "moe": ((NT * P, C), F32),
           "slot_of": ((NSEQ, P, TPS), U32), "weight_of": ((NSEQ, P, TPS), F32), "x3": ((NT * P, C), F32),
           "xs1": (((E1 * REGION1 + SPARE1) * BLK1, ROW1), F32), "told": ((2 * NT * P, C), F32),
           "share_of": ((NSEQ, P, 2 * TPS), F32),
           "tile_table": ((P, 2), U32)}


def laid_out(i):
    import numpy as np
    c = np.ascontiguousarray
    w = {k: np.asarray(v) for k, v in i.items()}
    x = w["L0_attn_x"]
    wqkv = w["L0_attn_w_qkv"]
    wv = wqkv[2 * C:].reshape(4, 2, D0, C)
    i_q, k = np.arange(P)[:, None] % QB, np.arange(WIN)[None, :]
    band = (k > i_q) & (k < i_q + 2 * BAND)
    masks = [band, band & (k >= BAND), band & (k < WIN - BAND)]
    tok = np.arange(P)
    return {
        "x": c(x), "xT": c(x.transpose(0, 2, 1)),
        "wqkvT": c(wqkv[:2 * C].T), "wv_by_parity": c(wv.transpose(3, 1, 0, 2).reshape(C, C)),
        "wprojT": c(w["L0_attn_w_proj"].T), "bqkv": c(w["L0_attn_b_qkv"].reshape(3, C).T),
        "bproj": c(np.broadcast_to(w["L0_attn_b_proj"], (P, C))),
        "gate0T": c(w["L0_ffn_gate_w"].T),
        "w1_0": c(w["L0_ffn_w1"]), "w2_0": c(w["L0_ffn_w2"]),
        "wqk1": c(np.concatenate([w["L1_attn_Wq"], w["L1_attn_Wk"]], 1)), "wv1": c(w["L1_attn_Wv"]),
        "gate1T": c(w["L1_ffn_gate_w"].T),
        "balance": c(np.broadcast_to(np.tile(w["L1_ffn_balance_bias"], TPS), (P, TPS * E1))),
        "w12_1": c(np.concatenate([w["L1_ffn_w1"].transpose(0, 2, 1),
                                   w["L1_ffn_w2"].reshape(E1, C, F1 // P, P).transpose(0, 3, 2, 1).reshape(E1, P, F1)], 2)),
        "band_mask": c(np.concatenate([np.where(m, 0, -1e30) for m in masks], 1).astype(np.float32)),
        "causal": np.where(tok[None, :] <= tok[:, None], 0, -1e30).astype(np.float32),
        "before": (tok[:, None] < tok[None, :]).astype(np.float32),
        "ident": np.eye(P, dtype=np.float32),
        "rev1": c(np.broadcast_to(np.tile(E1 - np.arange(E1), TPS), (P, TPS * E1)).astype(np.float32)),
        "region1": c(np.broadcast_to(np.tile(np.arange(E1) * REGION1 * BLK1, TPS), (P, TPS * E1)).astype(np.float32)),
        "block_starts": c(np.broadcast_to(np.tile(np.arange(REGION1 - 1) * BLK1, E1), (P, E1 * (REGION1 - 1))).astype(np.float32)),
        "up_to": c(np.broadcast_to(np.tri(E1).reshape(-1), (P, E1 * E1)).astype(np.float32)),
        "token_of": c((np.arange(2 * TPS)[None, :] * P + tok[:, None]).astype(np.float32)),
        "tile_number": c(np.broadcast_to(np.arange(TILES1), (P, TILES1)).astype(np.float32)),
        "row_number": c(tok[:, None].astype(np.float32)),
        "rev": c(np.broadcast_to(np.tile(E0 - np.arange(E0), TPS), (P, TPS * E0)).astype(np.float32)),
    }


def kernel(**inputs):
    import numpy as np
    import concourse.bacc as bacc
    from concourse.bass_utils import run_bass_kernel_spmd

    arrays = laid_out(inputs)
    nc = bacc.Bacc("TRN2", target_bir_lowering=False, num_devices=1)
    dram = {n: nc.dram_tensor("in_" + n, a.shape, mybir.dt.from_np(a.dtype), kind="ExternalInput").ap()
            for n, a in arrays.items()}
    for n, (shape, dt) in SCRATCH.items():
        dram[n] = nc.dram_tensor("scratch_" + n, shape, dt, kind="Internal").ap()
    dram["out"] = nc.dram_tensor("out_0", (NSEQ, SEQ, C), F32, kind="ExternalOutput").ap()
    build(nc, dram)
    r = run_bass_kernel_spmd(nc, [{"in_" + n: a for n, a in arrays.items()}], core_ids=[0])
    return np.asarray(r.results[0]["out_0"])
```

```python
from contextlib import ExitStack

import concourse.bass as bass
from concourse import mybir

F32 = mybir.dt.float32
BF16 = mybir.dt.bfloat16
U32 = mybir.dt.uint32
ALU = mybir.AluOpType
ACT = mybir.ActivationFunctionType
AX = mybir.AxisListType.X

P = 128
SEQ = 512
NSEQ = 16
TPS = SEQ // P
NT = NSEQ * TPS
C = 128
EPS = 1e-5

H0, D0, BAND = 8, 16, 16
QB = 32
WIN = QB + 2 * BAND
NBLK = P // QB
PAD = BAND
SEQP = SEQ + 2 * PAD

E0, F0 = 16, 512
CAP = 640
SLOTS = E0 * CAP
NCAP = CAP // P
ROW0 = C + 1

DQ = 64
E1, F1 = 8, 256

BLK1 = 2 * P
REGION1 = NT * P // BLK1 + 1
SPARE1 = E1
ROW1 = C + 4
TILES1 = 72

PACKED1 = (("wqk1", C), ("wv1", C), ("causal", P), ("before", P), ("gate1T", E1), ("balance", TPS * E1),
           ("rev1", TPS * E1), ("region1", TPS * E1), ("token_of", 2 * TPS))

UNROLL = 2 * TPS


def wait(eng, sem, n):
    if not (isinstance(n, int) and n <= 0):
        eng.wait_ge(sem, n)


def wait_apart(eng, sem, n):
    if not isinstance(n, int):
        n = eng.to_reg(n)
        eng.wait_ge(sem, 1)
        eng.wait_ge(sem, n)
    elif n > 0:
        eng.wait_ge(sem, n)


def lagged(it, s, lag, total=NT):
    return not isinstance(it, int) or 0 <= UNROLL * it + s - lag < total


def steps(eng, body, peel, lag):
    for it in range(peel):
        for s in range(UNROLL):
            body(it, s)
    with eng.Fori(peel, NT // UNROLL - 1) as it:
        for s in range(UNROLL):
            body(it, s)
    for s in range(UNROLL + lag + 1):
        body(NT // UNROLL - 1 + s // UNROLL, s % UNROLL)


def phase_attention0(nc, dram, const, sem, ctx):
    def sb(name, shape, dt=F32):
        return ctx.enter_context(nc.sbuf_tensor("a_" + name, shape, dt))

    def ps(name, shape=(P, 512)):
        return ctx.enter_context(nc.psum_tensor("a_ps_" + name, list(shape), F32))

    wq, wk, wv, wp = (sb(n, [P, C]) for n in ("wq", "wk", "wv", "wp"))
    bqkv = sb("bqkv", [P, 3])
    bproj = sb("bproj", [P, C])
    gate_w = sb("gate_w", [P, E0])
    maskf = sb("maskf", [P, 3 * WIN])
    mask = sb("mask", [P, 3, WIN], BF16)
    ident16 = sb("ident16", [P, P], BF16)
    ones16 = sb("ones16", [P, P], BF16)
    tri_f = sb("tri_f", [P, P])
    tri16 = sb("tri16", [P, P], BF16)
    rev = sb("rev", [P, TPS, E0])
    zeros = sb("zeros", [P, 10 * ROW0])
    token_of = sb("token_of", [P, 2, TPS])

    x = [sb(f"x{i}", [P, TPS, C]) for i in range(2)]
    xT = [sb(f"xT{i}", [P, SEQP]) for i in range(2)]
    kT = sb("kT", [P, SEQ])
    kexp = [sb(f"kexp{i}", [P, H0, SEQP]) for i in range(2)]
    qT = [sb(f"qT{i}", [P, SEQ]) for i in range(2)]
    vexp = [sb(f"vexp{i}", [P, NBLK, 4, 32]) for i in range(TPS)]
    prob = [sb(f"prob{i}", [P, H0, WIN]) for i in range(TPS)]
    probT = [sb(f"probT{i}", [P, 4, P]) for i in range(2)]
    attT = [sb(f"attT{i}", [P, P]) for i in range(2)]
    mx = [sb(f"mx{i}", [P, H0]) for i in range(2)]
    sm = [sb(f"sm{i}", [P, H0]) for i in range(2)]
    rinv = [sb(f"rinv{i}", [P, H0]) for i in range(TPS)]
    res = [sb(f"res{i}", [P, TPS, C]) for i in range(2)]
    y = [sb(f"y{i}", [P, TPS, ROW0]) for i in range(2)]
    yT = sb("yT", [P, SEQ])
    st = [sb(f"st{i}", [P, TPS, 6]) for i in range(2)]
    ln = [sb(f"ln{i}", [P, 6, TPS]) for i in range(2)]
    mv = [sb(f"mv{i}", [P, TPS, 2]) for i in range(2)]
    lmax = sb("lmax", [P, TPS])
    lsub = sb("lsub", [P, TPS, E0])
    lexp = sb("lexp", [P, TPS, E0])
    first = sb("first", [P, TPS, E0])
    rmx = sb("rmx", [P, TPS])
    onehot = sb("onehot", [P, TPS, E0], BF16)
    ranked = sb("ranked", [P, TPS, E0])
    seen = sb("seen", [P, E0], BF16)
    batch_n = sb("batch_n", [P, E0])
    g = sb("g", [P, 6, TPS])
    gweight = [sb(f"gweight{i}", [P, TPS]) for i in range(2)]
    slot = [sb(f"slot{i}", [P, TPS], U32) for i in range(2)]

    p_q, p_k, p_v, p_pt, p_ap, p_g = (ps(n) for n in ("q", "k", "v", "pt", "ap", "g"))
    p_s = [ps(f"s{i}") for i in range(2)]
    p_av, p_pj = p_ap[:, 0:P], p_ap[:, P:P + C]
    eps, ident = const["eps"], const["ident"]

    block = ctx.enter_context(nc.Block())
    x_rows = dram["x"].rearrange("b (t p) c -> b p t c", p=P)
    x1_rows = dram["x1"].rearrange("(b t p) c -> b p t c", p=P, t=TPS)

    @block.sync
    def _(sp):
        def load_xT(b, par):
            sp.dma_start(xT[par][:, PAD:PAD + SEQ], dram["xT"][b]).then_inc(sem[f"a_xT_in{par}"], 16)

        def spread_keys(par):
            for h in range(H0):
                rows = slice(D0 * h, D0 * h + D0)
                sp.dma_start(kexp[par][rows, h, PAD:PAD + SEQ], kT[rows, :]).then_inc(sem[f"a_kexp_in{par}"], 16)

        for dst, src in ((wk[:, :], dram["wqkvT"][:, C:2 * C]), (bqkv[:, :], dram["bqkv"]),
                         (wq[:, :], dram["wqkvT"][:, 0:C]), (xT[0][:, PAD:PAD + SEQ], dram["xT"][0])):
            sp.dma_start(dst, src).then_inc(sem["a_first_in"], 16)
        for dst, src in ((wv, dram["wv_by_parity"]), (maskf, dram["band_mask"]), (ident, dram["ident"])):
            sp.dma_start(dst[:, :], src).then_inc(sem["a_mask_in"], 16)
        sp.wait_ge(sem["a_k_sb"], 1)
        sp.wait_ge(sem["a_zero"], 1)
        spread_keys(0)
        sp.wait_ge(sem["a_zero_pool"], 1)
        def body(it, s):
            t, par = s % TPS, (s // TPS) % 2
            b = 2 * it + par
            if t == 0 and lagged(it, s, -4):
                wait(sp, sem["a_v_ps"], TPS * b)
                load_xT(b + 1, 1 - par)
            if t == 1 and lagged(it, s, -3):
                wait(sp, sem["a_k_sb"], b + 2)
                wait(sp, sem["a_s_ps"], TPS * b)
                spread_keys(1 - par)
            if t == 3 and lagged(it, s, -1):
                wait(sp, sem["a_res"], TPS * b)
                sp.dma_start(x[1 - par][:, :, :], x_rows[b + 1]).then_inc(sem[f"a_x_in{1 - par}"], 16)
            if t == 2 and lagged(it, s, 10):
                q = par
                bb = b - 2
                sp.wait_ge(sem["a_y"], TPS * (bb + 1))
                sp.dma_start(x1_rows[bb], y[q][:, :, 0:C]).then_inc(sem[f"a_y_out{q}"], 16)
            if t == 1 and lagged(it, s, 13):
                q = 1 - par
                bb = b - 3
                sp.wait_ge(sem["a_slot"], bb + 1)
                sp.dma_start(dram["slot_of"][bb], slot[q][:, :]).then_inc(sem[f"a_meta_out{q}"], 16)
                sp.dma_start(dram["weight_of"][bb], gweight[q][:, :]).then_inc(sem[f"a_meta_out{q}"], 16)
        steps(sp, body, 3, 15)
        for q in range(2):
            sp.wait_ge(sem[f"a_y_out{q}"], 16 * NSEQ // 2)
            sp.wait_ge(sem[f"a_meta_out{q}"], 32 * NSEQ // 2)

    @block.tensor
    def _(pe):
        def project(out, w, par, done):
            nc.tensor.matmul(out[:, :], w[:, :], xT[par][:, PAD:PAD + SEQ], start=True, stop=True).then_inc(done, 1)

        pe.wait_ge(sem["a_first_in"], 16 * 4)
        project(p_k, wk, 0, sem["a_k_ps"])
        project(p_q, wq, 0, sem["a_q_ps"])
        pe.wait_ge(sem["a_mask_in"], 16 * 3)
        pe.wait_ge(sem["a_setup"], 1)
        pe.wait_ge(sem["a_const_in"], 16 * 7)

        def body(it, s):
            t, par = s % TPS, (s // TPS) % 2
            n = UNROLL * it + s
            b = 2 * it + par
            if lagged(it, s, 0):
                wait(pe, sem["a_v_sb"], n)
                for j in range(NBLK):
                    for odd in range(2):
                        last = nc.tensor.matmul(p_v[64 * odd:64 * odd + 64, 64 * j:64 * j + 64],
                                                xT[par][:, P * t + QB * j:P * t + QB * j + WIN],
                                                wv[:, 64 * odd:64 * odd + 64], start=True, stop=True, skip_group_check=True)
                last.then_inc(sem["a_v_ps"], 1)
            if t == 1 and lagged(it, s, -3):
                pe.wait_ge(sem["a_k_sb"], b + 1)
                pe.wait_ge(sem[f"a_xT_in{1 - par}"], 16 * (it + 1))
                project(p_k, wk, 1 - par, sem["a_k_ps"])
            if t == 2 and lagged(it, s, -2):
                pe.wait_ge(sem["a_q_sb"], b + 1)
                project(p_q, wq, 1 - par, sem["a_q_ps"])
            if lagged(it, s, 0):
                if t == 0:
                    pe.wait_ge(sem["a_q_sb"], b + 1)
                    pe.wait_ge(sem[f"a_kexp_in{par}"], 16 * H0 * (it + 1))
                wait(pe, sem["a_sub"], n - 1)
                out = p_s[s % 2]
                edge = 1 if t == 0 else 2 if t == TPS - 1 else 0
                for j in range(NBLK):
                    m = edge if (t == 0 and j == 0) or (t == TPS - 1 and j == NBLK - 1) else 0
                    q = slice(QB * j, QB * j + QB)
                    nc.tensor.matmul(out[q, :], ident16[:, q], mask[:, m:m + 1, :].to_broadcast([P, H0, WIN]),
                                     start=True, stop=False, skip_group_check=True)
                for j in range(NBLK):
                    q = slice(QB * j, QB * j + QB)
                    last = nc.tensor.matmul(out[q, :], qT[par][:, P * t + QB * j:P * t + QB * j + QB],
                                            kexp[par][:, :, P * t + QB * j:P * t + QB * j + WIN], start=False, stop=True,
                                            skip_group_check=True)
                last.then_inc(sem["a_s_ps"], 1)
            if lagged(it, s, 3):
                pe.wait_ge(sem["a_pt_sb"], n - 2)
                pe.wait_ge(sem["a_v_sb"], n - 2)
                wait(pe, sem["a_res"], n - 3)
                for j in range(NBLK):
                    for hp in range(4):
                        last = nc.tensor.matmul(p_av[32 * hp:32 * hp + 32, QB * j:QB * j + QB],
                                                vexp[(s - 3) % TPS][:, j, hp, :],
                                                probT[(s - 3) % 2][:, hp, QB * j:QB * j + QB], start=True, stop=True,
                                                skip_group_check=True)
                last.then_inc(sem["a_av_ps"], 1)
            if lagged(it, s, 2):
                pe.wait_ge(sem["a_norm"], n - 1)
                wait(pe, sem["a_pt_sb"], n - 2)
                for hp in range(4):
                    last = nc.tensor.transpose(p_pt[:, hp * P:hp * P + P], prob[(s - 2) % TPS][:, 2 * hp:2 * hp + 2, :]
                                               .rearrange("p a b -> p (a b)"),
                                               ident[:, :])
                last.then_inc(sem["a_pt_ps"], 1)
            if t == 2 and lagged(it, s, 10):
                bb = b - 2
                pe.wait_ge(sem["a_y"], TPS * (bb + 1))
                wait(pe, sem["a_slot"], bb)
                for u in range(TPS):
                    last = nc.tensor.transpose(p_g[:, P * u:P * u + P], y[par][:, u, 0:C], ident[:, :])
                last.then_inc(sem["a_yT_ps"], 1)
            if t == 3 and lagged(it, s, 11):
                bb = b - 2
                pe.wait_ge(sem["a_yT_sb"], bb + 1)
                for u in range(TPS):
                    last = nc.tensor.matmul(p_g[:, E0 * u:E0 * u + E0], yT[:, P * u:P * u + P], gate_w[:, :],
                                            start=(u == 0), stop=(u == TPS - 1), skip_group_check=True)
                last.then_inc(sem["a_logit_ps"], 1)
            if t == 0 and lagged(it, s, 12):
                bb = b - 3
                pe.wait_ge(sem["a_onehot"], bb + 1)
                out = p_g[:, 64:128]
                nc.tensor.matmul(out, ones16[:, :], seen[:, :].rearrange("p (a e) -> p a e", a=1).to_broadcast([P, TPS, E0]),
                                 start=True, stop=False, skip_group_check=True)
                nc.tensor.matmul(out, tri16[:, :], onehot[:, :, :], start=False, stop=False, skip_group_check=True)
                for u in range(TPS - 1):
                    last = nc.tensor.matmul(out[:, E0 * (u + 1):64], ones16[:, :],
                                            onehot[:, u:u + 1, :].to_broadcast([P, TPS - 1 - u, E0]),
                                            start=False, stop=(u == TPS - 2), skip_group_check=True)
                last.then_inc(sem["a_rank_ps"], 1)
            if lagged(it, s, 3):
                pe.wait_ge(sem["a_att_sb"], n - 2)
                nc.tensor.matmul(p_pj, attT[(s - 3) % 2][:, :], wp[:, :], start=True, stop=True)\
                    .then_inc(sem["a_pj_ps"], 1)
        steps(pe, body, 3, 15)

    @block.scalar
    def _(act):
        nc.scalar.preload_act_table_set("natural_log_exp_and_others")

        def k_out(value, par_of_old, old):
            act.wait_ge(sem["a_k_ps"], value)
            if old is not None:
                act.wait_ge(sem[f"a_kexp_in{par_of_old}"], old)
            nc.scalar.activation(kT[:, :], p_k[:, :], ACT.Identity, bias=bqkv[:, 1:2]).then_inc(sem["a_k_sb"], 1)

        def q_out(value, par, used):
            act.wait_ge(sem["a_q_ps"], value)
            wait(act, sem["a_s_ps"], used)
            nc.scalar.activation(qT[par][:, :], p_q[:, :], ACT.Identity, bias=bqkv[:, 0:1]).then_inc(sem["a_q_sb"], 1)

        for dst, src in ((x[0][:, :, :], x_rows[0]), (wp[:, :], dram["wprojT"]), (bproj[:, :], dram["bproj"]),
                         (tri_f[:, :], dram["before"]), (gate_w[:, :], dram["gate0T"]),
                         (rev[:, :, :], dram["rev"].rearrange("p (t e) -> p t e", e=E0)),
                         (token_of[:, :, :], dram["token_of"].rearrange("p (q t) -> p q t", q=2))):
            nc.scalar.dma_start(dst, src).then_inc(sem["a_const_in"], 16)
        act.wait_ge(sem["a_first_in"], 16 * 4)
        k_out(1, 0, None)
        q_out(1, 0, 0)
        act.wait_ge(sem["a_zero_pool"], 1)

        def body(it, s):
            t, par = s % TPS, (s // TPS) % 2
            n = UNROLL * it + s
            b = 2 * it + par
            if lagged(it, s, 0):
                act.wait_ge(sem["a_v_ps"], n + 1)
                wait(act, sem["a_av_ps"], n - 3)
                for odd in range(2):
                    rows = slice(64 * odd, 64 * odd + 64)
                    nc.scalar.copy(vexp[t][rows, :, :, 16 * odd:16 * odd + 16],
                                   p_v[rows, 0:256].rearrange("p (j h d) -> p j h d", j=NBLK, h=4))\
                        .then_inc(sem["a_v_half"] if odd == 0 else sem["a_v_sb"], 1)
            if lagged(it, s, 3):
                act.wait_ge(sem["a_av_ps"], n - 2)
                wait(act, sem["a_pj_ps"], n - 4)
                nc.scalar.activation(attT[(s - 3) % 2][:, :], p_av, ACT.Identity, bias=bqkv[:, 2:3])\
                    .then_inc(sem["a_att_sb"], 1)
            if t == 1 and lagged(it, s, -3):
                k_out(b + 2, par, 16 * H0 * (it + 1))
            if t == 2 and lagged(it, s, -2):
                q_out(b + 2, 1 - par, TPS * b)
            if lagged(it, s, 2):
                act.wait_ge(sem["a_pt_ps"], n - 1)
                wait(act, sem["a_av_ps"], n - 3)
                nc.scalar.copy(probT[(s - 2) % 2][:, :, :].rearrange("p a b -> p (a b)"), p_pt[:, :]).then_inc(sem["a_pt_sb"], 1)
            if t == 3 and lagged(it, s, 7):
                q = (s // TPS + 1) % 2
                bb = b - 1
                act.wait_ge(sem["a_var"], TPS * (bb + 1))
                nc.scalar.activation(ln[q][:, 0, :], mv[q][:, :, 1], ACT.Ln, bias=eps[:, 0:1]).then_inc(sem["a_ln"], 1)
                act.wait_ge(sem["a_ln"], bb + 1)
                nc.scalar.activation(ln[q][:, 1, :], ln[q][:, 0, :], ACT.Exp, scale=-0.5).then_inc(sem["a_guess"], 1)
            for due in range(2):
                if t == due and lagged(it, s, 8 + due):
                    q, bb = par, b - 2
                    if due == 0:
                        act.wait_ge(sem["a_shift"], bb + 1)
                        if not isinstance(it, int) or bb >= 2:
                            act.wait_ge(sem[f"a_scatter_out{q}"], 64 * (it - 1))
                            act.wait_ge(sem[f"a_y_out{q}"], 16 * (it - 1))
                            act.wait_ge(sem["a_yT_ps"], bb - 1)
                    for u in (2 * due, 2 * due + 1):
                        nc.scalar.activation(y[q][:, u, 0:C], res[q][:, u, :], ACT.Identity, bias=ln[q][:, 4, u:u + 1],
                                             scale=ln[q][:, 5, u:u + 1]).then_inc(sem["a_y"], 1)
            if lagged(it, s, 0):
                act.wait_ge(sem["a_sub"], n + 1)
                e = prob[t][:, :, :].rearrange("p a b -> p (a b)")
                nc.scalar.activation(e, e, ACT.Exp, scale=float(C) ** -0.5).then_inc(sem["a_exp"], 1)
            if t == 2 and lagged(it, s, 10):
                bb = b - 2
                act.wait_ge(sem["a_yT_ps"], bb + 1)
                wait(act, sem["a_logit_ps"], bb)
                nc.scalar.copy(yT[:, :], p_g[:, :]).then_inc(sem["a_yT_sb"], 1)
            if t == 3 and lagged(it, s, 11):
                bb = b - 2
                act.wait_ge(sem["a_lsub"], bb + 1)
                wait(act, sem["a_slot"], bb)
                nc.scalar.activation(lexp[:, :, :], lsub[:, :, :], ACT.Exp).then_inc(sem["a_gate_exp"], 1)
        steps(act, body, 3, 15)

    @block.vector
    def _(dve):
        nc.vector.memset(kexp[0][:, :, :], 0.0).then_inc(sem["a_zero"], 1)
        for q in range(2):
            nc.vector.memset(xT[q][:, 0:PAD], 0.0)
            nc.vector.memset(xT[q][:, PAD + SEQ:SEQP], 0.0)
        nc.vector.memset(eps[:, :], EPS)
        nc.vector.memset(ones16[:, :], 1.0)
        nc.vector.memset(seen[:, :], 0.0)
        dve.wait_ge(sem["a_mask_in"], 16 * 3)
        nc.vector.tensor_copy(mask[:, :, :].rearrange("p a b -> p (a b)"), maskf[:, :])
        nc.vector.tensor_copy(ident16[:, :], ident[:, :])
        dve.wait_ge(sem["a_const_in"], 16 * 7)
        for q in range(2):
            nc.vector.tensor_scalar(y[q][:, :, C], token_of[:, q, :], -float(NT * P), None, ALU.add)
        nc.vector.tensor_copy(tri16[:, :], tri_f[:, :]).then_inc(sem["a_setup"], 1)

        def body(it, s):
            t, par = s % TPS, (s // TPS) % 2
            n = UNROLL * it + s
            b = 2 * it + par
            if lagged(it, s, 0):
                dve.wait_ge(sem["a_s_ps"], n + 1)
                scores = p_s[s % 2][:, :].rearrange("p (h k) -> p h k", h=H0)
                nc.vector.tensor_reduce(mx[s % 2][:, :], scores, AX, ALU.max).then_inc(sem["a_max"], 1)
            if lagged(it, s, 0):
                wait(dve, sem["a_pt_ps"], n - 3)
                dve.wait_ge(sem["a_max"], n + 1)
                nc.vector.tensor_tensor(prob[t][:, :, :], scores,
                                        mx[s % 2][:, :].rearrange("p (h a) -> p h a", a=1).to_broadcast([P, H0, WIN]),
                                        ALU.subtract).then_inc(sem["a_sub"], 1)
            if lagged(it, s, 3):
                u, q = (s - 3) % TPS, ((s - 3) // TPS) % 2
                bb = b if t == 3 else b - 1
                dve.wait_ge(sem["a_pj_ps"], n - 2)
                dve.wait_ge(sem["a_xb"], bb + 1)
                wait(dve, sem["a_y"], TPS * (bb - 1))
                nc.vector.tensor_tensor(res[q][:, u, :], x[q][:, u, :], p_pj, ALU.add).then_inc(sem["a_res"], 1)
            if t == 3 and lagged(it, s, 11):
                bb = b - 2
                dve.wait_ge(sem["a_logit_ps"], bb + 1)
                logits = p_g[:, 0:64].rearrange("p (t e) -> p t e", t=TPS)
                nc.vector.tensor_reduce(lmax[:, :], logits, AX, ALU.max).then_inc(sem["a_lmax"], 1)
                dve.wait_ge(sem["a_lmax"], bb + 1)
                wait(dve, sem["a_gate_exp"], bb)
                nc.vector.tensor_tensor(lsub[:, :, :], logits,
                                        lmax[:, :].rearrange("p (t a) -> p t a", a=1).to_broadcast([P, TPS, E0]),
                                        ALU.subtract).then_inc(sem["a_lsub"], 1)
                dve.wait_ge(sem["a_lsub"], bb + 1)
                nc.vector.scalar_tensor_tensor(first[:, :, :], lsub[:, :, :], 0.0, rev[:, :, :], ALU.is_ge, ALU.mult)\
                    .then_inc(sem["a_first"], 1)
                dve.wait_ge(sem["a_first"], bb + 1)
                nc.vector.tensor_reduce(rmx[:, :], first[:, :, :], AX, ALU.max).then_inc(sem["a_rmx"], 1)
                dve.wait_ge(sem["a_rmx"], bb + 1)
                nc.vector.tensor_tensor(onehot[:, :, :], rev[:, :, :],
                                        rmx[:, :].rearrange("p (t a) -> p t a", a=1).to_broadcast([P, TPS, E0]),
                                        ALU.is_equal).then_inc(sem["a_onehot"], 1)
            if t == 0 and lagged(it, s, 12):
                bb, q = b - 3, 1 - par
                valid, rank, off, inside, total, gprob = (g[:, i, :] for i in range(6))
                dve.wait_ge(sem["a_rank_ps"], bb + 1)
                nc.vector.tensor_tensor(ranked[:, :, :], p_g[:, 64:128].rearrange("p (t e) -> p t e", t=TPS),
                                        onehot[:, :, :], ALU.mult).then_inc(sem["a_ranked"], 1)
                nc.vector.tensor_reduce(batch_n[:, :], onehot[:, :, :].rearrange("p t e -> p e t"), AX, ALU.add)\
                    .then_inc(sem["a_batch_n"], 1)
                dve.wait_ge(sem["a_gate_exp"], bb + 1)
                nc.vector.tensor_reduce(total, lexp[:, :, :], AX, ALU.add).then_inc(sem["a_total"], 1)
                dve.wait_ge(sem["a_ranked"], bb + 1)
                nc.vector.tensor_reduce(rank, ranked[:, :, :], AX, ALU.add).then_inc(sem["a_rank"], 1)
                dve.wait_ge(sem["a_batch_n"], bb + 1)
                nc.vector.tensor_tensor(seen[:, :], seen[:, :], batch_n[:, :], ALU.add)
                dve.wait_ge(sem["a_total"], bb + 1)
                nc.vector.reciprocal(gprob, total).then_inc(sem["a_gprob"], 1)
                dve.wait_ge(sem["a_rank"], bb + 1)
                nc.vector.tensor_scalar(valid, rank, float(CAP), None, ALU.is_lt).then_inc(sem["a_valid"], 1)
                nc.vector.scalar_tensor_tensor(off, rmx[:, :], -float(CAP), rank, ALU.mult, ALU.add)\
                    .then_inc(sem["a_valid"], 1)
                dve.wait_ge(sem["a_valid"], 2 * (bb + 1))
                nc.vector.tensor_tensor(inside, off, valid, ALU.mult).then_inc(sem["a_inside"], 1)
                if not isinstance(it, int) or bb >= 2:
                    dve.wait_ge(sem[f"a_scatter_out{q}"], 64 * (it - 1 if q == 0 else it - 2))
                    dve.wait_ge(sem[f"a_meta_out{q}"], 32 * (it - 1 if q == 0 else it - 2))
                    nc.vector.tensor_scalar(y[q][:, :, C], y[q][:, :, C], float(2 * SEQ), None, ALU.add)
                dve.wait_ge(sem["a_gprob"], bb + 1)
                nc.vector.tensor_tensor(gweight[q][:, :], gprob, valid, ALU.mult)
                dve.wait_ge(sem["a_inside"], bb + 1)
                nc.vector.tensor_scalar(slot[q][:, :], inside, float(SLOTS), None, ALU.add).then_inc(sem["a_slot"], 1)
            if lagged(it, s, 0):
                dve.wait_ge(sem["a_exp"], n + 1)
                nc.vector.tensor_reduce(sm[s % 2][:, :], prob[t][:, :, :], AX, ALU.add).then_inc(sem["a_sum"], 1)
            if lagged(it, s, 3):
                u, q = (s - 3) % TPS, ((s - 3) // TPS) % 2
                dve.wait_ge(sem["a_res"], n - 2)
                nc.vector.bn_stats(st[q][:, u, :], res[q][:, u, :]).then_inc(sem["a_bn"], 1)
            if lagged(it, s, 3):
                u, q = (s - 3) % TPS, ((s - 3) // TPS) % 2
                wait_apart(dve, sem["a_bn"], n - 2)
                nc.vector.bn_aggr(mv[q][:, u, :], st[q][:, u, :]).then_inc(sem["a_var"], 1)
            if lagged(it, s, 0):
                wait(dve, sem["a_norm"], n - 3)
                dve.wait_ge(sem["a_sum"], n + 1)
                nc.vector.reciprocal(rinv[t][:, :], sm[s % 2][:, :]).then_inc(sem["a_rinv"], 1)
            if t == 3 and lagged(it, s, 7):
                q, bb = 1 - par, b - 1
                var, guess, half, square, rstd = mv[q][:, :, 1], ln[q][:, 1, :], ln[q][:, 2, :], ln[q][:, 3, :], ln[q][:, 5, :]
                shift = ln[q][:, 4, :]
                dve.wait_ge(sem["a_guess"], bb + 1)
                nc.vector.scalar_tensor_tensor(half, var, EPS, guess, ALU.add, ALU.mult).then_inc(sem["a_newton"], 1)
                dve.wait_ge(sem["a_newton"], 3 * bb + 1)
                nc.vector.tensor_tensor(square, half, guess, ALU.mult).then_inc(sem["a_newton"], 1)
                dve.wait_ge(sem["a_newton"], 3 * bb + 2)
                nc.vector.tensor_scalar(half, square, -0.5, 1.5, ALU.mult, ALU.add).then_inc(sem["a_newton"], 1)
                dve.wait_ge(sem["a_newton"], 3 * bb + 3)
                nc.vector.tensor_tensor(rstd, half, guess, ALU.mult).then_inc(sem["a_rstd"], 1)
                dve.wait_ge(sem["a_rstd"], bb + 1)
                nc.vector.scalar_tensor_tensor(shift, mv[q][:, :, 0], -1.0, rstd, ALU.mult, ALU.mult)\
                    .then_inc(sem["a_shift"], 1)
        steps(dve, body, 3, 15)

    @block.gpsimd
    def _(pool):
        for t in range(TPS):
            nc.gpsimd.memset(vexp[t][:, :, :, :], 0.0)
        nc.gpsimd.memset(zeros[:, :], 0.0)
        nc.gpsimd.memset(kexp[1][:, :, :], 0.0).then_inc(sem["a_zero_pool"], 1)
        pool.wait_ge(sem["a_zero_pool"], 1)
        slots_flat = dram["slots"].rearrange("(n p r) c -> n p (r c)", p=P, r=10)
        moe_flat = dram["moe"].rearrange("(n p r) c -> n p (r c)", p=P, r=8)
        pool.wait_ge(sem["a_const_in"], 16 * 7)

        def body(it, s):
            t, par = s % TPS, (s // TPS) % 2
            n = UNROLL * it + s
            b = 2 * it + par
            if lagged(it, s, 0):
                pool.wait_ge(sem["a_rinv"], n + 1)
                e = prob[t][:, :, :]
                nc.gpsimd.tensor_tensor(e, e, rinv[t][:, :].rearrange("p (h a) -> p h a", a=1)
                                        .to_broadcast([P, H0, WIN]), ALU.mult).then_inc(sem["a_norm"], 1)
            if isinstance(it, int) and it == 0:
                nc.gpsimd.dma_start(slots_flat[s], zeros[:, :]).then_inc(sem["slots_zeroed"], 16)
            if isinstance(it, int) and it == 1:
                nc.gpsimd.dma_start(moe_flat[s], zeros[:, 0:8 * C]).then_inc(sem["moe_zeroed"], 16)
            if t == 0 and lagged(it, s, 0):
                wait(pool, sem[f"a_x_in{par}"], 16 * (it + par))
                nc.gpsimd.tensor_tensor(x[par][:, :, :], x[par][:, :, :],
                                        bproj[:, :].rearrange("p (a c) -> p a c", a=1).to_broadcast([P, TPS, C]),
                                        ALU.add).then_inc(sem["a_xb"], 1)
            for due, which in ((1, (0, 1)), (2, (2, 3))):
                if t == due and lagged(it, s, 12 + due):
                    bb, q = b - 3, 1 - par
                    if due == 1:
                        pool.wait_ge(sem["a_slot"], bb + 1)
                        wait_apart(pool, sem["a_y"], TPS * (bb + 1))
                        if isinstance(it, int) and bb == 0:
                            pool.wait_ge(sem["slots_zeroed"], 16 * UNROLL)
                    for u in which:
                        pool.indirect_dma_start(dram["slots"], bass.IndirectOffsetOnAxis(slot[q][:, u:u + 1], 0),
                                                y[q][:, u, :], None, bounds_check=SLOTS - 1, oob_is_err=False)\
                            .then_inc(sem[f"a_scatter_out{q}"], 16)
        steps(pool, body, 3, 15)
        pool.wait_ge(sem["moe_zeroed"], 16 * UNROLL)
        for q in range(2):
            pool.wait_ge(sem[f"a_scatter_out{q}"], 64 * NSEQ // 2)


def phase_experts0(nc, dram, const, sem, ctx):
    def sb(name, shape, dt=F32):
        return ctx.enter_context(nc.sbuf_tensor("b_" + name, shape, dt))

    def ps(name):
        return ctx.enter_context(nc.psum_tensor("b_ps_" + name, [P, 512], F32))

    FC = F0 // P
    HALF = CAP // 2
    ident = const["ident"]
    xs = [sb(f"xs{i}", [P, NCAP, ROW0]) for i in range(2)]
    w1 = [sb(f"w1{i}", [P, F0]) for i in range(2)]
    w2 = [sb(f"w2{i}", [P, FC, C]) for i in range(2)]
    xsT = [sb(f"xsT{i}", [P, CAP]) for i in range(2)]
    hT = [sb(f"hT{i}", [P, FC, CAP]) for i in range(2)]
    ys = [sb(f"ys{i}", [P, NCAP, C]) for i in range(2)]
    token = [sb(f"token{i}", [P, NCAP], U32) for i in range(2)]
    p_x = [ps("x0"), ps("x1")]
    p_h = [ps(f"h{i}") for i in range(4)]
    p_y = [ps("y0"), ps("y1")]
    slots = dram["slots"].rearrange("(e t p) c -> e p t c", p=P, t=NCAP)
    w2_rows = dram["w2_0"].rearrange("e (k p) c -> e p k c", p=P)
    units = [(k, half) for k in range(FC) for half in range(2)]
    NU = len(units)
    block = ctx.enter_context(nc.Block())

    def turns(eng, body):
        for par in range(2):
            body(0, par, par == 0, False)
        with eng.Fori(1, E0 // 2 - 1) as it:
            for par in range(2):
                body(it, par, False, False)
        for par in range(2):
            body(E0 // 2 - 1, par, False, par == 1)

    @block.sync
    def _(sp):
        def load(e, par):
            sp.dma_start(xs[par][:, :, :], slots[e]).then_inc(sem[f"b_xs_in{par}"], 16)
            sp.dma_start(w1[par][:, :], dram["w1_0"][e]).then_inc(sem[f"b_w1_in{par}"], 16)
            sp.dma_start(w2[par][:, :, :], w2_rows[e]).then_inc(sem[f"b_w2_in{par}"], 16)

        load(0, 0)

        def body(it, par, first, last):
            e = 2 * it + par
            if not last:
                wait(sp, sem["b_y_ps"], e)
                wait(sp, sem["b_token"], e)
                load(e + 1, 1 - par)
        turns(sp, body)

    @block.gpsimd
    def _(pool):
        def body(it, par, first, last):
            e = 2 * it + par
            pool.wait_ge(sem["b_token"], e + 1)
            wait_apart(pool, sem["b_ys_sb"], 2 * e + 2)
            for t in range(NCAP):
                pool.indirect_dma_start(dram["moe"], bass.IndirectOffsetOnAxis(token[par][:, t:t + 1], 0),
                                        ys[par][:, t, :], None, bounds_check=NT * P - 1, oob_is_err=False)\
                    .then_inc(sem[f"b_ys_out{par}"], 16)
        turns(pool, body)
        for par in range(2):
            pool.wait_ge(sem[f"b_ys_out{par}"], 16 * NCAP * E0 // 2)

    @block.tensor
    def _(pe):
        def turn_rows(e, par, rounds):
            pe.wait_ge(sem[f"b_xs_in{par}"], 16 * rounds)
            wait(pe, sem["b_xsT_sb"], 2 * e)
            for t in range(NCAP):
                last = nc.tensor.transpose(p_x[t // 4][:, P * (t % 4):P * (t % 4) + P], xs[par][:, t, 0:C], ident[:, :])
                if t in (3, NCAP - 1):
                    last.then_inc(sem["b_xsT_ps"], 1)

        turn_rows(0, 0, 1)

        def body(it, par, first, last):
            e = 2 * it + par
            pe.wait_ge(sem["b_xsT_sb"], 2 * e + 2)
            pe.wait_ge(sem[f"b_w1_in{par}"], 16 * (it + 1))
            for u, (k, half) in enumerate(units):
                wait(pe, sem["b_gelu"], NU * e + u - 3)
                nc.tensor.matmul(p_h[u % 4][:, 0:HALF], w1[par][:, P * k:P * k + P],
                                 xsT[par][:, HALF * half:HALF * half + HALF], start=True, stop=True)\
                    .then_inc(sem["b_h_ps"], 1)
            if not last:
                turn_rows(e + 1, 1 - par, it + 1 + par)
            pe.wait_ge(sem[f"b_w2_in{par}"], 16 * (it + 1))
            pe.wait_ge(sem["b_gelu"], NU * (e + 1))
            wait(pe, sem["b_ys_sb"], 2 * e)
            for t in range(NCAP):
                for k in range(FC):
                    m = nc.tensor.matmul(p_y[t // 4][:, P * (t % 4):P * (t % 4) + P], hT[par][:, k, P * t:P * t + P],
                                         w2[par][:, k, :], start=(k == 0), stop=(k == FC - 1), skip_group_check=True)
            m.then_inc(sem["b_y_ps"], 1)
        turns(pe, body)

    @block.scalar
    def _(act):
        def body(it, par, first, last):
            e = 2 * it + par
            wait(act, sem["b_y_ps"], e - 1)
            for u, (k, half) in enumerate(units):
                act.wait_ge(sem["b_h_ps"], NU * e + u + 1)
                nc.scalar.activation(hT[par][:, k, HALF * half:HALF * half + HALF], p_h[u % 4][:, 0:HALF],
                                     ACT.Gelu_apprx_tanh).then_inc(sem["b_gelu"], 1)
        turns(act, body)

    @block.vector
    def _(dve):
        def xsT_out(e, par):
            wait(dve, sem["b_h_ps"], NU * (e - 1))
            dve.wait_ge(sem["b_xsT_ps"], 2 * e + 1)
            nc.vector.tensor_copy(xsT[par][:, 0:512], p_x[0][:, :]).then_inc(sem["b_xsT_sb"], 1)
            dve.wait_ge(sem["b_xsT_ps"], 2 * e + 2)
            nc.vector.tensor_copy(xsT[par][:, 512:CAP], p_x[1][:, 0:CAP - 512]).then_inc(sem["b_xsT_sb"], 1)

        xsT_out(0, 0)

        def body(it, par, first, last):
            e = 2 * it + par
            if not last:
                xsT_out(e + 1, 1 - par)
            wait(dve, sem[f"b_ys_out{par}"], 16 * NCAP * it)
            dve.wait_ge(sem[f"b_xs_in{par}"], 16 * (it + 1))
            nc.vector.tensor_scalar(token[par][:, :], xs[par][:, :, C], float(NT * P), None, ALU.add)\
                .then_inc(sem["b_token"], 1)
            dve.wait_ge(sem["b_y_ps"], e + 1)
            nc.vector.tensor_copy(ys[par][:, 0:4, :].rearrange("p t c -> p (t c)"), p_y[0][:, :]).then_inc(sem["b_ys_sb"], 1)
            nc.vector.tensor_copy(ys[par][:, 4, :], p_y[1][:, 0:C]).then_inc(sem["b_ys_sb"], 1)
        turns(dve, body)


def phase_attention1(nc, dram, const, sem, ctx):
    def sb(name, shape, dt=F32):
        return ctx.enter_context(nc.sbuf_tensor("c_" + name, shape, dt))

    def ps(name):
        return ctx.enter_context(nc.psum_tensor("c_ps_" + name, [P, 512], F32))

    ident, eps = const["ident"], const["eps"]
    packed = sb("packed", [P, sum(n for _, n in PACKED1)])
    parts, at0 = {}, 0
    for name, n in PACKED1:
        parts[name] = packed[:, at0:at0 + n]
        at0 += n
    wqk, wv, causal_f, tri_f, gate_w = (parts[n] for n in ("wqk1", "wv1", "causal", "before", "gate1T"))
    bias, rev, base = (parts[n].rearrange("p (t e) -> p t e", e=E1) for n in ("balance", "rev1", "region1"))
    token_of = parts["token_of"].rearrange("p (q t) -> p q t", q=2)
    causal16, ident16 = sb("causal16", [P, P], BF16), sb("ident16", [P, P], BF16)
    x1 = [sb(f"x1{i}", [P, TPS, C]) for i in range(2)]
    weight = [sb(f"weight{i}", [P, TPS]) for i in range(2)]
    moe = [sb(f"moe{i}", [P, TPS, C]) for i in range(2)]
    res1 = sb("res1", [P, TPS, C])
    x2 = [sb(f"x2{i}", [P, TPS, C]) for i in range(2)]
    x2T = sb("x2T", [P, SEQ])
    qT = [sb(f"qT{i}", [DQ, SEQ]) for i in range(2)]
    kT = [sb(f"kT{i}", [DQ, SEQ]) for i in range(2)]
    v = [sb(f"v{i}", [P, TPS, C]) for i in range(2)]
    prob = [sb(f"prob{i}", [P, SEQ]) for i in range(TPS)]
    probT = [sb(f"probT{i}", [P, TPS, P]) for i in range(2)]
    nmx = [sb(f"nmx{i}", [P, 1]) for i in range(2)]
    sm = [sb(f"sm{i}", [P, 1]) for i in range(TPS)]
    rinv = [sb(f"rinv{i}", [P, 1]) for i in range(2)]
    res2 = [sb(f"res2{i}", [P, TPS, C]) for i in range(2)]
    x3 = [sb(f"x3{i}", [P, TPS, ROW1]) for i in range(2)]
    st = [sb(f"st{i}", [P, TPS, 6]) for i in range(2)]
    mv = [sb(f"mv{i}", [P, TPS, 2]) for i in range(2)]
    ln = [sb(f"ln{i}", [P, 6, TPS]) for i in range(2)]
    p_x, p_qk, p_v, p_o = (ps(n) for n in ("x", "qk", "v", "o"))
    p_s = [ps(f"s{i}") for i in range(2)]
    p_pt, p_g = ps("pt"), ps("g")
    tri16, ones16 = sb("tri16", [P, P], BF16), sb("ones16", [P, P], BF16)
    zeros = sb("zeros", [P, 2 * ROW1])
    x3T = sb("x3T", [P, SEQ])
    z, ez, e1p, score, hit, score2, hit2, at, at1, at2 = (sb(f"gate{i}", [P, TPS, E1]) for i in range(10))
    hot1, hot2, hot = (sb(n, [P, TPS, E1], BF16) for n in ("hot1", "hot2", "hot"))
    seen, batch_n = const["seen"], sb("batch_n", [P, E1])
    top = sb("top", [P, 2, TPS])
    who = sb("who", [P, 2, TPS])
    total = sb("total", [P, 2, TPS])
    place = [sb(f"place{i}", [P, 2, TPS], U32) for i in range(2)]
    x1_rows = dram["x1"].rearrange("(b t p) c -> b p t c", p=P, t=TPS)
    moe_rows = dram["moe"].rearrange("(b t p) c -> b p t c", p=P, t=TPS)
    block = ctx.enter_context(nc.Block())

    def rows_of(eng, body):
        for it in (-1, 0, 1, 2):
            for s in range(UNROLL):
                body(it, s)
        with eng.Fori(3, NT // UNROLL - 1) as it:
            for s in range(UNROLL):
                body(it, s)
        for s in range(UNROLL + 13):
            body(NT // UNROLL - 1 + s // UNROLL, s % UNROLL)

    @block.sync
    def _(sp):
        def load(b, par):
            sp.dma_start(weight[par][:, :], dram["weight_of"][b]).then_inc(sem[f"c_x1_in{par}"], 16)
            sp.dma_start(x1[par][:, :, :], x1_rows[b]).then_inc(sem[f"c_x1_in{par}"], 16)
            sp.dma_start(moe[par][:, :, :], moe_rows[b]).then_inc(sem[f"c_x1_in{par}"], 16)

        load(0, 0)
        load(1, 1)
        sp.wait_ge(sem["c_zero"], 1)
        spare = dram["xs1"].rearrange("(k t p) c -> k p t c", p=P, t=2)

        def body(it, s):
            t, par = s % TPS, (s // TPS) % 2
            b = 2 * it + par
            if isinstance(it, int) and it == 0:
                sp.dma_start(spare[E1 * REGION1 + s], zeros[:, :].rearrange("p (t c) -> p t c", t=2)).then_inc(sem["c_spare"], 16)
            if t == 0 and lagged(it, s, -8) and not (isinstance(it, int) and it == -1):
                sp.wait_ge(sem["c_res1"], TPS * (b + 1))
                load(b + 2, par)
        rows_of(sp, body)
        sp.wait_ge(sem["c_spare"], 16 * SPARE1)

    @block.gpsimd
    def _(pool):
        def body(it, s):
            t, par = s % TPS, (s // TPS) % 2
            b = 2 * it + par
            if t == 0 and lagged(it, s, 12):
                bb, q = b - 3, 1 - par
                wait_apart(pool, sem["c_place"], bb + 1)
                for k in range(2):
                    for u in range(TPS):
                        pool.indirect_dma_start(dram["xs1"], bass.IndirectOffsetOnAxis(place[q][:, k, u:u + 1], 0),
                                                x3[q][:, u, :], None).then_inc(sem[f"c_scatter_out{q}"], 16)
        rows_of(pool, body)
        for q in range(2):
            pool.wait_ge(sem[f"c_scatter_out{q}"], 128 * NSEQ // 2)

    @block.tensor
    def _(pe):
        pe.wait_ge(sem["c_const_in"], 16)
        pe.wait_ge(sem["c_setup"], 5)

        def body(it, s):
            t, par = s % TPS, (s // TPS) % 2
            n = UNROLL * it + s
            b = 2 * it + par
            if lagged(it, s, 2):
                u = (s - 2) % TPS
                pe.wait_ge(sem["c_exp"], n - 1)
                wait(pe, sem["c_pt_sb"], n - 2)
                for c in range(u + 1):
                    last = nc.tensor.transpose(p_pt[:, P * c:P * c + P], prob[u][:, P * c:P * c + P], ident[:, :])
                last.then_inc(sem["c_pt_ps"], 1)
            def times_values(when):
                if lagged(it, s, 2) and t in when:
                    u, q = (s - 2) % TPS, ((s - 2) // TPS) % 2
                    pe.wait_ge(sem["c_pt_sb"], n - 1)
                    pe.wait_ge(sem["c_v_sb"], (b if t >= 2 else b - 1) + 1)
                    wait(pe, sem["c_res2"], n - 2)
                    for c in range(u + 1):
                        last = nc.tensor.matmul(p_o[:, 0:C], probT[s % 2][:, c, :], v[q][:, c, :],
                                                start=(c == 0), stop=(c == u))
                    last.then_inc(sem["c_o_ps"], 1)

            times_values((0,))
            if lagged(it, s, 0):
                if t == 0:
                    pe.wait_ge(sem["c_k_sb"], b + 1)
                wait(pe, sem["c_exp"], n - 1)
                nc.tensor.matmul(p_s[s % 2][:, 0:P * (t + 1)], qT[par][:, P * t:P * t + P], kT[par][:, 0:P * (t + 1)],
                                 start=True, stop=False, skip_group_check=True)
                nc.tensor.matmul(p_s[s % 2][:, P * t:P * t + P], ident16[:, :], causal16[:, :], start=False, stop=True,
                                 skip_group_check=True).then_inc(sem["c_s_ps"], 1)
            if t == 1 and lagged(it, s, 9):
                bb = b - 2
                pe.wait_ge(sem["c_x3T_sb"], bb + 1)
                for u in range(TPS):
                    last = nc.tensor.matmul(p_g[:, E1 * u:E1 * u + E1], x3T[:, P * u:P * u + P], gate_w[:, :],
                                            start=(u == 0), stop=(u == TPS - 1), skip_group_check=True)
                last.then_inc(sem["c_logit_ps"], 1)
            times_values((1, 2, 3))
            if t == 3 and lagged(it, s, 11):
                bb = b - 2
                pe.wait_ge(sem["c_hot"], bb + 1)
                out = p_g[:, 64:64 + TPS * E1]
                nc.tensor.matmul(out, ones16[:, :], seen[:, :].rearrange("p (a e) -> p a e", a=1).to_broadcast([P, TPS, E1]),
                                 start=True, stop=False, skip_group_check=True)
                nc.tensor.matmul(out, tri16[:, :], hot[:, :, :], start=False, stop=False, skip_group_check=True)
                for u in range(TPS - 1):
                    last = nc.tensor.matmul(out[:, E1 * (u + 1):TPS * E1], ones16[:, :],
                                            hot[:, u:u + 1, :].to_broadcast([P, TPS - 1 - u, E1]),
                                            start=False, stop=(u == TPS - 2), skip_group_check=True)
                last.then_inc(sem["c_rank_ps"], 1)
            if t == 0 and lagged(it, s, 8):
                bb, q = b - 2, par
                pe.wait_ge(sem["c_x3"], TPS * (bb + 1))
                wait(pe, sem["c_at"], bb)
                for u in range(TPS):
                    last = nc.tensor.transpose(p_g[:, P * u:P * u + P], x3[q][:, u, 0:C], ident[:, :])
                last.then_inc(sem["c_x3T_ps"], 1)
            if t == 2 and lagged(it, s, -2):
                pe.wait_ge(sem["c_x2"], TPS * (b + 2))
                wait(pe, sem["c_x2T_sb"], b + 1)
                for u in range(TPS):
                    last = nc.tensor.transpose(p_x[:, P * u:P * u + P], x2[1 - par][:, u, :], ident[:, :])
                last.then_inc(sem["c_x2T_ps"], 1)
            if t == 3 and lagged(it, s, -1):
                pe.wait_ge(sem["c_x2T_sb"], b + 2)
                wait(pe, sem["c_k_sb"], b + 1)
                nc.tensor.matmul(p_qk[:, :], wqk[:, :], x2T[:, :], start=True, stop=True).then_inc(sem["c_qk_ps"], 1)
                wait(pe, sem["c_v_sb"], b + 1)
                for u in range(TPS):
                    last = nc.tensor.matmul(p_v[:, P * u:P * u + P], x2T[:, P * u:P * u + P], wv[:, :],
                                            start=True, stop=True, skip_group_check=True)
                last.then_inc(sem["c_v_ps"], 1)
        rows_of(pe, body)

    @block.scalar
    def _(act):
        nc.scalar.dma_start(packed[:, :], dram["packed1"]).then_inc(sem["c_const_in"], 16)
        nc.scalar.preload_act_table_set("natural_log_exp_and_others")

        def guess(k, count):
            act.wait_ge(sem[f"c_var{k + 1}"], TPS * count)
            nc.scalar.activation(ln[k][:, 0, :], mv[k][:, :, 1], ACT.Ln, bias=eps[:, 0:1]).then_inc(sem[f"c_ln{k + 1}"], 1)
            act.wait_ge(sem[f"c_ln{k + 1}"], count)
            nc.scalar.activation(ln[k][:, 1, :], ln[k][:, 0, :], ACT.Exp, scale=-0.5).then_inc(sem[f"c_guess{k + 1}"], 1)

        def second_norm(q, tiles):
            for u in tiles:
                nc.scalar.activation(x3[q][:, u, 0:C], res2[q][:, u, :], ACT.Identity, bias=ln[1][:, 5, u:u + 1],
                                     scale=ln[1][:, 4, u:u + 1]).then_inc(sem["c_x3"], 1)

        def body(it, s):
            t, par = s % TPS, (s // TPS) % 2
            n = UNROLL * it + s
            b = 2 * it + par
            if lagged(it, s, 2):
                u = (s - 2) % TPS
                act.wait_ge(sem["c_pt_ps"], n - 1)
                wait(act, sem["c_o_ps"], n - 3)
                nc.scalar.copy(probT[s % 2][:, 0:u + 1, :].rearrange("p a b -> p (a b)"), p_pt[:, 0:P * (u + 1)])\
                    .then_inc(sem["c_pt_sb"], 1)
            if t == 1 and lagged(it, s, -3):
                guess(0, b + 2)
            if t == 0 and lagged(it, s, 0):
                act.wait_ge(sem["c_qk_ps"], b + 1)
                wait(act, sem["c_s_ps"], TPS * (b - 1))
                nc.scalar.activation(qT[par][:, :], p_qk[0:DQ, :], ACT.Identity, scale=float(DQ) ** -0.5)\
                    .then_inc(sem["c_q_sb"], 1)
                nc.scalar.copy(kT[par][:, :], p_qk[DQ:P, :]).then_inc(sem["c_k_sb"], 1)
            if t == 0 and lagged(it, s, 8):
                second_norm(par, (2, 3))
            if t == 2 and lagged(it, s, -2):
                act.wait_ge(sem["c_shift1"], b + 2)
                wait(act, sem["c_x2T_ps"], b)
                wait(act, sem["c_res2"], TPS * b)
                for u in range(TPS):
                    nc.scalar.activation(x2[1 - par][:, u, :], res1[:, u, :], ACT.Identity, bias=ln[0][:, 5, u:u + 1],
                                         scale=ln[0][:, 4, u:u + 1]).then_inc(sem["c_x2"], 1)
            if t == 2 and lagged(it, s, 6):
                guess(1, b)
            if lagged(it, s, 0):
                act.wait_ge(sem["c_nmax"], n + 1)
                wait(act, sem["c_pt_ps"], n - 3)
                wait(act, sem["c_rinv"], n - 3)
                nc.scalar.activation(prob[t][:, 0:P * (t + 1)], p_s[s % 2][:, 0:P * (t + 1)], ACT.Exp,
                                     bias=nmx[s % 2][:, 0:1], accum_out=sm[t][:, 0:1]).then_inc(sem["c_exp"], 1)
            if t == 1 and lagged(it, s, 9):
                bb = b - 2
                act.wait_ge(sem["c_z"], bb + 1)
                wait(act, sem["c_e1p"], bb)
                nc.scalar.activation(ez[:, :, :], z[:, :, :], ACT.Exp, scale=-1.0).then_inc(sem["c_ez"], 1)
            if t == 3 and lagged(it, s, 7):
                bb, q = b - 1, 1 - par
                act.wait_ge(sem["c_shift2"], bb + 1)
                if not isinstance(it, int) or bb >= 2:
                    act.wait_ge(sem[f"c_scatter_out{q}"], 128 * (it if q == 0 else it - 1))
                    act.wait_ge(sem["c_x3T_ps"], bb - 1)
                second_norm(q, (0, 1))
            if t == 0 and lagged(it, s, 8):
                bb = b - 2
                act.wait_ge(sem["c_x3T_ps"], bb + 1)
                wait(act, sem["c_logit_ps"], bb)
                nc.scalar.copy(x3T[:, :], p_g[:, :]).then_inc(sem["c_x3T_sb"], 1)
            if t == 0 and lagged(it, s, 0):
                act.wait_ge(sem["c_v_ps"], b + 1)
                wait(act, sem["c_o_ps"], TPS * (b - 1))
                nc.scalar.copy(v[par][:, :, :].rearrange("p t c -> p (t c)"), p_v[:, :]).then_inc(sem["c_v_sb"], 1)
            if t == 2 and lagged(it, s, -2):
                act.wait_ge(sem["c_x2T_ps"], b + 2)
                wait(act, sem["c_v_ps"], b + 1)
                nc.scalar.copy(x2T[:, :], p_x[:, :]).then_inc(sem["c_x2T_sb"], 1)
        rows_of(act, body)

    @block.vector
    def _(dve):
        nc.vector.memset(zeros[:, :], 0.0).then_inc(sem["c_zero"], 1)
        nc.vector.memset(seen[:, :], 0.0)
        nc.vector.memset(ones16[:, :], 1.0).then_inc(sem["c_setup"], 1)
        dve.wait_ge(sem["c_const_in"], 16)
        nc.vector.tensor_copy(tri16[:, :], tri_f[:, :]).then_inc(sem["c_setup"], 1)
        nc.vector.tensor_copy(causal16[:, :], causal_f[:, :]).then_inc(sem["c_setup"], 1)
        nc.vector.tensor_copy(ident16[:, :], ident[:, :]).then_inc(sem["c_setup"], 1)
        for q in range(2):
            last = nc.vector.tensor_scalar(x3[q][:, :, C], token_of[:, q, :], -2.0 * NT * P, None, ALU.add)
        last.then_inc(sem["c_setup"], 1)

        def newton(k, count, i):
            mean, var = mv[k][:, :, 0], mv[k][:, :, 1]
            _, first, half, square, rstd, shift = (ln[k][:, r, :] for r in range(6))
            done = sem[f"c_newton{k + 1}"]
            if i == 0:
                dve.wait_ge(sem[f"c_guess{k + 1}"], count + 1)
                nc.vector.scalar_tensor_tensor(half, var, EPS, first, ALU.add, ALU.mult).then_inc(done, 1)
            if i == 1:
                dve.wait_ge(done, 4 * count + 1)
                nc.vector.tensor_tensor(square, half, first, ALU.mult).then_inc(done, 1)
            if i == 2:
                dve.wait_ge(done, 4 * count + 2)
                nc.vector.tensor_scalar(half, square, -0.5, 1.5, ALU.mult, ALU.add).then_inc(done, 1)
            if i == 3:
                dve.wait_ge(done, 4 * count + 3)
                nc.vector.tensor_tensor(rstd, half, first, ALU.mult).then_inc(done, 1)
            if i == 4:
                dve.wait_ge(done, 4 * count + 4)
                nc.vector.scalar_tensor_tensor(shift, mean, -1.0, rstd, ALU.mult, ALU.mult)\
                    .then_inc(sem[f"c_shift{k + 1}"], 1)

        def spread(a):
            return a.rearrange("p (t a) -> p t a", a=1).to_broadcast([P, TPS, E1])

        def body(it, s):
            t, par = s % TPS, (s // TPS) % 2
            n = UNROLL * it + s
            b = 2 * it + par
            ln1 = t == 1 and lagged(it, s, -3)
            ln2 = t == 2 and lagged(it, s, 6)
            gate1, gate2, gate3 = (t == k and lagged(it, s, 8 + k) for k in (1, 2, 3))

            def between(i):
                if ln1:
                    newton(0, b + 1, i)
                if ln2:
                    newton(1, b - 1, i)

            def highest(when):
                if t in when and lagged(it, s, 0):
                    dve.wait_ge(sem["c_s_ps"], n + 1)
                    wait(dve, sem["c_exp"], n - 1)
                    nc.vector.tensor_reduce(nmx[s % 2][:, :], p_s[s % 2][:, 0:P * (t + 1)], AX, ALU.max, negate=True)\
                        .then_inc(sem["c_nmax"], 1)

            if lagged(it, s, 1):
                dve.wait_ge(sem["c_exp"], n)
                nc.vector.reciprocal(rinv[(s - 1) % 2][:, :], sm[(s - 1) % TPS][:, :]).then_inc(sem["c_rinv"], 1)
            highest((1, 2, 3))
            if gate2:
                dve.wait_ge(sem["c_ge1"], b - 1)
                nc.vector.tensor_tensor(hit2[:, :, :], hit[:, :, :], rev[:, :, :], ALU.mult).then_inc(sem["c_hit1"], 1)
            between(0)
            if gate2:
                dve.wait_ge(sem["c_hit1"], b - 1)
                nc.vector.tensor_reduce(who[:, 0, :], hit2[:, :, :], AX, ALU.max).then_inc(sem["c_who1"], 1)
            if gate1:
                dve.wait_ge(sem["c_logit_ps"], b - 1)
                wait(dve, sem["c_ez"], b - 2)
                nc.vector.tensor_tensor(z[:, :, :], p_g[:, 0:TPS * E1].rearrange("p (t e) -> p t e", t=TPS), bias[:, :, :],
                                        ALU.add).then_inc(sem["c_z"], 1)
            if t == 0 and lagged(it, s, -4):
                q = 1 - par
                dve.wait_ge(sem[f"c_x1_in{q}"], 48 * (it + 1 + par))
                wait(dve, sem["c_x2"], TPS * (b + 1))
                for u in range(TPS):
                    nc.vector.scalar_tensor_tensor(res1[:, u, :], moe[q][:, u, :], weight[q][:, u:u + 1], x1[q][:, u, :],
                                                   ALU.mult, ALU.add).then_inc(sem["c_res1"], 1)
            between(1)
            if gate2:
                dve.wait_ge(sem["c_who1"], b - 1)
                nc.vector.tensor_tensor(hot1[:, :, :], rev[:, :, :], spread(who[:, 0, :]), ALU.is_equal).then_inc(sem["c_hot1"], 1)
            between(2)
            if gate2:
                dve.wait_ge(sem["c_hot1"], b - 1)
                nc.vector.scalar_tensor_tensor(score2[:, :, :], hot1[:, :, :], -2.0, score[:, :, :], ALU.mult, ALU.add)\
                    .then_inc(sem["c_score2"], 1)
            between(3)
            highest((0,))
            if t == 0 and lagged(it, s, -4):
                dve.wait_ge(sem["c_res1"], TPS * (b + 2))
                for u in range(TPS):
                    nc.vector.bn_stats(st[0][:, u, :], res1[:, u, :]).then_inc(sem["c_bn1"], 1)
            between(4)
            if gate2:
                dve.wait_ge(sem["c_score2"], b - 1)
                nc.vector.tensor_reduce(top[:, 1, :], score2[:, :, :], AX, ALU.max).then_inc(sem["c_top2"], 1)
            if lagged(it, s, 2):
                u, q = (s - 2) % TPS, ((s - 2) // TPS) % 2
                bb = b if t >= 2 else b - 1
                dve.wait_ge(sem["c_o_ps"], n - 1)
                dve.wait_ge(sem["c_rinv"], n - 1)
                wait(dve, sem["c_x3"], TPS * (bb - 1))
                nc.vector.scalar_tensor_tensor(res2[q][:, u, :], p_o[:, 0:C], rinv[s % 2][:, 0:1], x2[q][:, u, :],
                                               ALU.mult, ALU.add).then_inc(sem["c_res2"], 1)
            if gate2:
                dve.wait_ge(sem["c_top2"], b - 1)
                nc.vector.tensor_tensor(hit[:, :, :], score2[:, :, :], spread(top[:, 1, :]), ALU.is_ge).then_inc(sem["c_ge2"], 1)
            if lagged(it, s, 2):
                dve.wait_ge(sem["c_res2"], n - 1)
                nc.vector.bn_stats(st[1][:, (s - 2) % TPS, :], res2[((s - 2) // TPS) % 2][:, (s - 2) % TPS, :]).then_inc(sem["c_bn2"], 1)
            if gate2:
                dve.wait_ge(sem["c_ge2"], b - 1)
                nc.vector.tensor_tensor(hit2[:, :, :], hit[:, :, :], rev[:, :, :], ALU.mult).then_inc(sem["c_hit2"], 1)
            if t == 0 and lagged(it, s, -4):
                wait_apart(dve, sem["c_bn1"], TPS * (b + 2))
                for u in range(TPS):
                    nc.vector.bn_aggr(mv[0][:, u, :], st[0][:, u, :]).then_inc(sem["c_var1"], 1)
            if lagged(it, s, 2):
                if ln2:
                    wait_apart(dve, sem["c_shift2"], b)
                wait_apart(dve, sem["c_bn2"], n - 1)
                u = (s - 2) % TPS
                nc.vector.bn_aggr(mv[1][:, u, :], st[1][:, u, :]).then_inc(sem["c_var2"], 1)
            if gate1:
                dve.wait_ge(sem["c_ez"], b - 1)
                nc.vector.tensor_scalar(e1p[:, :, :], ez[:, :, :], 1.0, None, ALU.add).then_inc(sem["c_e1p"], 1)
                dve.wait_ge(sem["c_e1p"], b - 1)
                nc.vector.reciprocal(score[:, :, :], e1p[:, :, :]).then_inc(sem["c_score"], 1)
                dve.wait_ge(sem["c_score"], b - 1)
                nc.vector.tensor_reduce(top[:, 0, :], score[:, :, :], AX, ALU.max).then_inc(sem["c_top1"], 1)
                dve.wait_ge(sem["c_top1"], b - 1)
                nc.vector.tensor_tensor(hit[:, :, :], score[:, :, :], spread(top[:, 0, :]), ALU.is_ge).then_inc(sem["c_ge1"], 1)
            if gate2:
                dve.wait_ge(sem["c_hit2"], b - 1)
                nc.vector.tensor_reduce(who[:, 1, :], hit2[:, :, :], AX, ALU.max).then_inc(sem["c_who2"], 1)
                dve.wait_ge(sem["c_who2"], b - 1)
                nc.vector.tensor_tensor(hot2[:, :, :], rev[:, :, :], spread(who[:, 1, :]), ALU.is_equal).then_inc(sem["c_hot2"], 1)
                dve.wait_ge(sem["c_hot2"], b - 1)
                wait(dve, sem["c_rank_ps"], b - 2)
                nc.vector.tensor_tensor(hot[:, :, :], hot1[:, :, :], hot2[:, :, :], ALU.add).then_inc(sem["c_hot"], 1)
            if gate3:
                bb, q = b - 2, par
                dve.wait_ge(sem["c_rank_ps"], bb + 1)
                nc.vector.tensor_tensor(at[:, :, :], p_g[:, 64:64 + TPS * E1].rearrange("p (t e) -> p t e", t=TPS),
                                        base[:, :, :], ALU.add).then_inc(sem["c_at"], 1)
                nc.vector.tensor_reduce(batch_n[:, :], hot[:, :, :].rearrange("p t e -> p e t"), AX, ALU.add)\
                    .then_inc(sem["c_batch_n"], 1)
                nc.vector.scalar_tensor_tensor(total[:, 0, :], top[:, 0, :], 1e-6, top[:, 1, :], ALU.add, ALU.add)\
                    .then_inc(sem["c_total"], 1)
                dve.wait_ge(sem["c_at"], bb + 1)
                nc.vector.tensor_tensor(at1[:, :, :], at[:, :, :], hot1[:, :, :], ALU.mult).then_inc(sem["c_at1"], 1)
                nc.vector.tensor_tensor(at2[:, :, :], at[:, :, :], hot2[:, :, :], ALU.mult).then_inc(sem["c_at2"], 1)
                dve.wait_ge(sem["c_batch_n"], bb + 1)
                nc.vector.tensor_tensor(seen[:, :], seen[:, :], batch_n[:, :], ALU.add).then_inc(sem["c_seen"], 1)
                dve.wait_ge(sem["c_total"], bb + 1)
                nc.vector.reciprocal(total[:, 1, :], total[:, 0, :]).then_inc(sem["c_rtotal"], 1)
                if not isinstance(it, int) or bb >= 2:
                    dve.wait_ge(sem[f"c_scatter_out{q}"], 128 * (it - 1))
                    nc.vector.tensor_scalar(x3[q][:, :, C], x3[q][:, :, C], float(2 * SEQ), None, ALU.add)
                nc.vector.tensor_copy(x3[q][:, :, C + 1], who[:, 0, :])
                with nc.allow_low_precision(reason="sums of one whole number and zeros, in float32 inside"):
                    dve.wait_ge(sem["c_at1"], bb + 1)
                    nc.vector.tensor_reduce(place[q][:, 0, :], at1[:, :, :], AX, ALU.add)
                    dve.wait_ge(sem["c_at2"], bb + 1)
                    nc.vector.tensor_reduce(place[q][:, 1, :], at2[:, :, :], AX, ALU.add)
                dve.wait_ge(sem["c_rtotal"], bb + 1)
                for k in range(2):
                    last = nc.vector.tensor_tensor(x3[q][:, :, C + 2 + k], top[:, k, :], total[:, 1, :], ALU.mult)
                last.then_inc(sem["c_place"], 1)
        rows_of(dve, body)


def phase_experts1(nc, dram, const, sem, ctx):
    def sb(name, shape, dt=F32):
        return ctx.enter_context(nc.sbuf_tensor("d_" + name, shape, dt))

    def ps(name):
        return ctx.enter_context(nc.psum_tensor("d_ps_" + name, [P, 512], F32))

    ident, seen = const["ident"], const["seen"]
    U, T, FC = 8, 2, F1 // P
    NB = REGION1 - 1
    ones16 = sb("ones16", [P, P], BF16)
    zeros = sb("zeros", [P, T, ROW1])
    starts, up_to = sb("starts", [P, E1, NB]), sb("up_to", [P, E1, E1])
    tile_number, base = sb("tile_number", [P, TILES1]), sb("base", [P, E1])
    count, full, blocks = sb("count", [P, E1]), sb("full", [P, E1, NB]), sb("blocks", [P, E1])
    part, cum = sb("part", [P, E1, E1]), sb("cum", [P, E1])
    ended, theirs = sb("ended", [P, TILES1, E1]), sb("theirs", [P, TILES1, E1])
    expert, first_of, local, place = (sb(n, [P, TILES1]) for n in ("expert", "first_of", "local", "place"))
    own = sb("own", [P, TILES1])
    tile_block, tile_expert = sb("tile_block", [1, TILES1]), sb("tile_expert", [1, TILES1])
    tile_code = sb("tile_code", [1, TILES1], U32)
    tails = sb("tails", [P, E1], U32)
    xs = [sb(f"xs{i}", [P, T, ROW1]) for i in range(U)]
    is_first, second, share0, share1, share = ([sb(f"{n}{i}", [P, T]) for i in range(U)]
                                               for n in ("is_first", "second", "share0", "share1", "share"))
    dest = [sb(f"dest{i}", [P, T], U32) for i in range(U)]
    w12 = [sb(f"w12{i}", [P, 2, F1]) for i in range(U)]
    xsT = [sb(f"xsT{i}", [P, BLK1]) for i in range(2)]
    hT = [sb(f"hT{i}", [P, FC, BLK1]) for i in range(2)]
    ys = [sb(f"ys{i}", [P, T, C]) for i in range(U)]
    p_x = [ps("x0"), ps("x1")]
    p_h = [ps(f"h{i}") for i in range(4)]
    p_y = [ps("y0"), ps("y1")]
    xs_blocks = dram["xs1"].rearrange("(k t p) c -> k p t c", p=P, t=T)
    NBLOCKS = E1 * REGION1 + SPARE1
    block = ctx.enter_context(nc.Block())

    def live(it, s, lag):
        return not isinstance(it, int) or 0 <= U * it + s - lag < TILES1

    def turns(eng, body):
        for it in (-1, 0, 1):
            for s in range(U):
                body(it, s)
        with eng.Fori(2, TILES1 // U - 1) as it:
            for s in range(U):
                body(it, s)
        for s in range(U + 3):
            body(TILES1 // U - 1 + s // U, s % U)

    def zero_tails(eng, experts):
        eng.wait_ge(sem["d_tails"], 1)
        for e in experts:
            row = eng.value_load(tails[0:1, e:e + 1], min_val=e * REGION1 * BLK1, max_val=(e + 1) * REGION1 * BLK1 - BLK1)
            eng.dma_start(dram["xs1"][bass.ds(row, BLK1), :].rearrange("(t p) c -> p t c", p=P), zeros[:, :, :])\
                .then_inc(sem["d_tails_out"], 16)

    @block.sync
    def _(sp):
        sp.dma_start(base[:, :], dram["region1"].rearrange("p (t e) -> p t e", e=E1)[:, 0, :], ).then_inc(sem["d_base_in"], 16)
        sp.dma_start(starts[:, :, :].rearrange("p a b -> p (a b)"), dram["block_starts"]).then_inc(sem["d_const_in"], 16)
        sp.dma_start(up_to[:, :, :].rearrange("p a b -> p (a b)"), dram["up_to"]).then_inc(sem["d_const_in"], 16)
        sp.dma_start(tile_number[:, :], dram["tile_number"]).then_inc(sem["d_const_in"], 16)
        zero_tails(sp, range(0, E1 // 2))
        sp.wait_ge(sem["d_tails_out"], 16 * E1)
        sp.wait_ge(sem["d_table"], 1)

        def body(it, s):
            n = U * it + s
            if live(it, s, 1 - U):
                q = (s - 1) % U
                wait(sp, sem["d_y_ps"], n)
                wait(sp, sem["d_kept"], n)
                wait(sp, sem["d_dest"], n)
                i = n + U - 1
                code = sp.value_load(tile_code[0:1, bass.ds(i, 1)], min_val=0, max_val=NBLOCKS * E1 - 1)
                blk, exp = code >> 3, code & 7
                sp.dma_start(xs[q][:, :, :], xs_blocks[blk]).then_inc(sem[f"d_xs_in{q}"], 16)
                sp.dma_start(w12[q][:, :, :].rearrange("p a b -> p (a b)"), dram["w12_1"][exp]).then_inc(sem[f"d_w_in{q}"], 16)
        turns(sp, body)

    @block.gpsimd
    def _(pool):
        def body(it, s):
            n = U * it + s
            if live(it, s, 2):
                q = (s - 2) % U
                pool.wait_ge(sem["d_dest"], n - 1)
                wait_apart(pool, sem["d_ys_sb"], T * (n - 1))
                for t in range(T):
                    pool.indirect_dma_start(dram["told"], bass.IndirectOffsetOnAxis(dest[q][:, t:t + 1], 0),
                                            ys[q][:, t, :], None, bounds_check=2 * NT * P - 1, oob_is_err=False)\
                        .then_inc(sem[f"d_ys_out{q}"], 16)
        turns(pool, body)
        for q in range(U):
            pool.wait_ge(sem[f"d_ys_out{q}"], 16 * T * TILES1 // U)

    @block.tensor
    def _(pe):
        pe.wait_ge(sem["d_ones"], 1)
        nc.tensor.matmul(p_y[0][:, 0:E1], ones16[:, :], seen[:, :], start=True, stop=True).then_inc(sem["d_count_ps"], 1)
        pe.wait_ge(sem["d_count"], 1)

        def body(it, s):
            n = U * it + s
            if live(it, s, -1):
                q = (s + 1) % U
                pe.wait_ge(sem[f"d_xs_in{q}"], 16 * (it + 1 + (s + 1) // U))
                wait(pe, sem["d_xsT_sb"], n)
                for t in range(T):
                    last = nc.tensor.transpose(p_x[(s + 1) % 2][:, P * t:P * t + P], xs[q][:, t, 0:C], ident[:, :])
                last.then_inc(sem["d_xsT_ps"], 1)
            if live(it, s, 0):
                pe.wait_ge(sem["d_xsT_sb"], n + 1)
                pe.wait_ge(sem[f"d_w_in{s}"], 16 * (it + 1))
                for k in range(FC):
                    wait(pe, sem["d_silu"], 2 * n + k - 3)
                    nc.tensor.matmul(p_h[2 * (s % 2) + k][:, 0:BLK1], w12[s][:, 0, P * k:P * k + P], xsT[s % 2][:, :],
                                     start=True, stop=True).then_inc(sem["d_h_ps"], 1)
            if live(it, s, 1):
                q = (s - 1) % U
                pe.wait_ge(sem["d_silu"], 2 * n)
                wait(pe, sem["d_ys_sb"], T * (n - 2))
                for t in range(T):
                    for k in range(FC):
                        last = nc.tensor.matmul(p_y[q % 2][:, P * t:P * t + P], hT[q % 2][:, k, P * t:P * t + P],
                                                w12[q][:, 1, C * k:C * k + C], start=(k == 0), stop=(k == FC - 1),
                                                skip_group_check=True)
                last.then_inc(sem["d_y_ps"], 1)
        turns(pe, body)

    @block.scalar
    def _(act):
        zero_tails(act, range(E1 // 2, E1))

        def body(it, s):
            n = U * it + s
            if live(it, s, 0):
                wait(act, sem["d_y_ps"], n - 1)
                for k in range(FC):
                    act.wait_ge(sem["d_h_ps"], 2 * n + k + 1)
                    nc.scalar.activation(hT[s % 2][:, k, :], p_h[2 * (s % 2) + k][:, 0:BLK1], ACT.Silu)\
                        .then_inc(sem["d_silu"], 1)
                act.wait_ge(sem["d_first"], n + 1)
                if not isinstance(it, int) or n >= U:
                    act.wait_ge(sem[f"d_ys_out{s % U}"], 16 * T * it)
                for t in range(T):
                    last = nc.scalar.activation(ys[s % U][:, t, :], xs[s % U][:, t, 0:C], ACT.Identity,
                                                scale=is_first[s % U][:, t:t + 1])
                last.then_inc(sem["d_kept"], 1)
        turns(act, body)

    @block.vector
    def _(dve):
        def spread(a, n):
            return a.rearrange("p (e a) -> p e a", a=1).to_broadcast([P, E1, n])

        step = [0]

        def then(ins):
            step[0] += 1
            ins.then_inc(sem["d_plan"], 1)
            dve.wait_ge(sem["d_plan"], step[0])

        nc.vector.memset(ones16[:, :], 1.0).then_inc(sem["d_ones"], 1)
        nc.vector.memset(zeros[:, :, :], 0.0)
        dve.wait_ge(sem["d_count_ps"], 1)
        nc.vector.tensor_copy(count[:, :], p_y[0][:, 0:E1]).then_inc(sem["d_count"], 1)
        dve.wait_ge(sem["d_count"], 1)
        dve.wait_ge(sem["d_base_in"], 16)
        nc.vector.tensor_tensor(tails[:, :], count[:, :], base[:, :], ALU.add).then_inc(sem["d_tails"], 1)
        dve.wait_ge(sem["d_const_in"], 16 * 3)
        then(nc.vector.tensor_tensor(full[:, :, :], starts[:, :, :], spread(count[:, :], NB), ALU.is_lt))
        then(nc.vector.tensor_reduce(blocks[:, :], full[:, :, :], AX, ALU.add))
        then(nc.vector.tensor_tensor(part[:, :, :], up_to[:, :, :],
                                     blocks[:, :].rearrange("p (a e) -> p a e", a=1).to_broadcast([P, E1, E1]), ALU.mult))
        then(nc.vector.tensor_reduce(cum[:, :], part[:, :, :], AX, ALU.add))
        then(nc.vector.tensor_tensor(ended[:, :, :], tile_number[:, :].rearrange("p (n a) -> p n a", a=1)
                                     .to_broadcast([P, TILES1, E1]),
                                     cum[:, :].rearrange("p (a e) -> p a e", a=1).to_broadcast([P, TILES1, E1]), ALU.is_ge))
        nc.vector.tensor_tensor(theirs[:, :, :], ended[:, :, :],
                                blocks[:, :].rearrange("p (a e) -> p a e", a=1).to_broadcast([P, TILES1, E1]), ALU.mult)
        then(nc.vector.tensor_reduce(expert[:, :], ended[:, :, :], AX, ALU.add))
        nc.vector.tensor_scalar(own[:, :], expert[:, :], -1.0, float(E1), ALU.mult, ALU.add)
        then(nc.vector.tensor_reduce(first_of[:, :], theirs[:, :, :], AX, ALU.add))
        nc.vector.tensor_scalar(tile_expert[:, :], expert[0:1, :], float(E1 - 1), None, ALU.min)
        then(nc.vector.tensor_tensor(local[:, :], tile_number[:, :], first_of[:, :], ALU.subtract))
        then(nc.vector.scalar_tensor_tensor(place[:, :], expert[:, :], float(REGION1), local[:, :], ALU.mult, ALU.add))
        then(nc.vector.tensor_scalar(tile_block[:, :], place[0:1, :], float(NBLOCKS - 1), None, ALU.min))
        nc.vector.scalar_tensor_tensor(tile_code[:, :], tile_block[:, :], float(E1), tile_expert[:, :], ALU.mult, ALU.add)\
            .then_inc(sem["d_table"], 1)

        def body(it, s):
            n = U * it + s
            if live(it, s, -1):
                dve.wait_ge(sem["d_xsT_ps"], n + 2)
                wait(dve, sem["d_h_ps"], 2 * n)
                nc.vector.tensor_copy(xsT[(s + 1) % 2][:, :], p_x[(s + 1) % 2][:, 0:BLK1]).then_inc(sem["d_xsT_sb"], 1)
            if live(it, s, 0):
                q, mine = s % U, own[:, bass.ds(n, 1)]
                ids, firsts, s0, s1 = (xs[q][:, :, C + i] for i in range(4))
                if not isinstance(it, int) or n >= U:
                    dve.wait_ge(sem[f"d_ys_out{q}"], 16 * T * it)
                nc.vector.tensor_scalar(is_first[q][:, :], firsts, mine, None, ALU.is_equal).then_inc(sem["d_first"], 1)
                nc.vector.tensor_scalar(second[q][:, :], firsts, mine, float(NT * P), ALU.not_equal, ALU.mult)\
                    .then_inc(sem["d_second"], 1)
                nc.vector.scalar_tensor_tensor(share0[q][:, :], firsts, mine, s0, ALU.is_equal, ALU.mult)
                nc.vector.scalar_tensor_tensor(share1[q][:, :], firsts, mine, s1, ALU.not_equal, ALU.mult)\
                    .then_inc(sem["d_shares"], 1)
                dve.wait_ge(sem["d_second"], n + 1)
                nc.vector.scalar_tensor_tensor(dest[q][:, :], ids, 2.0 * NT * P, second[q][:, :], ALU.add, ALU.add)\
                    .then_inc(sem["d_dest"], 1)
                dve.wait_ge(sem["d_shares"], n + 1)
                nc.vector.tensor_tensor(share[q][:, :], share0[q][:, :], share1[q][:, :], ALU.add).then_inc(sem["d_share"], 1)
            if live(it, s, 1):
                q = (s - 1) % U
                dve.wait_ge(sem["d_kept"], n)
                dve.wait_ge(sem["d_share"], n)
                dve.wait_ge(sem["d_y_ps"], n)
                for t in range(T):
                    nc.vector.scalar_tensor_tensor(ys[q][:, t, :], p_y[q % 2][:, P * t:P * t + P], share[q][:, t:t + 1],
                                                   ys[q][:, t, :], ALU.mult, ALU.add).then_inc(sem["d_ys_sb"], 1)
        turns(dve, body)


def phase_combine1(nc, dram, const, sem, ctx):
    def sb(name, shape, dt=F32):
        return ctx.enter_context(nc.sbuf_tensor("e_" + name, shape, dt))

    eps = const["eps"]
    NB = 4
    told = [sb(f"told{i}", [P, 2, TPS, C]) for i in range(NB)]
    res = [sb(f"res{i}", [P, TPS, C]) for i in range(NB)]
    y = [sb(f"y{i}", [P, TPS, C]) for i in range(NB)]
    st = [sb(f"st{i}", [P, TPS, 6]) for i in range(NB)]
    mv = [sb(f"mv{i}", [P, TPS, 2]) for i in range(NB)]
    ln = [sb(f"ln{i}", [P, 6, TPS]) for i in range(NB)]
    told_rows = dram["told"].rearrange("(k b t p) c -> k b p t c", p=P, t=TPS, k=2)
    out_rows = dram["out"].rearrange("b (t p) c -> b p t c", p=P)
    block = ctx.enter_context(nc.Block())

    def live(it, s, lag):
        return not isinstance(it, int) or 0 <= NB * it + s - lag < NSEQ

    def turns(eng, body):
        for it in (-1, 0, 1):
            for s in range(NB):
                body(it, s)
        with eng.Fori(2, NSEQ // NB - 1) as it:
            for s in range(NB):
                body(it, s)
        for s in range(NB + 3):
            body(NSEQ // NB - 1 + s // NB, s % NB)

    @block.sync
    def _(sp):
        def body(it, s):
            b = NB * it + s
            if live(it, s, -3):
                q = (s + 3) % NB
                wait(sp, sem["e_res"], b)
                for k in range(2):
                    sp.dma_start(told[q][:, k, :, :], told_rows[k][b + 3]).then_inc(sem[f"e_in{q}"], 16)
            if live(it, s, 2):
                q = (s - 2) % NB
                sp.wait_ge(sem["e_y"], TPS * (b - 1))
                sp.dma_start(out_rows[b - 2], y[q][:, :, :]).then_inc(sem[f"e_out{q}"], 16)
        turns(sp, body)
        for q in range(NB):
            sp.wait_ge(sem[f"e_out{q}"], 16 * NSEQ // NB)

    @block.gpsimd
    def _(pool):
        def body(it, s):
            b = NB * it + s
            if live(it, s, 0):
                pool.wait_ge(sem[f"e_in{s}"], 32 * (it + 1))
                if not isinstance(it, int) or b >= NB:
                    pool.wait_ge(sem["e_y"], TPS * (b - NB + 1))
                nc.gpsimd.tensor_tensor(res[s][:, :, :], told[s][:, 0, :, :], told[s][:, 1, :, :], ALU.add)\
                    .then_inc(sem["e_res"], 1)
        turns(pool, body)

    @block.scalar
    def _(act):
        nc.scalar.preload_act_table_set("natural_log_exp_and_others")

        def body(it, s):
            b = NB * it + s
            if live(it, s, 0):
                act.wait_ge(sem["e_var"], TPS * (b + 1))
                nc.scalar.activation(ln[s][:, 0, :], mv[s][:, :, 1], ACT.Ln, bias=eps[:, 0:1]).then_inc(sem["e_ln"], 1)
                act.wait_ge(sem["e_ln"], b + 1)
                nc.scalar.activation(ln[s][:, 1, :], ln[s][:, 0, :], ACT.Exp, scale=-0.5).then_inc(sem["e_guess"], 1)
            if live(it, s, 1):
                q = (s - 1) % NB
                act.wait_ge(sem["e_shift"], b)
                if not isinstance(it, int) or b - 1 >= NB:
                    act.wait_ge(sem[f"e_out{q}"], 16 * (it if s >= 1 else it - 1))
                for u in range(TPS):
                    nc.scalar.activation(y[q][:, u, :], res[q][:, u, :], ACT.Identity, bias=ln[q][:, 5, u:u + 1],
                                         scale=ln[q][:, 4, u:u + 1]).then_inc(sem["e_y"], 1)
        turns(act, body)

    @block.vector
    def _(dve):
        def body(it, s):
            b = NB * it + s
            q, c = (s - 1) % NB, b - 1
            mean, var = mv[q][:, :, 0], mv[q][:, :, 1]
            _, first, half, square, rstd, shift = (ln[q][:, r, :] for r in range(6))
            done = sem["e_newton"]
            if live(it, s, 0):
                dve.wait_ge(sem["e_res"], b + 1)
                for u in range(TPS):
                    nc.vector.bn_stats(st[s][:, u, :], res[s][:, u, :]).then_inc(sem["e_bn"], 1)
                wait_apart(dve, sem["e_bn"], TPS * (b + 1))
                for u in range(TPS):
                    nc.vector.bn_aggr(mv[s][:, u, :], st[s][:, u, :]).then_inc(sem["e_var"], 1)
            if live(it, s, 1):
                dve.wait_ge(sem["e_guess"], b)
                nc.vector.scalar_tensor_tensor(half, var, EPS, first, ALU.add, ALU.mult).then_inc(done, 1)
                dve.wait_ge(done, 4 * c + 1)
                nc.vector.tensor_tensor(square, half, first, ALU.mult).then_inc(done, 1)
                dve.wait_ge(done, 4 * c + 2)
                nc.vector.tensor_scalar(half, square, -0.5, 1.5, ALU.mult, ALU.add).then_inc(done, 1)
                dve.wait_ge(done, 4 * c + 3)
                nc.vector.tensor_tensor(rstd, half, first, ALU.mult).then_inc(done, 1)
                dve.wait_ge(done, 4 * c + 4)
                nc.vector.scalar_tensor_tensor(shift, mean, -1.0, rstd, ALU.mult, ALU.mult).then_inc(sem["e_shift"], 1)
        turns(dve, body)


PHASES = (phase_attention0, phase_experts0, phase_attention1, phase_experts1, phase_combine1)


class Semaphores(dict):

    def __init__(self, nc):
        self.nc = nc

    def __missing__(self, name):
        self[name] = self.nc.alloc_semaphore(name=name)
        return self[name]


def build(nc, dram, phases=PHASES):
    assert TILES1 >= 2 * NT * P // BLK1 + E1 - 1 and SPARE1 == UNROLL and E1 == 8
    with ExitStack() as ctx:
        const = {"eps": ctx.enter_context(nc.sbuf_tensor("eps", [P, 1], F32)),
                 "ident": ctx.enter_context(nc.sbuf_tensor("ident", [P, P], F32)),
                 "seen": ctx.enter_context(nc.sbuf_tensor("seen", [P, E1], BF16))}
        for phase in phases:
            sem = Semaphores(nc)
            with ExitStack() as of_phase:
                phase(nc, dram, const, sem, of_phase)
            nc.clear_and_free_semaphores(list(sem.values()))
            nc.all_engine_barrier()


SCRATCH = {"x1": ((NT * P, C), F32), "slots": ((SLOTS, ROW0), F32), "moe": ((NT * P, C), F32),
           "slot_of": ((NSEQ, P, TPS), U32), "weight_of": ((NSEQ, P, TPS), F32),
           "xs1": (((E1 * REGION1 + SPARE1 + 1) * BLK1, ROW1), F32), "told": ((2 * NT * P, C), F32)}


def laid_out(i):
    import numpy as np
    c = np.ascontiguousarray
    w = {k: np.asarray(v) for k, v in i.items()}
    x = w["L0_attn_x"]
    wqkv = w["L0_attn_w_qkv"]
    wv = wqkv[2 * C:].reshape(4, 2, D0, C)
    i_q, k = np.arange(P)[:, None] % QB, np.arange(WIN)[None, :]
    band = (k > i_q) & (k < i_q + 2 * BAND)
    masks = [band, band & (k >= BAND), band & (k < WIN - BAND)]
    tok = np.arange(P)
    arrays = {
        "x": c(x), "xT": c(x.transpose(0, 2, 1)),
        "wqkvT": c(wqkv[:2 * C].T), "wv_by_parity": c(wv.transpose(3, 1, 0, 2).reshape(C, C)),
        "wprojT": c(w["L0_attn_w_proj"].T), "bqkv": c(w["L0_attn_b_qkv"].reshape(3, C).T),
        "bproj": c(np.broadcast_to(w["L0_attn_b_proj"], (P, C))),
        "gate0T": c(w["L0_ffn_gate_w"].T),
        "w1_0": c(w["L0_ffn_w1"]), "w2_0": c(w["L0_ffn_w2"]),
        "wqk1": c(np.concatenate([w["L1_attn_Wq"], w["L1_attn_Wk"]], 1)), "wv1": c(w["L1_attn_Wv"]),
        "gate1T": c(w["L1_ffn_gate_w"].T),
        "balance": c(np.broadcast_to(np.tile(w["L1_ffn_balance_bias"], TPS), (P, TPS * E1))),
        "w12_1": c(np.concatenate([w["L1_ffn_w1"].transpose(0, 2, 1),
                                   w["L1_ffn_w2"].reshape(E1, C, F1 // P, P).transpose(0, 3, 2, 1).reshape(E1, P, F1)], 2)),
        "band_mask": c(np.concatenate([np.where(m, 0, -1e30) for m in masks], 1).astype(np.float32)),
        "causal": np.where(tok[None, :] <= tok[:, None], 0, -1e30).astype(np.float32),
        "before": (tok[:, None] < tok[None, :]).astype(np.float32),
        "ident": np.eye(P, dtype=np.float32),
        "rev1": c(np.broadcast_to(np.tile(E1 - np.arange(E1), TPS), (P, TPS * E1)).astype(np.float32)),
        "region1": c(np.broadcast_to(np.tile(np.arange(E1) * REGION1 * BLK1, TPS), (P, TPS * E1)).astype(np.float32)),
        "block_starts": c(np.broadcast_to(np.tile(np.arange(REGION1 - 1) * BLK1, E1), (P, E1 * (REGION1 - 1))).astype(np.float32)),
        "up_to": c(np.broadcast_to(np.tri(E1).reshape(-1), (P, E1 * E1)).astype(np.float32)),
        "token_of": c((np.arange(2 * TPS)[None, :] * P + tok[:, None]).astype(np.float32)),
        "tile_number": c(np.broadcast_to(np.arange(TILES1), (P, TILES1)).astype(np.float32)),
        "rev": c(np.broadcast_to(np.tile(E0 - np.arange(E0), TPS), (P, TPS * E0)).astype(np.float32)),
    }
    arrays["packed1"] = c(np.concatenate([arrays[name] for name, _ in PACKED1], 1))
    return {name: a for name, a in arrays.items() if name not in ("wqk1", "wv1", "causal", "gate1T", "balance", "rev1")}


def kernel(**inputs):
    import numpy as np
    import concourse.bacc as bacc
    from concourse.bass_utils import run_bass_kernel_spmd

    arrays = laid_out(inputs)
    nc = bacc.Bacc("TRN2", target_bir_lowering=False, num_devices=1)
    dram = {n: nc.dram_tensor("in_" + n, a.shape, mybir.dt.from_np(a.dtype), kind="ExternalInput").ap()
            for n, a in arrays.items()}
    for n, (shape, dt) in SCRATCH.items():
        dram[n] = nc.dram_tensor("scratch_" + n, shape, dt, kind="Internal").ap()
    dram["out"] = nc.dram_tensor("out_0", (NSEQ, SEQ, C), F32, kind="ExternalOutput").ap()
    build(nc, dram)
    r = run_bass_kernel_spmd(nc, [{"in_" + n: a for n, a in arrays.items()}], core_ids=[0])
    return np.asarray(r.results[0]["out_0"])
```
